# Optimizing a Trainium2 kernel written in Bass

```python
import numpy as np
import jax
import jax.numpy as jnp

def _softmax(x, axis=-1):
    return jax.nn.softmax(x, axis=axis)

def _gelu(x):
    return jax.nn.gelu(x, approximate=True)

def _silu(x):
    return jax.nn.silu(x)

def _sigmoid(x):
    return jax.nn.sigmoid(x)

def _layernorm(x, axis=-1, eps=1e-05):
    m = jnp.mean(x, axis=axis, keepdims=True)
    v = jnp.var(x, axis=axis, keepdims=True)
    return (x - m) / jnp.sqrt(v + eps)

def _scatter_add(tgt, idx, src, axis=0):
    return tgt.at[idx].add(src)

def _segment_sum(src, seg, n):
    return jax.ops.segment_sum(src, seg, n)
kernel_name = 'mk_perceiver_d1_seqx_r2_6ea839'

def setup_inputs(seed: int=0):
    np.random.seed(seed)
    _w = jnp.asarray

    def _rec_inputs():
        import jax
        import jax.numpy as jnp
        _rk = jax.random.key(seed)
        x = -9.806e-05 + 1 * jax.random.normal(jax.random.fold_in(_rk, 1), (1, 512, 512), jnp.float32)
        _lenS = 512 - jax.random.randint(jax.random.fold_in(_rk, 7), (1,), 0, max(1, 512 // 4) + 1, jnp.int32)
        _lenS2 = 8192 - jax.random.randint(jax.random.fold_in(_rk, 8), (1,), 0, max(1, 8192 // 4) + 1, jnp.int32)
        _ctx_1024P = jax.random.normal(jax.random.fold_in(_rk, 11), (1, 16, 512), jnp.float32)
        _ctx_1024c = jax.random.dirichlet(jax.random.fold_in(_rk, 511), 0.3 * jnp.ones((16,), jnp.float32), (1, 8192))
        _ctx_1024t = jnp.einsum('bsk,bkd->bsd', _ctx_1024c, _ctx_1024P)
        _ctx_1024t = _ctx_1024t * jax.lax.rsqrt(jnp.mean(jnp.square(_ctx_1024t)) + 1e-12) * 0.953939
        ctx_1024 = -1.52775e-05 + 0.999936 * (_ctx_1024t + 0.3 * jax.random.normal(jax.random.fold_in(_rk, 611), (1, 8192, 512), jnp.float32))
        return (x, ctx_1024)
    x, ctx_1024 = _rec_inputs()

    def _L0_xattn_setup():
        import jax, jax.numpy as jnp
        import numpy as np
        EPS = 1e-06
        NUM_ITERS = 3

        def rmsnorm(x, w, eps=EPS):
            return x * jax.lax.rsqrt(jnp.mean(x * x, axis=-1, keepdims=True) + eps) * w

        def gru_cell(x, h, wi, wh, bi, bh):
            d = h.shape[-1]
            gi = jnp.einsum('...d,ed->...e', x, wi) + bi
            gh = jnp.einsum('...d,ed->...e', h, wh) + bh
            ir, iz, inn = (gi[..., :d], gi[..., d:2 * d], gi[..., 2 * d:])
            hr, hz, hn = (gh[..., :d], gh[..., d:2 * d], gh[..., 2 * d:])
            r = jax.nn.sigmoid(ir + hr)
            z = jax.nn.sigmoid(iz + hz)
            n = jnp.tanh(inn + r * hn)
            return (1.0 - z) * n + z * h
        key = jax.random.key(seed)
        ks = jax.random.split(key, 12)
        B, K, M, d = (8, 64, 2048, 512)
        s = 0.02
        return {'slots': jax.random.normal(ks[0], (B, K, d), jnp.float32), 'P': jax.random.normal(ks[1], (B, M, d), jnp.float32), 'Wq': jax.random.normal(ks[2], (d, d), jnp.float32) * s, 'Wk': jax.random.normal(ks[3], (d, d), jnp.float32) * s, 'Wv': jax.random.normal(ks[4], (d, d), jnp.float32) * s, 'gru_wi': jax.random.normal(ks[5], (3 * d, d), jnp.float32) * s, 'gru_wh': jax.random.normal(ks[6], (3 * d, d), jnp.float32) * s, 'gru_bi': jax.random.normal(ks[7], (3 * d,), jnp.float32) * s, 'gru_bh': jax.random.normal(ks[8], (3 * d,), jnp.float32) * s, 'slot_norm_w': jnp.ones((d,), jnp.float32), 'input_norm_w': jnp.ones((d,), jnp.float32)}
    _L0_xattn_all = _L0_xattn_setup()
    _L0_xattn_in = {k: v for k, v in _L0_xattn_all.items() if k in ('Wq', 'Wk', 'Wv', 'gru_wi', 'gru_wh', 'gru_bi', 'gru_bh', 'slot_norm_w', 'input_norm_w')}
    del _L0_xattn_all

    def _L0_attn_setup():
        import jax, jax.numpy as jnp
        import numpy as np
        EPS = 1e-06
        ROPE_BASE = 10000.0

        def _rope(t):
            B, T, H, D = t.shape
            half = D // 2
            inv_freq = 1.0 / ROPE_BASE ** (jnp.arange(0, half, dtype=jnp.float32) * 2.0 / D)
            ang = jnp.arange(T, dtype=jnp.float32)[:, None] * inv_freq[None, :]
            cos = jnp.cos(ang)[None, :, None, :]
            sin = jnp.sin(ang)[None, :, None, :]
            x1, x2 = (t[..., :half], t[..., half:])
            return jnp.concatenate([x1 * cos - x2 * sin, x2 * cos + x1 * sin], axis=-1)

        def _rmsnorm(t, w):
            ms = jnp.mean(t * t, axis=-1, keepdims=True)
            return t * jax.lax.rsqrt(ms + EPS) * w
        key = jax.random.key(seed)
        k1, k2, k3 = jax.random.split(key, 3)
        B, T, C, H = (2, 1024, 512, 16)
        D = C // H
        s = 1.0 / np.sqrt(C)
        return {'x': jax.random.normal(k1, (B, T, C), dtype=jnp.float32), 'w_qkv': jax.random.normal(k2, (3 * C, C), dtype=jnp.float32) * s, 'w_out': jax.random.normal(k3, (C, C), dtype=jnp.float32) * s, 'q_norm_w': jnp.ones((D,), dtype=jnp.float32), 'k_norm_w': jnp.ones((D,), dtype=jnp.float32)}
    _L0_attn_all = _L0_attn_setup()
    _L0_attn_in = {k: v for k, v in _L0_attn_all.items() if k in ('w_qkv', 'w_out', 'q_norm_w', 'k_norm_w')}
    del _L0_attn_all

    def _L0_ffn_setup():
        import jax, jax.numpy as jnp
        import numpy as np
        B, T, D_MODEL = (4, 1024, 512)
        N_EXPERTS, TOP_K, D_EXPERT = (6, 2, 256)
        QUANT_TEMP = 0.3
        _ANCHOR_IDS = [63, 6, 0, 18, 45, 27]

        def _q6_idx_to_vertex(idx):
            bits = [idx >> 5 - b & 1 for b in range(6)]
            return [2.0 * b - 1.0 for b in bits]

        def _anchors():
            return jnp.asarray(np.array([_q6_idx_to_vertex(i) for i in _ANCHOR_IDS], dtype=np.float32))

        def _router(x, proj_w, anchors, routing_temp):
            z = jnp.einsum('btd,ed->bte', x, proj_w)
            q = jnp.tanh(z / QUANT_TEMP)
            dot = jnp.einsum('btd,ed->bte', q, anchors)
            hamming = (6.0 - dot) * 0.5
            logits = -hamming / jnp.clip(routing_temp, 0.1)
            topk_logits, topk_idx = jax.lax.top_k(logits, TOP_K)
            topk_w = jax.nn.softmax(topk_logits, axis=-1)
            onehot = jax.nn.one_hot(topk_idx, N_EXPERTS, dtype=x.dtype)
            expert_weights = jnp.einsum('btke,btk->bte', onehot, topk_w)
            return (expert_weights, q)
        key = jax.random.key(seed)
        k_x, k_p, k_w1, k_w2 = jax.random.split(key, 4)
        x = jax.random.normal(k_x, (B, T, D_MODEL), dtype=jnp.float32)
        proj_w = jax.random.normal(k_p, (6, D_MODEL), dtype=jnp.float32) * 0.02
        anchors = _anchors()
        routing_temp = jnp.array(1.0, dtype=jnp.float32)
        s1 = 1.0 / np.sqrt(D_MODEL)
        s2 = 1.0 / np.sqrt(D_EXPERT)
        w1 = jax.random.uniform(k_w1, (N_EXPERTS, D_MODEL, D_EXPERT), jnp.float32, -s1, s1)
        w2 = jax.random.uniform(k_w2, (N_EXPERTS, D_EXPERT, D_MODEL), jnp.float32, -s2, s2)
        return {'x': x, 'proj_w': proj_w, 'anchors': anchors, 'routing_temp': routing_temp, 'w1': w1, 'w2': w2}
    _L0_ffn_all = _L0_ffn_setup()
    _L0_ffn_in = {k: v for k, v in _L0_ffn_all.items() if k in ('proj_w', 'anchors', 'routing_temp', 'w1', 'w2')}
    del _L0_ffn_all
    return {'x': x, 'ctx_1024': ctx_1024, 'L0_xattn_Wq': _L0_xattn_in['Wq'], 'L0_xattn_Wk': _L0_xattn_in['Wk'], 'L0_xattn_Wv': _L0_xattn_in['Wv'], 'L0_xattn_gru_wi': _L0_xattn_in['gru_wi'], 'L0_xattn_gru_wh': _L0_xattn_in['gru_wh'], 'L0_xattn_gru_bi': _L0_xattn_in['gru_bi'], 'L0_xattn_gru_bh': _L0_xattn_in['gru_bh'], 'L0_xattn_slot_norm_w': _L0_xattn_in['slot_norm_w'], 'L0_xattn_input_norm_w': _L0_xattn_in['input_norm_w'], 'L0_attn_w_qkv': _L0_attn_in['w_qkv'], 'L0_attn_w_out': _L0_attn_in['w_out'], 'L0_attn_q_norm_w': _L0_attn_in['q_norm_w'], 'L0_attn_k_norm_w': _L0_attn_in['k_norm_w'], 'L0_ffn_proj_w': _L0_ffn_in['proj_w'], 'L0_ffn_anchors': _L0_ffn_in['anchors'], 'L0_ffn_routing_temp': _L0_ffn_in['routing_temp'], 'L0_ffn_w1': _L0_ffn_in['w1'], 'L0_ffn_w2': _L0_ffn_in['w2']}

def reference(x, ctx_1024, L0_xattn_Wq, L0_xattn_Wk, L0_xattn_Wv, L0_xattn_gru_wi, L0_xattn_gru_wh, L0_xattn_gru_bi, L0_xattn_gru_bh, L0_xattn_slot_norm_w, L0_xattn_input_norm_w, L0_attn_w_qkv, L0_attn_w_out, L0_attn_q_norm_w, L0_attn_k_norm_w, L0_ffn_proj_w, L0_ffn_anchors, L0_ffn_routing_temp, L0_ffn_w1, L0_ffn_w2):
    import jax
    import jax.numpy as jnp

    def _L0_xattn_ref(slots, P, Wq, Wk, Wv, gru_wi, gru_wh, gru_bi, gru_bh, slot_norm_w, input_norm_w):
        import jax, jax.numpy as jnp
        import numpy as np
        EPS = 1e-06
        NUM_ITERS = 3

        def rmsnorm(x, w, eps=EPS):
            return x * jax.lax.rsqrt(jnp.mean(x * x, axis=-1, keepdims=True) + eps) * w

        def gru_cell(x, h, wi, wh, bi, bh):
            d = h.shape[-1]
            gi = jnp.einsum('...d,ed->...e', x, wi) + bi
            gh = jnp.einsum('...d,ed->...e', h, wh) + bh
            ir, iz, inn = (gi[..., :d], gi[..., d:2 * d], gi[..., 2 * d:])
            hr, hz, hn = (gh[..., :d], gh[..., d:2 * d], gh[..., 2 * d:])
            r = jax.nn.sigmoid(ir + hr)
            z = jax.nn.sigmoid(iz + hz)
            n = jnp.tanh(inn + r * hn)
            return (1.0 - z) * n + z * h
        d = slots.shape[-1]
        scale = d ** (-0.5)
        Pn = rmsnorm(P, input_norm_w)
        k_proj = jnp.einsum('bmd,ed->bme', Pn, Wk)
        v_proj = jnp.einsum('bmd,ed->bme', Pn, Wv)
        for _ in range(NUM_ITERS):
            sn = rmsnorm(slots, slot_norm_w)
            q = jnp.einsum('bkd,ed->bke', sn, Wq)
            scores = jnp.einsum('bkd,bmd->bkm', q, k_proj) * scale
            attn = jax.nn.softmax(scores, axis=-2)
            attn = attn / (jnp.sum(attn, axis=-1, keepdims=True) + EPS)
            updates = jnp.einsum('bkm,bmd->bkd', attn, v_proj)
            slots = gru_cell(updates, slots, gru_wi, gru_wh, gru_bi, gru_bh)
        return slots

    def _L0_attn_ref(x, w_qkv, w_out, q_norm_w, k_norm_w):
        import jax, jax.numpy as jnp
        import numpy as np
        EPS = 1e-06
        ROPE_BASE = 10000.0

        def _rope(t):
            B, T, H, D = t.shape
            half = D // 2
            inv_freq = 1.0 / ROPE_BASE ** (jnp.arange(0, half, dtype=jnp.float32) * 2.0 / D)
            ang = jnp.arange(T, dtype=jnp.float32)[:, None] * inv_freq[None, :]
            cos = jnp.cos(ang)[None, :, None, :]
            sin = jnp.sin(ang)[None, :, None, :]
            x1, x2 = (t[..., :half], t[..., half:])
            return jnp.concatenate([x1 * cos - x2 * sin, x2 * cos + x1 * sin], axis=-1)

        def _rmsnorm(t, w):
            ms = jnp.mean(t * t, axis=-1, keepdims=True)
            return t * jax.lax.rsqrt(ms + EPS) * w
        B, T, C = x.shape
        H = 16
        D = C // H
        qkv = x @ w_qkv.T
        q, k, v = jnp.split(qkv, 3, axis=-1)
        q = q.reshape(B, T, H, D)
        k = k.reshape(B, T, H, D)
        v = v.reshape(B, T, H, D)
        q = _rmsnorm(_rope(q), q_norm_w)
        k = _rmsnorm(_rope(k), k_norm_w)
        scale = 1.0 / np.sqrt(D)
        attn = jnp.einsum('bqhd,bkhd->bhqk', q, k) * scale
        causal = jnp.tril(jnp.ones((T, T), dtype=bool))
        attn = jnp.where(causal[None, None], attn, -jnp.inf)
        attn = jax.nn.softmax(attn, axis=-1)
        out = jnp.einsum('bhqk,bkhd->bqhd', attn, v).reshape(B, T, C)
        return out @ w_out.T

    def _L0_ffn_ref(x, proj_w, anchors, routing_temp, w1, w2):
        import jax, jax.numpy as jnp
        import numpy as np
        B, T, D_MODEL = (4, 1024, 512)
        N_EXPERTS, TOP_K, D_EXPERT = (6, 2, 256)
        QUANT_TEMP = 0.3
        _ANCHOR_IDS = [63, 6, 0, 18, 45, 27]

        def _q6_idx_to_vertex(idx):
            bits = [idx >> 5 - b & 1 for b in range(6)]
            return [2.0 * b - 1.0 for b in bits]

        def _anchors():
            return jnp.asarray(np.array([_q6_idx_to_vertex(i) for i in _ANCHOR_IDS], dtype=np.float32))

        def _router(x, proj_w, anchors, routing_temp):
            z = jnp.einsum('btd,ed->bte', x, proj_w)
            q = jnp.tanh(z / QUANT_TEMP)
            dot = jnp.einsum('btd,ed->bte', q, anchors)
            hamming = (6.0 - dot) * 0.5
            logits = -hamming / jnp.clip(routing_temp, 0.1)
            topk_logits, topk_idx = jax.lax.top_k(logits, TOP_K)
            topk_w = jax.nn.softmax(topk_logits, axis=-1)
            onehot = jax.nn.one_hot(topk_idx, N_EXPERTS, dtype=x.dtype)
            expert_weights = jnp.einsum('btke,btk->bte', onehot, topk_w)
            return (expert_weights, q)
        expert_weights, q = _router(x, proj_w, anchors, routing_temp)
        h = jax.nn.gelu(jnp.einsum('btd,edh->bteh', x, w1))
        out = jnp.einsum('bteh,ehd,bte->btd', h, w2, expert_weights)
        return out
    x = x + _L0_xattn_ref(_layernorm(x, axis=-1), ctx_1024, L0_xattn_Wq, L0_xattn_Wk, L0_xattn_Wv, L0_xattn_gru_wi, L0_xattn_gru_wh, L0_xattn_gru_bi, L0_xattn_gru_bh, L0_xattn_slot_norm_w, L0_xattn_input_norm_w)
    x = x + _L0_attn_ref(_layernorm(x, axis=-1), L0_attn_w_qkv, L0_attn_w_out, L0_attn_q_norm_w, L0_attn_k_norm_w)
    x = x + _L0_ffn_ref(_layernorm(x, axis=-1), L0_ffn_proj_w, L0_ffn_anchors, L0_ffn_routing_temp, L0_ffn_w1, L0_ffn_w2)
    return x

_drawn_inputs = setup_inputs


def setup_inputs(seed=0):
    import zlib

    import numpy as np

    out = dict(_drawn_inputs(seed))
    spreads = {'L0_xattn_slot_norm_w': (1.0, 0.6),
     'L0_xattn_input_norm_w': (1.0, 0.6),
     'L0_attn_q_norm_w': (1.0, 0.6),
     'L0_attn_k_norm_w': (1.0, 0.6)}
    factors = {'L0_xattn_Wq': 6.695, 'L0_xattn_Wk': 7.821, 'L0_xattn_gru_bh': 4.411}
    for name, (base, spread) in spreads.items():
        noise = np.random.default_rng([zlib.crc32(name.encode()), seed]).standard_normal(out[name].shape)
        drawn = base * np.exp(spread * noise) if base else spread * noise
        out[name] = jnp.asarray(drawn.astype(out[name].dtype))
    for name, factor in factors.items():
        out[name] = (out[name] * factor).astype(out[name].dtype)
    return out
```

```python
from contextlib import ExitStack

import numpy as np

import concourse.bass as bass
from concourse import mybir

F32 = mybir.dt.float32
F16 = mybir.dt.float16
BF16 = mybir.dt.bfloat16
ALU = mybir.AluOpType
ACT = mybir.ActivationFunctionType
AX = mybir.AxisListType

P = 128
D = 512
C = D // P
K = 512
TT = K // P
M = 8192
NT = M // P
NG = 16
RING = NT // NG
ITERS = 3
H = 16
HD = D // H
HG = H // 4
NE = 6
DE = 256
TOPK = 2
EPS = 1e-6
LN_EPS = 1e-5
QUANT_TEMP = 0.3
SCALE = float(D) ** -0.5
ATT_SCALE = float(HD) ** -0.5

S_X = 2.0 ** 10
S_A = 2.0 ** 15
S_W = 2.0 ** 15
TINY = 1e-30

QK_UNITS = C
GATE_UNITS = 6 * C
UNITS = QK_UNITS + GATE_UNITS
WRING = 7
GATE_LANES = WRING - QK_UNITS
GATE_GROUPS = GATE_UNITS // GATE_LANES
assert GATE_UNITS % GATE_LANES == 0 and GATE_LANES < RING and GATE_GROUPS < NG - 1
assert UNITS % WRING == 0 and NT % RING == 0 and NG >= 3

BI, BH, WSLOT, WIN = 0, 12, 24, 28
QW, KW, TEMP, ANCH = 32, 33, 34, 35
LOWER = ANCH + 36
COS = LOWER + 36
SIN = COS + TT * HD
IDENT = SIN + TT * HD
SMALL = IDENT + P

PARTS3 = ((0, 0), (0, 1), (1, 0))


def slot_kernel(nc, x, ctx, wq, wk, wv, wi_t, wh_u, win_b, small, half, wqkv_t, wout_t, w1_t, w2,
                proj_t, out):
    stack = ExitStack()
    with stack:
        def sb(name, shape, dt=F32):
            return stack.enter_context(nc.sbuf_tensor(name, shape, dt))

        def sem(name):
            return stack.enter_context(nc.semaphore(name))

        pt_dram = nc.dram_tensor("pt_scratch", (NT, P, 2 * C * P), F16, kind="Internal").ap()
        wu_dram = nc.dram_tensor("weight_units", (UNITS, P, 2 * C * P), F16, kind="Internal").ap()

        pn = sb("pn", [P, NT * 2 * D], F16)
        pt = sb("pt", [P, RING, 2, C, P], F16)
        cx = sb("cx", [P, RING, D])
        wr = sb("wr", [P, WRING, 2, C, P], F16)
        h32 = sb("h32", [P, C, K])
        hs = sb("hs", [P, 2, C, K], F16)
        qu = sb("qu", [P, 2, C, K], F16)
        ea = sb("ea", [P, 4, K])
        ah = sb("ah", [P, 2, 2, K], F16)
        acc = sb("acc", [P, K])
        diag = sb("diag", [P, TT, P])
        rb = sb("rb", [P, K])
        sm = sb("sm", [P, SMALL])
        hf = sb("hf", [P, 2 * P], F16)
        bm = sb("bm", [P, 2 * P], BF16)
        ones = sb("ones", [P, P])
        st = sb("st", [P, 112])
        pj = sb("pj", [P, C * NE])
        ident = sm[:, IDENT:IDENT + P]
        ident16, zeros16 = hf[:, 0:P], hf[:, P:2 * P]
        identb, maskb = bm[:, 0:P], bm[:, P:2 * P]

        def pn_tile(t, part):
            return pn[:, bass.ds(t * (2 * D) + part * D, D)]

        def pn_w(t, part, c):
            return pn[:, bass.ds(t * (2 * D) + part * D + c * P, P)]

        pn32 = pn[:, :].bitcast(F32)

        def region(at, n):
            return pn32[:, at:at + n]

        base = NT * D
        GU = C * P
        pick = ea[:, 2:4].rearrange("p a k -> p (a k)")[0:NE, 0:NE * P].rearrange("p (e k) -> p e k", e=NE)
        def take(n):
            nonlocal base
            base -= n
            return region(base, n)
        w_all = take(GATE_UNITS * GU).rearrange("p (a g c e) -> p a g c e", a=C, g=6, c=C)
        w_units = w_all.rearrange("p a g c e -> p (a g c e)")
        wiT = take(C * 3 * D).rearrange("p (c e) -> p c e", c=C)
        wv_s = take(C * D).rearrange("p (c e) -> p c e", c=C)
        wq_s = take(C * D).rearrange("p (c e) -> p c e", c=C)
        wk_s = take(C * D).rearrange("p (c e) -> p c e", c=C)
        wqk = take(C * D).rearrange("p (c e) -> p c e", c=C)
        winb = take(D)
        x_s = take(TT * D).rearrange("p (t d) -> p t d", t=TT)
        assert base >= 4 * D
        wqkv_s = region(0, C * 3 * D).rearrange("p (c e) -> p c e", c=C)
        hw_s = region(0, 12 * K).rearrange("p (q t) -> p q t", q=12)
        wout_s = region(C * 3 * D, C * D).rearrange("p (c e) -> p c e", c=C)
        w1_s = region(C * 4 * D, 12 * GU).rearrange("p (c e) -> p c e", c=C)
        w2_s = region(C * 4 * D + 12 * GU, 12 * D).rearrange("p (q e) -> p q e", q=12)
        TAIL_W = C * 4 * D + 12 * GU + 12 * D
        TAIL_TILES = TAIL_W // D
        vals = [region(TAIL_W + i * TT * D, TT * D).rearrange("p (t d) -> p t d", t=TT) for i in range(6)]
        x1, xn, xnT, q_n, k_n, v_n = vals
        assert TAIL_W + 6 * TT * D <= NT * D
        qT = cx[:, :, :]
        kT = pt[:, :, :, :, :].bitcast(F32).rearrange("p a b c d -> p a (b c d)")
        attT = hs[:, :, :, :].bitcast(F32).rearrange("p a c k -> p (a c k)").rearrange("p (h t) -> p h t", h=HG)
        pT = qu[:, :, :, :].bitcast(F32).rearrange("p a c k -> p (a c k)").rearrange("p (s b k) -> p s b k", s=4, b=TT)
        rope_t = wr[:, :, :, :, :].bitcast(F32).rearrange("p s a c k -> p (s a c k)")[:, 0:6 * D].rearrange("p (s d) -> p s d", s=6)

        ps = [stack.enter_context(nc.psum_tensor(f"bank{i}", [P, 512], F32)) for i in range(8)]
        U = ps[0:4]
        SC = ps[4:6]
        TP = ps[6:8]
        RED, BC = ps[7], ps[7]

        consts_in = sem("consts_in")
        x_in, wqk_in, wv_in, wi_in, wh_in = (sem(n) for n in ("x_in", "wqk_in", "wv_in", "wi_in", "wh_in"))
        ones_set = sem("ones_set")
        vec = sem("vec_step")
        pool_pow = sem("pool_pow")
        ln_stats = sem("ln_stats")
        x_normed = sem("x_normed")
        x_turned = sem("x_turned")
        slots_copied = sem("slots_copied")
        slots_high, slots_low = sem("slots_high"), sem("slots_low")
        wqk_mm, wqk_kept, wqk_sq = sem("wqk_mm"), sem("wqk_kept"), sem("wqk_sq")
        g_mm, g_kept = sem("g_mm"), sem("g_kept")
        gate_sq = sem("gate_sq")
        norm_sum = sem("norm_sum")
        norm_in = sem("norm_in")
        gate_sq_sum = sem("gate_sq_sum")
        scales_set = sem("scales_set")
        unit_high, unit_low = sem("unit_high"), sem("unit_low")
        unit_stored = [sem(f"unit_stored{i}") for i in range(WRING)]
        unit_in = [sem(f"unit_in{i}") for i in range(WRING)]
        unit_used = sem("unit_used")
        setup_done = sem("setup_done")
        ctx_in = [sem(f"ctx_in{i}") for i in range(RING)]
        row_sq, row_ms, row_r = sem("row_sq"), sem("row_ms"), sem("row_r")
        part_high, part_low = sem("part_high"), sem("part_low")
        turned, kept = sem("tile_turned"), sem("tile_kept")
        stored = [sem(f"tile_stored{i}") for i in range(RING)]
        pt_in = [sem(f"pt_in{i}") for i in range(RING)]
        slot_sq = sem("slot_sq")
        sum_mm = sem("sum_mm")
        sum_in = sem("sum_in")
        factor = sem("factor")
        diag_set = sem("diag_set")
        bc_mm = sem("bc_mm")
        bc_kept = sem("bc_kept")
        q_kept, q_high, q_low = sem("q_kept"), sem("q_high"), sem("q_low")
        scored, maxed, nmaxed, exped = sem("scored"), sem("maxed"), sem("nmaxed"), sem("exped")
        recip = sem("recip")
        attn_set, attn_high, attn_low = sem("attn_set"), sem("attn_high"), sem("attn_low")
        updated = sem("updated")
        acc_done = sem("acc_done")
        u_kept, u_high, u_low = sem("u_kept"), sem("u_high"), sem("u_low")
        tanh_r, tanh_z, tanh_n = sem("tanh_r"), sem("tanh_z"), sem("tanh_n")
        hid_set, n_in_set, h_new = sem("hid_set"), sem("n_in_set"), sem("h_new")
        gru_step = sem("gru_step")

        wqkv_in, x1_in, wout_in, w1_in, w2_in = (sem(n) for n in ("wqkv_in", "x1_in", "wout_in", "w1_in", "w2_in"))
        y_set, out_stored = sem("y_set"), sem("out_stored")
        back_turned, x1_set, xn_set, xn_turned, xnT_set = (sem(n) for n in ("back_turned", "x1_set", "xn_set", "xn_turned", "xnT_set"))
        qkv_mm, qkv_kept = sem("qkv_mm"), sem("qkv_kept")
        rope_sq, head_ms, head_r, qk_set = sem("rope_sq"), sem("head_ms"), sem("head_r"), sem("qk_set")
        qk_turned, qk_kept = sem("qk_turned"), sem("qk_kept")
        s_mm, s_max, s_exp, p_set, p_turned, p_kept, pv_mm, att_kept = (
            sem(n) for n in ("s_mm", "s_max", "s_exp", "p_set", "p_turned", "p_kept", "pv_mm", "att_kept"))
        o_mm = sem("o_mm")
        z_mm, z_tanh, l_sub, l_exp, w_set, w_turned, wT_kept = (
            sem(n) for n in ("z_mm", "z_tanh", "l_sub", "l_exp", "w_set", "w_turned", "wT_kept"))
        h_mm, h_act, wb_mm, hw_set, y_mm = (sem(n) for n in ("h_mm", "h_act", "wb_mm", "hw_set", "y_mm"))
        steps = [(hg, hh, i) for hg in range(HG) for hh in range(4) for i in range(TT)]
        NS = len(steps)
        LEAD = 3
        LEAD_T = 3
        LEAD_S = RING
        pick_set = sem("pick_set")
        head_sum = sem("head_sum")
        mask_set, identb_set = sem("mask_set"), sem("identb_set")
        z_step, rope_step = sem("z_step"), sem("rope_step")
        junk = sb("junk", [P, D], F16)
        gb = sb("gb", [P, 3 * C])
        qk_rot = sem("qk_rot")

        def TPB(j):
            return j % 2

        def GB(a):
            return ps[4:8] if a % 2 == 0 else ps[0:4]

        def keep_pT(act, n):
            w = (steps[n][2] + 1) * P
            act.wait_ge(p_turned, n + 1)
            if n >= 4:
                act.wait_ge(pv_mm, n - 3)
            act.activation(pT[:, n % 4].rearrange("p b k -> p (b k)")[:, 0:w], ps[4 + n % 2][:, 0:w], ACT.Copy)\
                .then_inc(p_kept, 1)

        block = stack.enter_context(nc.Block())

        def iterations(eng, body):
            body(0, True)
            with eng.Fori(1, ITERS) as it:
                body(it, False)

        def tiles(eng, body, first=0, last=NG):
            with eng.Fori(first, last) as g:
                for j in range(RING):
                    body(g, j)

        def ahead(g, j, k):
            return g + (j + k) // RING, (j + k) % RING

        def gate_unit(g, j):
            return w_units[:, bass.ds((g * GATE_LANES + j) * GU, GU)]

        def is_first(g):
            return isinstance(g, int) and g == 0

        @block.sync
        def _(sp):
            sp.dma_start(sm[:, :], small).then_inc(consts_in, 16)
            sp.dma_start(hf[:, :], half).then_inc(consts_in, 16)
            sp.dma_start(x_s, x[0].rearrange("(t p) d -> p t d", p=P)).then_inc(x_in, 16)
            sp.dma_start(wq_s, wq.rearrange("(c p) e -> p c e", p=P)).then_inc(wqk_in, 16)
            sp.dma_start(wk_s, wk.rearrange("(c p) e -> p c e", p=P)).then_inc(wqk_in, 16)
            sp.dma_start(winb, win_b).then_inc(wqk_in, 16)
            sp.dma_start(pj[:, :], proj_t).then_inc(consts_in, 16)
            sp.dma_start(wv_s, wv.rearrange("(c p) e -> p c e", p=P)).then_inc(wv_in, 16)
            sp.dma_start(wiT, wi_t.rearrange("(c p) e -> p c e", p=P)).then_inc(wi_in, 16)
            for a in range(C):
                sp.dma_start(w_all[:, a, 0:3], wh_u[:, a]).then_inc(wh_in, 16)

            ctx_v = ctx[0].rearrange("(p t) d -> p (t d)", t=NT)

            def load_ctx(g, j):
                sp.dma_start(cx[:, j, :], ctx_v[:, bass.ds((g * RING + j) * D, D)]).then_inc(ctx_in[j], 16)

            for j in range(RING):
                load_ctx(0, j)
            for u in range(QK_UNITS):
                sp.wait_ge(unit_low, u + 1)
                sp.dma_start(wu_dram[u], wr[:, u].rearrange("p a c e -> p (a c e)")).then_inc(unit_stored[u], 16)

            def load_units(it, first, last):
                for u in range(first, last):
                    if is_first(it) and u < WRING:
                        sp.wait_ge(unit_stored[u], 16 if u < QK_UNITS else 16 * GATE_GROUPS)
                    else:
                        sp.wait_ge(unit_used, it * UNITS + (u - WRING + 1))
                    sp.dma_start(wr[:, u % WRING].rearrange("p a c e -> p (a c e)"), wu_dram[u])\
                        .then_inc(unit_in[u % WRING], 16)

            load_units(0, 0, QK_UNITS)

            def store_tile(g, j):
                sp.wait_ge(kept, g * RING + j + 1)
                sp.dma_start(pt_dram[bass.ds(g * RING + j, 1)].rearrange("a p n -> p (a n)"),
                             pt[:, j].rearrange("p a c e -> p (a c e)")).then_inc(stored[j], 16)

            def store_unit(g, j):
                sp.wait_ge(unit_low, g * GATE_LANES + (QK_UNITS + j + 1))
                sp.dma_start(wu_dram[bass.ds(g * GATE_LANES + (QK_UNITS + j), 1)].rearrange("a p n -> p (a n)"),
                             wr[:, QK_UNITS + j].rearrange("p a c e -> p (a c e)")).then_inc(unit_stored[QK_UNITS + j], 16)

            def store_and_load(g, j):
                sp.wait_ge(part_low, g * RING + j + 1)
                load_ctx(g + 1, j)
                store_tile(g, j)

            def store_all(g, j):
                store_and_load(g, j)
                if j < GATE_LANES:
                    store_unit(g - 1, j)

            for j in range(RING):
                store_and_load(0, j)
            tiles(sp, store_all, 1, GATE_GROUPS + 1)
            tiles(sp, store_and_load, GATE_GROUPS + 1, NG - 1)
            for j in range(RING):
                store_tile(NG - 1, j)
            for s in stored:
                sp.wait_ge(s, 16 * (NG))
            for u in range(QK_UNITS, WRING):
                sp.wait_ge(unit_stored[u], 16 * GATE_GROUPS)
            load_units(0, QK_UNITS, UNITS)

            def load_pt(it, g, j):
                sp.wait_ge(scored, it * NT + (g * RING + (j + 1 - RING)))
                sp.dma_start(pt[:, j].rearrange("p a c e -> p (a c e)"),
                             pt_dram[bass.ds(g * RING + j, 1)].rearrange("a p n -> p (a n)")).then_inc(pt_in[j], 16)

            with sp.Fori(1, ITERS) as it:
                load_units(it, 0, QK_UNITS)
                tiles(sp, lambda g, j: load_pt(it, g, j))
                load_units(it, QK_UNITS, UNITS)
            for i in range(TT):
                sp.wait_ge(y_set, i + 1)
                sp.dma_start(out[0, i * P:(i + 1) * P, :], x1[:, i]).then_inc(out_stored, 16)
            sp.wait_ge(out_stored, 16 * TT)


        @block.gpsimd
        def _(pool):
            pool.memset(ones[:, :], 1.0).then_inc(ones_set, 1)
            pool.memset(st[:, 0:1], -0.5).then_inc(ones_set, 1)
            pool.memset(st[:, 1:2], EPS / S_X ** 2).then_inc(ones_set, 1)
            pool.wait_ge(ones_set, 3)

            def power(src, dst, n, done):
                pool.tensor_tensor(dst, src, st[:, 0:1].to_broadcast([P, n]), ALU.pow).then_inc(done, 1)

            pool.wait_ge(ln_stats, 1)
            power(st[:, 8:12], st[:, 12:16], 4, pool_pow)
            pool.wait_ge(norm_in, 1)
            power(st[:, 16:17], st[:, 18:19], 1, pool_pow)
            pool.wait_ge(norm_in, 2)
            power(st[:, 17:18], st[:, 19:20], 1, pool_pow)

            def iteration(it, first):
                pool.wait_ge(sum_in, it + 1)
                power(st[:, 32:36], st[:, 36:40], 4, factor)
                pool.memset(acc[:, :], 0.0).then_inc(acc_done, 1)

                def row_scale(g, j):
                    pool.wait_ge(row_sq, g * RING + j + 1)
                    pool.tensor_tensor(st[:, 44 + j:45 + j], st[:, 40 + j:41 + j], st[:, 1:2], ALU.add).then_inc(row_ms, 1)
                    pool.wait_ge(row_ms, g * RING + j + 1)
                    power(st[:, 44 + j:45 + j], st[:, 48 + j:49 + j], 1, row_r)

                def add(g, j):
                    T = it * NT + g * RING + j
                    pool.wait_ge(attn_set, T + 1)
                    pool.wait_ge(acc_done, T + it + 2)
                    pool.tensor_tensor(acc[:, :], acc[:, :], ea[:, 2 + j % 2], ALU.add).then_inc(acc_done, 1)

                def with_scale(g, j):
                    row_scale(*ahead(g, j, LEAD_S))
                    add(g, j)

                if first:
                    for j in range(LEAD_S):
                        row_scale(0, j)
                    tiles(pool, with_scale, 0, NG - 1)
                    for j in range(RING):
                        add(NG - 1, j)
                else:
                    tiles(pool, add)

            pool.sem_inc(acc_done, 1)
            pool.memset(maskb, 0.0).then_inc(mask_set, 1)
            pool.wait_ge(mask_set, 1)
            pool.affine_select(out=maskb, in_=maskb, compare_op=ALU.is_ge, fill=-1e30, base=0,
                               pattern=[[-1, P]], channel_multiplier=1).then_inc(mask_set, 1)
            iterations(pool, iteration)
            pool.wait_ge(updated, ITERS * NT)
            pool.dma_start(x1, x[0].rearrange("(t p) d -> p t d", p=P)).then_inc(x1_in, 16)
            pool.dma_start(wqkv_s, wqkv_t.rearrange("(c p) e -> p c e", p=P)).then_inc(wqkv_in, 16)
            pool.dma_start(wout_s, wout_t.rearrange("(c p) e -> p c e", p=P)).then_inc(wout_in, 16)
            pool.dma_start(w1_s, w1_t.rearrange("(c p) e -> p c e", p=P)).then_inc(w1_in, 16)
            pool.dma_start(w2_s, w2.rearrange("(q p) e -> p q e", p=P)).then_inc(w2_in, 16)
            for n in range(2):
                pool.wait_ge(ln_stats, 2 + n)
                power(st[:, 8:12], st[:, 12:16], 4, pool_pow)
                if n == 0:
                    for i in range(2 * TT):
                        pool.wait_ge(head_ms, i + 1)
                        power(rope_t[:, 5, (i % 2) * 64:(i % 2) * 64 + H], rope_t[:, 5, (i % 2) * 64 + 16:(i % 2) * 64 + 16 + H],
                              H, head_r)

        @block.scalar
        def _(act):
            def split_high(dst, src, scale, done):
                act.activation(dst, src, ACT.Copy, scale=scale).then_inc(done, 1)

            act.wait_ge(consts_in, 48)
            act.wait_ge(wqk_kept, C)
            act.activation(ea[:, :, :], wqk, ACT.Square, accum_out=st[:, 20:21]).then_inc(wqk_sq, 1)
            for c in range(C):
                act.wait_ge(x_turned, c + 1)
                act.activation(h32[:, c], ps[c][:, :], ACT.Copy).then_inc(slots_copied, 1)
                act.wait_ge(slots_copied, c + 1)
                split_high(hs[:, 0, c], h32[:, c], S_X, slots_high)
            for n in range(3 * C):
                c, gt = n // 3, n % 3
                act.wait_ge(g_mm, n + 1)
                act.activation(w_all[:, :, 3 + gt, c, :], ps[4 + n % 4][:, :].rearrange("p (a e) -> p a e", a=C),
                               ACT.Copy, scale=sm[:, WIN + c:WIN + c + 1]).then_inc(g_kept, 1)
                act.wait_ge(g_kept, n + 1)
                if n == 0:
                    act.wait_ge(wqk_sq, 1)
                act.wait_ge(gate_sq, n + min(C, max(0, n - 3)))
                act.activation(ea[:, 0].rearrange("p (a e) -> p a e", a=C), w_all[:, :, 3 + gt, c, :], ACT.Square,
                               accum_out=st[:, 56 + n:57 + n]).then_inc(gate_sq, 1)
                if 3 <= n < 3 + C:
                    a = n - 3
                    act.wait_ge(wh_in, 16 * C)
                    act.wait_ge(gate_sq, n + 1 + a)
                    act.activation(ea[:, 0:3].rearrange("p a k -> p (a k)"),
                                   w_all[:, a, 0:3].rearrange("p g c e -> p (g c e)"), ACT.Square,
                                   accum_out=st[:, 68 + a:69 + a]).then_inc(gate_sq, 1)
                if n == 5:
                    act.wait_ge(scales_set, 1)
                    for u in range(QK_UNITS):
                        split_high(wr[:, u, 0], wqk[:, :, u * P:(u + 1) * P], st[:, 24:25], unit_high)
            def gate_high(g, j):
                if is_first(g):
                    act.wait_ge(scales_set, 2)
                else:
                    act.wait_ge(unit_stored[QK_UNITS + j], 16 * g)
                act.activation(wr[:, QK_UNITS + j, 0].rearrange("p c e -> p (c e)"), gate_unit(g, j), ACT.Copy,
                               scale=st[:, 26:27]).then_inc(unit_high, 1)

            def iteration(it, first):
                if first:
                    act.wait_ge(slots_copied, C)
                    act.wait_ge(gate_sq, 4 * C)
                else:
                    act.wait_ge(h_new, C * it)
                act.activation(ea[:, :, :], h32[:, :, :], ACT.Square).then_inc(slot_sq, 1)
                for f in range(C):
                    act.wait_ge(q_kept, C * it + f + 1)
                    split_high(qu[:, 0, f], ea[:, f], 1.0, q_high)

                def square(g, j):
                    act.wait_ge(ctx_in[j], 16 * g + 16)
                    act.activation(junk[:, :], cx[:, j, :], ACT.Square, scale=D ** -0.5 / S_X, accum_out=st[:, 40 + j:41 + j]).then_inc(row_sq, 1)

                def keep(g, j):
                    act.wait_ge(turned, g * RING + j + 1)
                    if not is_first(g):
                        act.wait_ge(stored[j], 16 * g)
                    act.activation(pt[:, j].rearrange("p a c e -> p (a c e)"), TP[j % 2][:, :].bitcast(F16), ACT.Copy)\
                        .then_inc(kept, 1)

                def soft(g, j):
                    act.wait_ge(nmaxed, it * NT + g * RING + j + 1)
                    act.activation(ea[:, j % 2], SC[j % 2][:, :], ACT.Exp, bias=st[:, 80 + j % 2:81 + j % 2],
                                   scale=st[:, 25:26], accum_out=st[:, 84 + j % 2:85 + j % 2]).then_inc(exped, 1)

                def high(g, j):
                    act.wait_ge(attn_set, it * NT + g * RING + j + 1)
                    act.activation(ah[:, j % 2, 0], ea[:, 2 + j % 2], ACT.Copy).then_inc(attn_high, 1)

                def plain(g, j):
                    soft(g, j)
                    high(g, j)

                def full(g, j):
                    soft(g, j)
                    square(*ahead(g, j, LEAD_S))
                    high(g, j)
                    keep(*ahead(g, j, 2))

                if first:
                    for j in range(LEAD_S):
                        if j:
                            act.wait_ge(row_sq, j)
                        square(0, j)
                    keep(0, 0)
                    keep(0, 1)
                    def with_gates(g, j):
                        full(g, j)
                        if j < GATE_LANES:
                            gate_high(g, j)

                    for j in range(RING):
                        with_gates(0, j)
                    tiles(act, with_gates, 1, GATE_GROUPS)
                    tiles(act, full, GATE_GROUPS, NG - 1)
                    for j in range(RING):
                        soft(NG - 1, j)
                        high(NG - 1, j)
                        if j + 2 < RING:
                            keep(NG - 1, j + 2)
                else:
                    tiles(act, plain)
                for c in range(C):
                    act.wait_ge(u_kept, C * it + c + 1)
                    split_high(qu[:, 0, c], ea[:, c], 1.0, u_high)
                for a in range(C):
                    n = C * it + a
                    unit = it * UNITS + QK_UNITS + 6 * a
                    act.wait_ge(unit_used, unit + 4)
                    if a == 0:
                        act.wait_ge(u_low, C * (it + 1))
                    else:
                        act.wait_ge(h_new, n)
                    A = GB(a)
                    act.activation(ea[:, 0], A[0][:, :], ACT.Tanh, bias=gb[:, a:a + 1],
                                   scale=st[:, 27:28]).then_inc(tanh_r, 1)
                    act.wait_ge(unit_used, unit + 5)
                    act.activation(ea[:, 1], A[1][:, :], ACT.Tanh, bias=gb[:, C + a:C + a + 1],
                                   scale=st[:, 27:28]).then_inc(tanh_z, 1)
                    act.wait_ge(n_in_set, n + 1)
                    act.activation(ea[:, 3], ea[:, 2], ACT.Tanh, bias=sm[:, BI + 8 + a:BI + 9 + a]).then_inc(tanh_n, 1)
                act.wait_ge(unit_used, it * UNITS + UNITS - 3)
                for c in range(C):
                    act.wait_ge(h_new, C * it + c + 1)
                    split_high(hs[:, 0, c], h32[:, c], S_X, slots_high)

            iterations(act, iteration)

            for i in range(2 * TT):
                act.wait_ge(qk_rot, i + 1)
                act.activation(rope_t[:, 3 + i % 2], rope_t[:, i % 2], ACT.Square).then_inc(rope_sq, 1)
            for n in range(NS):
                _, _, i = steps[n]
                w = (i + 1) * P
                act.wait_ge(s_max, n + 1)
                act.activation(ea[:, n % 4, 0:w], ps[n % 4][:, 0:w], ACT.Exp, bias=st[:, 56 + n % 4:57 + n % 4],
                               accum_out=st[:, 60 + n % 4:61 + n % 4]).then_inc(s_exp, 1)
                if n >= 2:
                    keep_pT(act, n - 2)
            for n in range(NS - 2, NS):
                keep_pT(act, n)
            act.wait_ge(z_mm, 1)
            act.activation(rope_t[:, 0, 0:TT * NE], ps[0][:, 0:TT * NE], ACT.Tanh, scale=1 / QUANT_TEMP).then_inc(z_tanh, 1)
            act.wait_ge(l_sub, 1)
            act.activation(rope_t[:, 2, 128:128 + TT * NE], rope_t[:, 2, 64:64 + TT * NE], ACT.Exp).then_inc(l_exp, 1)
            for q in range(12):
                act.wait_ge(h_mm, q + 1)
                if q >= 2:
                    act.wait_ge(hw_set, q - 1)
                act.activation(ea[:, q % 2], ps[4 + q % 2][:, :], ACT.Gelu_apprx_tanh).then_inc(h_act, 1)

        @block.vector
        def _(dve):
            count = [0]

            def step(ins):
                count[0] += 1
                ins.then_inc(vec, 1)
                dve.wait_ge(vec, count[0])

            def split_low(dst, src, scale, high, done):
                dve.scalar_tensor_tensor(dst, src, scale, high, ALU.mult, ALU.subtract).then_inc(done, 1)

            def layer_norm(src, dst, n, done):
                for i in range(TT):
                    step(dve.bn_stats(st[:, 96:102], src[:, i]))
                    step(dve.bn_aggr(st[:, 102:104], st[:, 96:102]))
                    step(dve.tensor_copy(st[:, 4 + i:5 + i], st[:, 102:103]))
                    ins = dve.tensor_scalar(st[:, 8 + i:9 + i], st[:, 103:104], LN_EPS, None, ALU.add)
                    if i < TT - 1:
                        step(ins)
                ins.then_inc(ln_stats, 1)
                dve.wait_ge(pool_pow, n)
                for i in range(TT):
                    dve.tensor_scalar(dst[:, i], src[:, i], st[:, 4 + i:5 + i], st[:, 12 + i:13 + i],
                                      ALU.subtract, ALU.mult).then_inc(done, 1)

            dve.wait_ge(x_in, 16)
            layer_norm(x_s, x_s, 1, x_normed)
            dve.wait_ge(consts_in, 48)
            dve.tensor_copy(identb, ident).then_inc(identb_set, 1)
            for c in range(C):
                dve.wait_ge(wqk_mm, c + 1)
                dve.wait_ge(wqk_in, 48)
                dve.scalar_tensor_tensor(wqk[:, c], ps[c][:, :], sm[:, WSLOT + c:WSLOT + c + 1], winb,
                                         ALU.mult, ALU.mult).then_inc(wqk_kept, 1)
            step(dve.tensor_tensor(gb[:, 0:8], sm[:, BI:BI + 8], sm[:, BH:BH + 8], ALU.add))
            step(dve.tensor_scalar(gb[:, 0:8], gb[:, 0:8], 0.5, None, ALU.mult))
            step(dve.tensor_scalar(gb[:, 8:12], sm[:, BH + 8:BH + 12], 0.5, None, ALU.mult))
            for c in range(C):
                dve.wait_ge(slots_high, c + 1)
                split_low(hs[:, 1, c], h32[:, c], S_X, hs[:, 0, c], slots_low)
            dve.wait_ge(norm_sum, 1)
            dve.tensor_scalar(st[:, 16:17], ps[0][:, 0:1], S_W ** -2, TINY, ALU.mult, ALU.add).then_inc(norm_in, 1)
            dve.wait_ge(pool_pow, 2)
            step(dve.reciprocal(st[:, 22:23], st[:, 18:19]))
            step(dve.tensor_scalar(st[:, 25:26], st[:, 22:23], SCALE * S_W / S_X ** 2, None, ALU.mult))
            step(dve.tensor_scalar(st[:, 28:29], st[:, 25:26], -1.0, None, ALU.mult))
            dve.tensor_copy(st[:, 24:25], st[:, 18:19]).then_inc(scales_set, 1)
            for u in range(QK_UNITS):
                dve.wait_ge(unit_high, u + 1)
                split_low(wr[:, u, 1], wqk[:, :, u * P:(u + 1) * P], st[:, 24:25], wr[:, u, 0], unit_low)
            dve.wait_ge(gate_sq, 4 * C)
            dve.reduce_sum(st[:, 21:22], st[:, 56:56 + 4 * C], AX.X).then_inc(gate_sq_sum, 1)
            dve.wait_ge(norm_sum, 2)
            dve.tensor_scalar(st[:, 17:18], ps[0][:, 8:9], S_W ** -2, TINY, ALU.mult, ALU.add).then_inc(norm_in, 1)
            dve.wait_ge(pool_pow, 3)
            step(dve.reciprocal(st[:, 23:24], st[:, 19:20]))
            step(dve.tensor_scalar(st[:, 29:30], st[:, 23:24], 1 / S_X, None, ALU.mult))
            step(dve.tensor_scalar(st[:, 27:28], st[:, 23:24], 0.5 / S_X, None, ALU.mult))
            dve.tensor_copy(st[:, 26:27], st[:, 19:20]).then_inc(scales_set, 1)

            def gate_low(g, j):
                dve.wait_ge(unit_high, g * GATE_LANES + (QK_UNITS + j + 1))
                split_low(wr[:, QK_UNITS + j, 1].rearrange("p c e -> p (c e)"), gate_unit(g, j), st[:, 26:27],
                          wr[:, QK_UNITS + j, 0].rearrange("p c e -> p (c e)"), unit_low)

            def iteration(it, first):
                def spread(n):
                    for i in range(TT):
                        dve.tensor_scalar(diag[:, i], ident, st[:, 36 + i:37 + i], None, ALU.mult).then_inc(diag_set, 1)
                    dve.wait_ge(bc_mm, 2 * it + n + 1)
                    dve.tensor_copy(rb[:, :], BC[:, :]).then_inc(bc_kept, 1)
                    dve.wait_ge(bc_kept, 2 * it + n + 1)

                dve.wait_ge(sum_mm, 2 * it + 1)
                dve.tensor_scalar(st[:, 32:36], RED[:, 0:TT], 1 / D, EPS, ALU.mult, ALU.add).then_inc(sum_in, 1)
                dve.wait_ge(factor, it + 1)
                spread(0)
                for f in range(C):
                    dve.wait_ge(unit_used, it * UNITS + f + 1)
                    dve.scalar_tensor_tensor(ea[:, f], U[f][:, :], 1 / S_W, rb[:, :], ALU.mult, ALU.mult).then_inc(q_kept, 1)
                    dve.wait_ge(q_high, C * it + f + 1)
                    dve.tensor_tensor(qu[:, 1, f], ea[:, f], qu[:, 0, f], ALU.subtract).then_inc(q_low, 1)

                def prepare(g, j):
                    t = g * RING + j
                    dve.wait_ge(row_r, t + 1)
                    dve.tensor_scalar(pn_tile(t, 0), cx[:, j], st[:, 48 + j:49 + j], None, ALU.mult).then_inc(part_high, 1)
                    dve.wait_ge(part_high, t + 1)
                    split_low(pn_tile(t, 1), cx[:, j], st[:, 48 + j:49 + j], pn_tile(t, 0), part_low)

                def maximum(g, j):
                    T, b = it * NT + g * RING + j, j % 2
                    dve.wait_ge(scored, T + 1)
                    dve.reduce_max(st[:, 88 + b:89 + b], SC[b][:, :], AX.X).then_inc(maxed, 1)
                    dve.wait_ge(maxed, T + 1)
                    dve.tensor_scalar(st[:, 80 + b:81 + b], st[:, 88 + b:89 + b], st[:, 28:29], None, ALU.mult)\
                        .then_inc(nmaxed, 1)

                def weights(g, j):
                    T, b = it * NT + g * RING + j, j % 2
                    dve.wait_ge(exped, T + 1)
                    dve.reciprocal(st[:, 90 + b:91 + b], st[:, 84 + b:85 + b]).then_inc(recip, 1)
                    dve.wait_ge(recip, T + 1)
                    dve.wait_ge(acc_done, T + it + 1)
                    dve.tensor_scalar(ea[:, 2 + b], ea[:, b], st[:, 90 + b:91 + b], S_A, ALU.mult, ALU.mult)\
                        .then_inc(attn_set, 1)
                    dve.wait_ge(attn_high, T + 1)
                    dve.tensor_tensor(ah[:, b, 1], ea[:, 2 + b], ah[:, b, 0], ALU.subtract).then_inc(attn_low, 1)

                def plain(g, j):
                    maximum(g, j)
                    weights(g, j)

                def full(g, j):
                    maximum(g, j)
                    prepare(*ahead(g, j, LEAD_T))
                    weights(g, j)

                if first:
                    for j in range(LEAD_T):
                        prepare(0, j)

                    def with_gates(g, j):
                        maximum(g, j)
                        prepare(*ahead(g, j, LEAD_T))
                        if 0 < j <= GATE_LANES:
                            gate_low(g, j - 1)
                        weights(g, j)

                    tiles(dve, with_gates, 0, GATE_GROUPS)
                    tiles(dve, full, GATE_GROUPS, NG - 1)
                    for j in range(RING):
                        maximum(NG - 1, j)
                        if j + LEAD_T < RING:
                            prepare(NG - 1, j + LEAD_T)
                        weights(NG - 1, j)
                else:
                    tiles(dve, plain)
                dve.wait_ge(sum_mm, 2 * it + 2)
                dve.tensor_scalar(st[:, 32:36], RED[:, 0:TT], EPS * S_A, None, ALU.add).then_inc(gru_step, 1)
                dve.wait_ge(gru_step, 2 * it + 1)
                dve.reciprocal(st[:, 36:40], st[:, 32:36]).then_inc(gru_step, 1)
                dve.wait_ge(gru_step, 2 * it + 2)
                spread(1)
                for c in range(C):
                    dve.tensor_tensor(ea[:, c], U[c][:, :], rb[:, :], ALU.mult).then_inc(u_kept, 1)
                    dve.wait_ge(u_high, C * it + c + 1)
                    dve.tensor_tensor(qu[:, 1, c], ea[:, c], qu[:, 0, c], ALU.subtract).then_inc(u_low, 1)
                for a in range(C):
                    n = C * it + a
                    A = GB(a)
                    unit = it * UNITS + QK_UNITS + 6 * a
                    dve.wait_ge(unit_used, unit + 3)
                    dve.wait_ge(tanh_r, n + 1)
                    dve.tensor_scalar(ea[:, 2], A[2][:, :], st[:, 27:28], gb[:, 8 + a:9 + a], ALU.mult, ALU.add).then_inc(hid_set, 1)
                    dve.wait_ge(hid_set, 2 * n + 1)
                    dve.scalar_tensor_tensor(ea[:, 2], ea[:, 0], 1.0, ea[:, 2], ALU.add, ALU.mult).then_inc(hid_set, 1)
                    dve.wait_ge(hid_set, 2 * n + 2)
                    dve.wait_ge(unit_used, unit + 6)
                    dve.scalar_tensor_tensor(ea[:, 2], A[3][:, :], st[:, 29:30], ea[:, 2], ALU.mult, ALU.add).then_inc(n_in_set, 1)
                    dve.wait_ge(tanh_n, n + 1)
                    dve.wait_ge(tanh_z, n + 1)
                    dve.tensor_tensor(ea[:, 2], h32[:, a], ea[:, 3], ALU.subtract).then_inc(z_step, 1)
                    dve.wait_ge(z_step, 2 * n + 1)
                    dve.scalar_tensor_tensor(ea[:, 2], ea[:, 1], 1.0, ea[:, 2], ALU.add, ALU.mult).then_inc(z_step, 1)
                    dve.wait_ge(z_step, 2 * n + 2)
                    dve.scalar_tensor_tensor(h32[:, a], ea[:, 2], 0.5, ea[:, 3], ALU.mult, ALU.add).then_inc(h_new, 1)
                for c in range(C):
                    dve.wait_ge(slots_high, C * (it + 1) + c + 1)
                    split_low(hs[:, 1, c], h32[:, c], S_X, hs[:, 0, c], slots_low)

            iterations(dve, iteration)

            dve.wait_ge(x1_in, 16)
            for i in range(TT):
                dve.wait_ge(back_turned, i + 1)
                dve.tensor_tensor(x1[:, i], x1[:, i], ps[i][:, :], ALU.add).then_inc(x1_set, 1)
            dve.wait_ge(x1_set, TT)
            layer_norm(x1, xn, 4, xn_set)
            for c in range(C):
                dve.wait_ge(xn_turned, c + 1)
                dve.tensor_copy(xnT[:, c], ps[4 + c][:, :]).then_inc(xnT_set, 1)
            def rotate(n):
                i, w = n // 2, n % 2
                src = ps[(3 * i + w) % 8][:, :]
                cos = sm[:, COS + i * HD:COS + (i + 1) * HD].unsqueeze(1).to_broadcast([P, H, HD])
                sn = sm[:, SIN + i * HD:SIN + (i + 1) * HD].rearrange("p (s d) -> p s d", s=2)
                sh = src.rearrange("p (h s d) -> p h s d", h=H, s=2)
                sw = rope_t[:, 2].rearrange("p (h s d) -> p h s d", h=H, s=2)
                rot = rope_t[:, n % 2]
                dve.wait_ge(qkv_mm, 3 * i + w + 1)
                if n >= 2:
                    dve.wait_ge(qk_set, n - 1)
                dve.tensor_tensor(rot.rearrange("p (h d) -> p h d", h=H), src.rearrange("p (h d) -> p h d", h=H),
                                  cos, ALU.mult).then_inc(rope_step, 1)
                if n >= 1:
                    dve.wait_ge(qk_rot, n)
                for s in range(2):
                    dve.tensor_tensor(sw[:, :, s], sh[:, :, 1 - s], sn[:, s].unsqueeze(1).to_broadcast([P, H, HD // 2]),
                                      ALU.mult).then_inc(rope_step, 1)
                dve.wait_ge(rope_step, 3 * n + 3)
                dve.tensor_tensor(rot, rot, rope_t[:, 2], ALU.add).then_inc(qk_rot, 1)
                if w == 1:
                    dve.wait_ge(qkv_mm, 3 * i + 3)
                    dve.tensor_copy(v_n[:, i], ps[(3 * i + 2) % 8][:, :]).then_inc(qkv_kept, 1)

            def head_norm(n):
                dst, o = (q_n, k_n)[n % 2][:, n // 2], (n % 2) * 64
                ms, r = rope_t[:, 5, o:o + H], rope_t[:, 5, o + 16:o + 16 + H]
                dve.wait_ge(rope_sq, n + 1)
                dve.reduce_sum(ms, rope_t[:, 3 + n % 2].rearrange("p (h d) -> p h d", h=H), AX.X).then_inc(head_sum, 1)
                dve.wait_ge(head_sum, n + 1)
                dve.tensor_scalar(ms, ms, 1 / HD, EPS, ALU.mult, ALU.add).then_inc(head_ms, 1)

            def head_scale(n):
                dst, o = (q_n, k_n)[n % 2][:, n // 2], (n % 2) * 64
                r = rope_t[:, 5, o + 16:o + 16 + H]
                dve.wait_ge(head_r, n + 1)
                dve.tensor_tensor(dst.rearrange("p (h d) -> p h d", h=H), rope_t[:, n % 2].rearrange("p (h d) -> p h d", h=H),
                                  r.unsqueeze(2).to_broadcast([P, H, HD]), ALU.mult).then_inc(qk_set, 1)

            for n in range(2 * TT + 1):
                if n < 2 * TT:
                    if n >= 2:
                        head_scale(n - 2)
                    rotate(n)
                if n >= 1:
                    head_norm(n - 1)
            head_scale(2 * TT - 2)
            head_scale(2 * TT - 1)
            step(dve.tensor_scalar(st[:, 52:53], sm[:, QW:QW + 1], sm[:, KW:KW + 1], ATT_SCALE, ALU.mult, ALU.mult))
            for n in range(2 * HG):
                dve.wait_ge(qk_turned, n + 1)
                if n < HG:
                    dve.tensor_scalar(qT[:, n], ps[n][:, :], st[:, 52:53], None, ALU.mult).then_inc(qk_kept, 1)
                else:
                    dve.tensor_copy(kT[:, n - HG], ps[n][:, :]).then_inc(qk_kept, 1)

            def s_maximum(n):
                w = (steps[n][2] + 1) * P
                dve.wait_ge(s_mm, n + 1)
                dve.tensor_reduce(st[:, 56 + n % 4:57 + n % 4], ps[n % 4][:, 0:w], AX.X, ALU.max, negate=True).then_inc(s_max, 1)

            def s_normal(n):
                w = (steps[n][2] + 1) * P
                dve.wait_ge(s_exp, n + 1)
                step(dve.reciprocal(st[:, 72 + n % 2:73 + n % 2], st[:, 60 + n % 4:61 + n % 4]))
                dve.tensor_scalar(ea[:, n % 4, 0:w], ea[:, n % 4, 0:w], st[:, 72 + n % 2:73 + n % 2], None, ALU.mult)\
                    .then_inc(p_set, 1)

            def keep_att(hg):
                dve.wait_ge(pv_mm, 16 * hg + 16)
                dve.tensor_copy(attT[:, hg], ps[6 + hg % 2][:, :]).then_inc(att_kept, 1)

            for n in range(NS + 1):
                if n < NS:
                    s_maximum(n)
                if n >= 1:
                    s_normal(n - 1)
                if n >= 24 and (n - 24) % 16 == 0:
                    keep_att((n - 24) // 16)
            keep_att(HG - 1)
            for i in range(TT):
                dve.wait_ge(o_mm, i + 1)
                dve.tensor_tensor(x1[:, i], x1[:, i], ps[i][:, :], ALU.add).then_inc(x1_set, 1)
            dve.wait_ge(x1_set, 2 * TT)
            layer_norm(x1, xn, 5, xn_set)
            for c in range(C):
                dve.wait_ge(xn_turned, C + c + 1)
                dve.tensor_copy(xnT[:, c], ps[4 + c][:, :]).then_inc(xnT_set, 1)
            dve.tensor_copy(pick, ident[0:NE, 0:NE].unsqueeze(2).to_broadcast([NE, NE, P])).then_inc(pick_set, 1)
            q_r = rope_t[:, 0, 0:TT * NE].rearrange("p (t d) -> p t d", t=TT)
            prod = rope_t[:, 1, 0:TT * NE * NE].rearrange("p (t e d) -> p t e d", t=TT, e=NE)
            logit = rope_t[:, 2, 0:TT * NE]
            lg = logit.rearrange("p (t e) -> p t e", t=TT)
            top = rope_t[:, 2, 192:192 + TT]
            gt_, eq_ = (rope_t[:, 3, o:o + TT * NE * NE].rearrange("p (t e d) -> p t e d", t=TT, e=NE) for o in (0, 160))
            rank = rope_t[:, 3, 320:320 + TT * NE]
            shifted = rope_t[:, 2, 64:64 + TT * NE]
            ex = rope_t[:, 2, 128:128 + TT * NE]
            step(dve.tensor_scalar(st[:, 53:54], sm[:, TEMP:TEMP + 1], 0.1, None, ALU.max))
            step(dve.reciprocal(st[:, 54:55], st[:, 53:54]))
            step(dve.tensor_scalar(st[:, 54:55], st[:, 54:55], 0.5, None, ALU.mult))
            anch = sm[:, ANCH:ANCH + NE * NE].rearrange("p (e d) -> p e d", e=NE)
            lower = sm[:, LOWER:LOWER + NE * NE].rearrange("p (e d) -> p e d", e=NE)
            full4 = [P, TT, NE, NE]
            dve.wait_ge(z_tanh, 1)
            step(dve.tensor_tensor(prod, q_r.unsqueeze(2).to_broadcast(full4), anch.unsqueeze(1).to_broadcast(full4), ALU.mult))
            step(dve.reduce_sum(logit, prod.rearrange("p t e d -> p (t e) d"), AX.X))
            step(dve.tensor_scalar(logit, logit, -6.0, st[:, 54:55], ALU.add, ALU.mult))
            l_e, l_j = lg.unsqueeze(3).to_broadcast(full4), lg.unsqueeze(2).to_broadcast(full4)
            step(dve.tensor_tensor(gt_, l_j, l_e, ALU.is_gt))
            step(dve.tensor_tensor(eq_, l_j, l_e, ALU.is_equal))
            step(dve.tensor_tensor(eq_, eq_, lower.unsqueeze(1).to_broadcast(full4), ALU.mult))
            step(dve.tensor_tensor(gt_, gt_, eq_, ALU.add))
            step(dve.reduce_sum(rank, gt_.rearrange("p t e d -> p (t e) d"), AX.X))
            step(dve.tensor_scalar(rank, rank, float(TOPK), None, ALU.is_lt))
            step(dve.reduce_max(top, lg, AX.X))
            dve.tensor_tensor(shifted.rearrange("p (t e) -> p t e", t=TT), lg, top.unsqueeze(2).to_broadcast([P, TT, NE]),
                              ALU.subtract).then_inc(l_sub, 1)
            dve.wait_ge(l_exp, 1)
            step(dve.tensor_tensor(ex, ex, rank, ALU.mult))
            step(dve.reduce_sum(top, ex.rearrange("p (t e) -> p t e", t=TT), AX.X))
            step(dve.reciprocal(top, top))
            dve.tensor_tensor(shifted.rearrange("p (t e) -> p t e", t=TT), ex.rearrange("p (t e) -> p t e", t=TT),
                              top.unsqueeze(2).to_broadcast([P, TT, NE]), ALU.mult).then_inc(w_set, 1)
            dve.wait_ge(w_turned, 1)
            dve.tensor_copy(rb[0:NE, :], ps[6][0:NE, :]).then_inc(wT_kept, 1)
            for q in range(12):
                dve.wait_ge(h_act, q + 1)
                dve.wait_ge(wb_mm, q // 2 + 1)
                dve.tensor_tensor(hw_s[:, q], ea[:, q % 2], ps[6 + (q // 2) % 2][:, :], ALU.mult).then_inc(hw_set, 1)
            for i in range(TT):
                dve.wait_ge(y_mm, i + 1)
                dve.tensor_tensor(x1[:, i], x1[:, i], ps[i][:, :], ALU.add).then_inc(y_set, 1)

        @block.tensor
        def _(pe):
            def mm(o, w, r, start=True, stop=True, **kw):
                return pe.matmul(o, w, r, start=start, stop=stop, **kw)

            def turn(o, i):
                return pe.transpose(o, i, ident)

            pe.wait_ge(wqk_in, 48)
            for c in range(C):
                for k in range(C):
                    ins = mm(ps[c][:, :], wq_s[:, k, c * P:(c + 1) * P], wk_s[:, k, :], k == 0, k == C - 1)
                ins.then_inc(wqk_mm, 1)

            def gate_product(n):
                c, gt = n // 3, n % 3
                if n >= 4:
                    pe.wait_ge(g_kept, n - 3)
                for k in range(C):
                    ins = mm(ps[4 + n % 4][:, :], wv_s[:, k, c * P:(c + 1) * P], wiT[:, k, gt * D:(gt + 1) * D], k == 0, k == C - 1)
                ins.then_inc(g_mm, 1)

            pe.wait_ge(wv_in, 16)
            pe.wait_ge(wi_in, 16)
            for n in range(3):
                gate_product(n)
            pe.wait_ge(x_normed, TT)
            pe.wait_ge(consts_in, 48)
            for c in range(C):
                pe.wait_ge(wqk_kept, c + 1)
                for i in range(TT):
                    ins = turn(ps[c][:, i * P:(i + 1) * P], x_s[:, i, c * P:(c + 1) * P])
                ins.then_inc(x_turned, 1)
            for n in range(3, 6):
                gate_product(n)
            pe.wait_ge(ones_set, 1)
            pe.wait_ge(wqk_sq, 1)
            pe.wait_ge(slots_copied, 1)
            mm(ps[0][:, 0:1], ones[:, :], st[:, 20:21]).then_inc(norm_sum, 1)
            for n in range(6, 12):
                gate_product(n)
            pe.wait_ge(gate_sq_sum, 1)
            pe.wait_ge(norm_in, 1)
            mm(ps[0][:, 8:9], ones[:, :], st[:, 21:22]).then_inc(norm_sum, 1)

            def iteration(it, first):
                def unit_product(u, bank, move, starts, stops):
                    pe.wait_ge(unit_in[u % WRING], it * (16 * (UNITS // WRING)) + 16 * (u // WRING + 1))
                    for c in range(C):
                        for pi, (a, b) in enumerate(PARTS3):
                            ins = mm(bank[:, :], wr[:, u % WRING, a, c, :], move[:, b, c, :],
                                     starts and c == 0 and pi == 0, stops and c == C - 1 and pi == 2)
                    ins.then_inc(unit_used, 1)

                def slot_sums(col):
                    for i in range(TT):
                        cs = col(i)
                        for m, src in enumerate(cs):
                            ins = mm(RED[:, i:i + 1], src, ones[:, 0:1], m == 0, m == len(cs) - 1)
                    ins.then_inc(sum_mm, 1)

                def broadcast(n):
                    pe.wait_ge(diag_set, TT * (2 * it + n + 1))
                    mm(BC[:, :], ones[:, :], diag[:, :, :].rearrange("p a b -> p (a b)")).then_inc(bc_mm, 1)

                pe.wait_ge(slots_high, C * (it + 1))
                pe.wait_ge(slots_low, C * (it + 1))
                pe.wait_ge(slot_sq, it + 1)
                slot_sums(lambda i: [ea[:, c, i * P:(i + 1) * P] for c in range(C)])
                if first:
                    pe.wait_ge(norm_in, 2)
                for f in range(C):
                    unit_product(f, U[f], hs, True, True)
                    if f == 1:
                        broadcast(0)
                pe.wait_ge(q_high, C * (it + 1))
                pe.wait_ge(q_low, C * (it + 1))
                pe.wait_ge(bc_kept, 2 * it + 1)

                def turn_tile(g, j):
                    t = g * RING + j
                    pe.wait_ge(part_low, t + 1)
                    for a in range(2):
                        for c in range(C):
                            ins = pe.transpose(TP[j % 2][:, :].bitcast(F16)[:, (a * C + c) * P:(a * C + c + 1) * P],
                                               pn_w(t, a, c), ident16)
                    ins.then_inc(turned, 1)

                def scores(g, j):
                    if first:
                        pe.wait_ge(kept, g * RING + j + 1)
                    else:
                        pe.wait_ge(pt_in[j], (it - 1) * (16 * NG) + (16 * g + 16))
                    for c in range(C):
                        for pi, (a, b) in enumerate(PARTS3):
                            ins = mm(SC[j % 2][:, :], pt[:, j, a, c, :], qu[:, b, c, :], c == 0 and pi == 0, c == C - 1 and pi == 2)
                    ins.then_inc(scored, 1)

                def update(g, j, last=False):
                    t = g * RING + j
                    pe.wait_ge(attn_high, it * NT + t + 1)
                    pe.wait_ge(attn_low, it * NT + t + 1)
                    for c in range(C):
                        for pi, (a, b) in enumerate(PARTS3):
                            ins = mm(U[c][:, :], pn_w(t, a, c), ah[:, j % 2, b], False, last and pi == 2, skip_group_check=True)
                    ins.then_inc(updated, 1)

                if first:
                    turn_tile(0, 0)
                    turn_tile(0, 1)
                    pe.wait_ge(kept, 1)
                    turn_tile(0, 2)
                scores(0, 0)
                scores(0, 1)
                for c in range(C):
                    mm(U[c][:, :], zeros16, qu[:, 0, 0, :], True, False, skip_group_check=True)

                def turn_ahead(g, j):
                    pe.wait_ge(kept, g * RING + j + LEAD_T - 1)
                    turn_tile(*ahead(g, j, LEAD_T))

                def scores_ahead(g, j):
                    pe.wait_ge(exped, it * NT + g * RING + j + 1)
                    scores(*ahead(g, j, 2))

                def full(g, j):
                    update(g, j)
                    if first:
                        turn_ahead(g, j)
                    scores_ahead(g, j)

                tiles(pe, full, 0, NG - 1)
                for j in range(RING):
                    update(NG - 1, j, j == RING - 1)
                    if first and j + LEAD_T < RING:
                        turn_ahead(NG - 1, j)
                    if j + 2 < RING:
                        scores_ahead(NG - 1, j)

                pe.wait_ge(acc_done, it * NT + NT + it + 2)
                slot_sums(lambda i: [acc[:, i * P:(i + 1) * P]])
                for a in range(C):
                    B = GB(a)
                    u0 = QK_UNITS + 6 * a
                    n = C * it + a
                    if a >= 2:
                        pe.wait_ge(h_new, n - 1)
                    if a == 1:
                        pe.wait_ge(u_low, C * (it + 1))
                    unit_product(u0, B[0], hs, True, False)
                    if a == 0:
                        broadcast(1)
                    unit_product(u0 + 1, B[1], hs, True, False)
                    unit_product(u0 + 2, B[2], hs, True, True)
                    if a == 0:
                        pe.wait_ge(u_high, C * (it + 1))
                        pe.wait_ge(u_low, C * (it + 1))
                        pe.wait_ge(bc_kept, 2 * it + 2)
                    unit_product(u0 + 3, B[0], qu, False, True)
                    unit_product(u0 + 4, B[1], qu, False, True)
                    unit_product(u0 + 5, B[3], qu, True, True)

            iterations(pe, iteration)

            pe.wait_ge(h_new, C * ITERS)
            for i in range(TT):
                for c in range(C):
                    ins = turn(ps[i][:, c * P:(c + 1) * P], h32[:, c, i * P:(i + 1) * P])
                ins.then_inc(back_turned, 1)

            def turn_xn(n):
                pe.wait_ge(xn_set, TT * (n + 1))
                for c in range(C):
                    for i in range(TT):
                        ins = turn(ps[4 + c][:, i * P:(i + 1) * P], xn[:, i, c * P:(c + 1) * P])
                    ins.then_inc(xn_turned, 1)
                pe.wait_ge(xnT_set, C * (n + 1))

            turn_xn(0)
            pe.wait_ge(wqkv_in, 16)
            for i in range(TT):
                for w in range(3):
                    n = 3 * i + w
                    if n >= 8:
                        m = n - 8
                        pe.wait_ge(qk_set, 2 * (m // 3) + min(m % 3 + 1, 2))
                        if m % 3 == 2:
                            pe.wait_ge(qkv_kept, m // 3 + 1)
                    for c in range(C):
                        ins = mm(ps[n % 8][:, :], xnT[:, c, i * P:(i + 1) * P], wqkv_s[:, c, w * D:(w + 1) * D], c == 0, c == C - 1)
                    ins.then_inc(qkv_mm, 1)
            pe.wait_ge(qk_set, 2 * TT)
            pe.wait_ge(qkv_kept, TT)
            for n in range(2 * HG):
                src = q_n if n < HG else k_n
                for i in range(TT):
                    ins = turn(ps[n][:, i * P:(i + 1) * P], src[:, i, (n % HG) * P:(n % HG + 1) * P])
                ins.then_inc(qk_turned, 1)
            pe.wait_ge(qk_kept, 2 * HG)
            pe.wait_ge(mask_set, 2)
            pe.wait_ge(identb_set, 1)

            def s_product(n):
                hg, hh, i = steps[n]
                w = (i + 1) * P
                r = slice(HD * hh, HD * hh + HD)
                if n >= 4:
                    pe.wait_ge(s_exp, n - 3)
                mm(ps[n % 4][:, 0:w], qT[r, hg, i * P:(i + 1) * P], kT[r, hg, 0:w], True, False,
                   tile_position=(HD * hh, 0), skip_group_check=True)
                mm(ps[n % 4][:, i * P:w], identb, maskb, False, True, skip_group_check=True).then_inc(s_mm, 1)

            def turn_p(n):
                i = steps[n][2]
                pe.wait_ge(p_set, n + 1)
                if n >= 2:
                    pe.wait_ge(p_kept, n - 1)
                for b in range(i + 1):
                    ins = turn(ps[4 + n % 2][:, b * P:(b + 1) * P], ea[:, n % 4, b * P:(b + 1) * P])
                ins.then_inc(p_turned, 1)

            def pv(n):
                hg, hh, i = steps[n]
                pe.wait_ge(p_kept, n + 1)
                if hg >= 2 and hh == 0 and i == 0:
                    pe.wait_ge(att_kept, hg - 1)
                for b in range(i + 1):
                    ins = mm(ps[6 + hg % 2][HD * hh:HD * hh + HD, i * P:(i + 1) * P],
                             v_n[:, b, (4 * hg + hh) * HD:(4 * hg + hh + 1) * HD], pT[:, n % 4, b], b == 0, b == i,
                             tile_position=(0, HD * hh), skip_group_check=True)
                ins.then_inc(pv_mm, 1)

            for n in range(LEAD):
                s_product(n)
            for n in range(NS + 2):
                if n + LEAD < NS:
                    s_product(n + LEAD)
                if n < NS:
                    turn_p(n)
                if n >= 2:
                    pv(n - 2)
            pe.wait_ge(att_kept, HG)
            pe.wait_ge(wout_in, 16)
            for i in range(TT):
                for g in range(HG):
                    ins = mm(ps[i][:, :], attT[:, g, i * P:(i + 1) * P], wout_s[:, g, :], g == 0, g == HG - 1)
                ins.then_inc(o_mm, 1)
            turn_xn(1)
            for i in range(TT):
                for c in range(C):
                    ins = mm(ps[0][:, i * NE:(i + 1) * NE], xnT[:, c, i * P:(i + 1) * P], pj[:, c * NE:(c + 1) * NE], c == 0, c == C - 1)
            ins.then_inc(z_mm, 1)
            pe.wait_ge(w1_in, 16)
            pe.wait_ge(w2_in, 16)

            def hidden(q):
                if q >= 2:
                    pe.wait_ge(h_act, q - 1)
                for c in range(C):
                    ins = mm(ps[4 + q % 2][:, :], w1_s[:, c, q * P:(q + 1) * P], xnT[:, c, :], c == 0, c == C - 1)
                ins.then_inc(h_mm, 1)

            def weight_rows(e):
                if e >= 2:
                    pe.wait_ge(hw_set, 2 * (e - 1))
                mm(ps[6 + e % 2][:, :], pick[:, e], rb[0:NE, :]).then_inc(wb_mm, 1)

            def expert_out(q):
                pe.wait_ge(hw_set, q + 1)
                for i in range(TT):
                    ins = mm(ps[i][:, :], hw_s[:, q, i * P:(i + 1) * P], w2_s[:, q, :], q == 0, q == 11)
                    if q == 11:
                        ins.then_inc(y_mm, 1)

            hidden(0)
            hidden(1)
            pe.wait_ge(w_set, 1)
            for i in range(TT):
                ins = pe.transpose(ps[6][0:NE, i * P:(i + 1) * P], rope_t[:, 2, 64 + i * NE:64 + (i + 1) * NE], ident)
            ins.then_inc(w_turned, 1)
            pe.wait_ge(wT_kept, 1)
            pe.wait_ge(pick_set, 1)
            weight_rows(0)
            weight_rows(1)
            for q in range(12):
                if q + 2 < 12:
                    hidden(q + 2)
                if q % 2 == 1 and q // 2 + 2 < NE:
                    weight_rows(q // 2 + 2)
                expert_out(q)


_INS = ['x', 'ctx', 'wq', 'wk', 'wv', 'wi_t', 'wh_u', 'win_b', 'small', 'half', 'wqkv_t', 'wout_t', 'w1_t', 'w2', 'proj_t']


def layouts(x, ctx_1024, L0_xattn_Wq, L0_xattn_Wk, L0_xattn_Wv, L0_xattn_gru_wi, L0_xattn_gru_wh,
            L0_xattn_gru_bi, L0_xattn_gru_bh, L0_xattn_slot_norm_w, L0_xattn_input_norm_w, L0_attn_w_qkv,
            L0_attn_w_out, L0_attn_q_norm_w, L0_attn_k_norm_w, L0_ffn_proj_w, L0_ffn_anchors,
            L0_ffn_routing_temp, L0_ffn_w1, L0_ffn_w2):
    f = lambda a: np.asarray(a)
    cols = lambda a, n: f(a).reshape(n, P).T
    rows = lambda a: np.broadcast_to(f(a).reshape(1, -1), (P, f(a).size))
    half = HD // 2
    inv = (1.0 / np.float32(10000.0) ** (np.arange(half, dtype=np.float32) * np.float32(2.0) / np.float32(HD))).astype(np.float32)
    ang = np.arange(K, dtype=np.float32)[:, None] * inv[None, :]
    cos, sin = np.cos(ang), np.sin(ang)
    by_tile = lambda a: a.reshape(TT, P, HD).transpose(1, 0, 2).reshape(P, TT * HD)
    cos = by_tile(np.concatenate([cos, cos], axis=1).astype(np.float32))
    sin = by_tile(np.concatenate([-sin, sin], axis=1).astype(np.float32))
    lower = rows(np.tril(np.ones((NE, NE), np.float32), -1))
    small = np.concatenate([
        cols(L0_xattn_gru_bi, 12), cols(L0_xattn_gru_bh, 12), cols(L0_xattn_slot_norm_w, C), cols(L0_xattn_input_norm_w, C),
        np.tile(f(L0_attn_q_norm_w), 4)[:, None], np.tile(f(L0_attn_k_norm_w), 4)[:, None], rows(L0_ffn_routing_temp),
        rows(L0_ffn_anchors), lower, cos, sin, np.eye(P, dtype=np.float32)], axis=1)
    wh_u = f(L0_xattn_gru_wh).reshape(3, C, P, C, P).transpose(4, 1, 0, 3, 2)
    return {
        "x": f(x), "ctx": f(ctx_1024), "wq": f(L0_xattn_Wq), "wk": f(L0_xattn_Wk), "wv": f(L0_xattn_Wv),
        "wi_t": f(L0_xattn_gru_wi).T, "wh_u": wh_u, "win_b": rows(L0_xattn_input_norm_w), "small": small,
        "half": np.concatenate([np.eye(P), np.zeros((P, P))], axis=1).astype(np.float16),
        "wqkv_t": f(L0_attn_w_qkv).T, "wout_t": f(L0_attn_w_out).T,
        "w1_t": f(L0_ffn_w1).transpose(1, 0, 2).reshape(D, NE * DE), "w2": f(L0_ffn_w2).reshape(NE * DE, D),
        "proj_t": f(L0_ffn_proj_w).reshape(NE, C, P).transpose(2, 1, 0).reshape(P, C * NE),
    }


def kernel(**inputs):
    import concourse.bacc as _bacc
    from concourse.bass_utils import run_bass_kernel_spmd as _run

    nc = _bacc.Bacc("TRN2", target_bir_lowering=False, num_devices=1)
    arrays, args = {}, []
    laid = layouts(**inputs)
    for name in _INS:
        a = np.ascontiguousarray(laid[name])
        arrays[f"in_{name}"] = a
        args.append(nc.dram_tensor(f"in_{name}", a.shape, mybir.dt.from_np(a.dtype), kind="ExternalInput").ap())
    args.append(nc.dram_tensor("out_0", (1, K, D), F32, kind="ExternalOutput").ap())
    slot_kernel(nc, *args)
    r = _run(nc, [arrays], core_ids=[0])
    return r.results[0]["out_0"]
```

```python
from contextlib import ExitStack

import numpy as np

import concourse.bass as bass
from concourse import mybir

F32 = mybir.dt.float32
F16 = mybir.dt.float16
BF16 = mybir.dt.bfloat16
ALU = mybir.AluOpType
ACT = mybir.ActivationFunctionType
AX = mybir.AxisListType

P = 128
D = 512
C = D // P
K = 512
TT = K // P
M = 8192
NT = M // P
NG = 16
RING = NT // NG
ITERS = 3
H = 16
HD = D // H
HG = H // 4
NE = 6
DE = 256
TOPK = 2
EPS = 1e-6
LN_EPS = 1e-5
QUANT_TEMP = 0.3
SCALE = float(D) ** -0.5
ATT_SCALE = float(HD) ** -0.5

S_X = 2.0 ** 10
S_A = 2.0 ** 15
S_W = 2.0 ** 15
TINY = 1e-30

G_PLACE = (3, 5, 4)
QK_UNITS = C
GATE_UNITS = 6 * C
UNITS = QK_UNITS + GATE_UNITS
WRING = 7
GATE_LANES = WRING - QK_UNITS
GATE_GROUPS = GATE_UNITS // GATE_LANES
assert GATE_UNITS % GATE_LANES == 0 and GATE_LANES < RING and GATE_GROUPS < NG - 1
assert UNITS % WRING == 0 and NT % RING == 0 and NG >= 3

BI, BH, WSLOT, WIN = 0, 12, 24, 28
QW, KW, TEMP, ANCH = 32, 33, 34, 35
LOWER = ANCH + 36
COS = LOWER + 36
SIN = COS + TT * HD
IDENT = SIN + TT * HD
SMALL = IDENT + P

PARTS3 = ((0, 0), (0, 1), (1, 0))


def slot_kernel(nc, x, ctx, wq, wk, wv, wi_t, wh_u, win_b, small, half, wqkv_t, wout_t, w1_t, w2,
                proj_t, out):
    stack = ExitStack()
    with stack:
        def sb(name, shape, dt=F32):
            return stack.enter_context(nc.sbuf_tensor(name, shape, dt))

        def sem(name):
            return stack.enter_context(nc.semaphore(name))

        pt_dram = nc.dram_tensor("pt_scratch", (NT, P, 2 * C * P), F16, kind="Internal").ap()
        wu_dram = nc.dram_tensor("weight_units", (UNITS, P, 2 * C * P), F16, kind="Internal").ap()

        pn = sb("pn", [P, NT * 2 * D], F16)
        pt = sb("pt", [P, RING, 2, C, P], F16)
        cx = sb("cx", [P, RING, D])
        wr = sb("wr", [P, WRING, 2, C, P], F16)
        h32 = sb("h32", [P, C, K])
        hs = sb("hs", [P, 2, C, K], F16)
        qu = sb("qu", [P, 2, C, K], F16)
        ea = sb("ea", [P, 4, K])
        ah = sb("ah", [P, 2, 2, K], F16)
        acc = sb("acc", [P, K])
        diag = sb("diag", [P, TT, P])
        rb = sb("rb", [P, K])
        sm = sb("sm", [P, SMALL])
        hf = sb("hf", [P, 2 * P], F16)
        bm = sb("bm", [P, 2 * P], BF16)
        ones = sb("ones", [P, P])
        st = sb("st", [P, 128])
        pj = sb("pj", [P, C * NE])
        ident = sm[:, IDENT:IDENT + P]
        ident16, zeros16 = hf[:, 0:P], hf[:, P:2 * P]
        identb, maskb = bm[:, 0:P], bm[:, P:2 * P]

        def pn_tile(t, part):
            return pn[:, bass.ds(t * (2 * D) + part * D, D)]

        def pn_w(t, part, c):
            return pn[:, bass.ds(t * (2 * D) + part * D + c * P, P)]

        pn32 = pn[:, :].bitcast(F32)

        def region(at, n):
            return pn32[:, at:at + n]

        base = NT * D
        GU = C * P
        pick = ea[:, 2:4].rearrange("p a k -> p (a k)")[0:NE, 0:NE * P].rearrange("p (e k) -> p e k", e=NE)
        def take(n):
            nonlocal base
            base -= n
            return region(base, n)
        w_all = take(GATE_UNITS * GU).rearrange("p (a g c e) -> p a g c e", a=C, g=6, c=C)
        w_units = w_all.rearrange("p a g c e -> p (a g c e)")
        wiT = take(C * 3 * D).rearrange("p (c e) -> p c e", c=C)
        wv_s = take(C * D).rearrange("p (c e) -> p c e", c=C)
        wq_s = take(C * D).rearrange("p (c e) -> p c e", c=C)
        wk_s = take(C * D).rearrange("p (c e) -> p c e", c=C)
        wqk = take(C * D).rearrange("p (c e) -> p c e", c=C)
        winb = take(D)
        x_s = take(TT * D).rearrange("p (t d) -> p t d", t=TT)
        assert base >= 4 * D
        wqkv_s = region(0, C * 3 * D).rearrange("p (c e) -> p c e", c=C)
        hw_s = region(0, 12 * K).rearrange("p (q t) -> p q t", q=12)
        wout_s = region(C * 3 * D, C * D).rearrange("p (c e) -> p c e", c=C)
        w1_s = region(C * 4 * D, 12 * GU).rearrange("p (c e) -> p c e", c=C)
        w2_s = region(C * 4 * D + 12 * GU, 12 * D).rearrange("p (q e) -> p q e", q=12)
        TAIL_W = C * 4 * D + 12 * GU + 12 * D
        TAIL_TILES = TAIL_W // D
        vals = [region(TAIL_W + i * TT * D, TT * D).rearrange("p (t d) -> p t d", t=TT) for i in range(6)]
        x1, xn, xnT, q_n, k_n, v_n = vals
        assert TAIL_W + 6 * TT * D <= NT * D
        qT = cx[:, :, :]
        kT = pt[:, :, :, :, :].bitcast(F32).rearrange("p a b c d -> p a (b c d)")
        attT = hs[:, :, :, :].bitcast(F32).rearrange("p a c k -> p (a c k)").rearrange("p (h t) -> p h t", h=HG)
        pT = qu[:, :, :, :].bitcast(F32).rearrange("p a c k -> p (a c k)").rearrange("p (s b k) -> p s b k", s=4, b=TT)
        rope_t = wr[:, :, :, :, :].bitcast(F32).rearrange("p s a c k -> p (s a c k)")[:, 0:6 * D].rearrange("p (s d) -> p s d", s=6)

        ps = [stack.enter_context(nc.psum_tensor(f"bank{i}", [P, 512], F32)) for i in range(8)]
        U = ps[0:4]
        SC = ps[4:6]
        TP = ps[6:8]
        RED, BC = ps[7], ps[7]
        QB = (ps[4], ps[5], ps[6], ps[0])
        slot_squares = (acc[:, :], rb[:, :], diag[:, :, :].rearrange("p a b -> p (a b)"), ea[:, 3])

        consts_in = sem("consts_in")
        x_in, wqk_in, wv_in, wi_in, wh_in = (sem(n) for n in ("x_in", "wqk_in", "wv_in", "wi_in", "wh_in"))
        ones_set = sem("ones_set")
        vec = sem("vec_step")
        pool_pow = sem("pool_pow")
        ln_stats = sem("ln_stats")
        x_normed = sem("x_normed")
        x_turned = sem("x_turned")
        slots_copied = sem("slots_copied")
        slots_high, slots_low = sem("slots_high"), sem("slots_low")
        wqk_mm, wqk_kept, wqk_sq = sem("wqk_mm"), sem("wqk_kept"), sem("wqk_sq")
        g_mm, g_kept = sem("g_mm"), sem("g_kept")
        gate_sq = sem("gate_sq")
        norm_sum = sem("norm_sum")
        norm_in = sem("norm_in")
        gate_sq_sum = sem("gate_sq_sum")
        scales_set = sem("scales_set")
        unit_high, unit_low = sem("unit_high"), sem("unit_low")
        unit_stored = [sem(f"unit_stored{i}") for i in range(WRING)]
        unit_in = [sem(f"unit_in{i}") for i in range(WRING)]
        unit_used = sem("unit_used")
        setup_done = sem("setup_done")
        ctx_in = [sem(f"ctx_in{i}") for i in range(RING)]
        row_sq, row_ms, row_r = sem("row_sq"), sem("row_ms"), sem("row_r")
        part_high, part_low = sem("part_high"), sem("part_low")
        turned, kept = sem("tile_turned"), sem("tile_kept")
        stored = [sem(f"tile_stored{i}") for i in range(RING)]
        pt_in = [sem(f"pt_in{i}") for i in range(RING)]
        slot_sq = sem("slot_sq")
        sum_mm = sem("sum_mm")
        sum_in = sem("sum_in")
        factor = sem("factor")
        diag_set = sem("diag_set")
        bc_mm = sem("bc_mm")
        bc_kept = sem("bc_kept")
        q_kept, q_high, q_low = sem("q_kept"), sem("q_high"), sem("q_low")
        scored, maxed, nmaxed, exped = sem("scored"), sem("maxed"), sem("nmaxed"), sem("exped")
        recip = sem("recip")
        attn_set, attn_high, attn_low = sem("attn_set"), sem("attn_high"), sem("attn_low")
        updated = sem("updated")
        acc_done = sem("acc_done")
        u_kept, u_high, u_low = sem("u_kept"), sem("u_high"), sem("u_low")
        tanh_r, tanh_z, tanh_n = sem("tanh_r"), sem("tanh_z"), sem("tanh_n")
        hid_set, n_in_set, h_new = sem("hid_set"), sem("n_in_set"), sem("h_new")
        gru_step = sem("gru_step")

        wqkv_in, x1_in, wout_in, w1_in, w2_in = (sem(n) for n in ("wqkv_in", "x1_in", "wout_in", "w1_in", "w2_in"))
        y_set, out_stored = sem("y_set"), sem("out_stored")
        back_turned, x1_set, xn_set, xn_turned, xnT_set = (sem(n) for n in ("back_turned", "x1_set", "xn_set", "xn_turned", "xnT_set"))
        qkv_mm, qkv_kept = sem("qkv_mm"), sem("qkv_kept")
        rope_sq, head_rms, qk_set = sem("rope_sq"), sem("head_rms"), sem("qk_set")
        qk_turned, qk_kept = sem("qk_turned"), sem("qk_kept")
        s_mm, s_max, s_exp, p_set, p_turned, p_kept, pv_mm, att_kept = (
            sem(n) for n in ("s_mm", "s_max", "s_exp", "p_set", "p_turned", "p_kept", "pv_mm", "att_kept"))
        o_mm = sem("o_mm")
        z_mm, z_tanh, l_sub, l_exp, w_set, w_turned, wT_kept = (
            sem(n) for n in ("z_mm", "z_tanh", "l_sub", "l_exp", "w_set", "w_turned", "wT_kept"))
        h_mm, h_act, wb_mm, hw_set, y_mm = (sem(n) for n in ("h_mm", "h_act", "wb_mm", "hw_set", "y_mm"))
        steps = [(hg, hh, i) for hg in range(HG) for hh in range(4) for i in range(TT)]
        NS = len(steps)
        LEAD = 3
        LEAD_T = 3
        LEAD_S = RING
        pick_set = sem("pick_set")
        winb_in = sem("winb_in")
        head_sum = sem("head_sum")
        mask_set, identb_set = sem("mask_set"), sem("identb_set")
        z_step, rope_step = sem("z_step"), sem("rope_step")
        junk = sb("junk", [P, D], F16)
        gb = sb("gb", [P, 3 * C])
        qk_rot = sem("qk_rot")

        def TPB(j):
            return j % 2

        def GB(a):
            return (ps[6], ps[4], ps[5], ps[7]) if a % 2 == 0 else ps[0:4]

        def keep_pT(act, n):
            w = (steps[n][2] + 1) * P
            act.wait_ge(p_turned, n + 1)
            if n >= 4:
                act.wait_ge(pv_mm, n - 3)
            act.activation(pT[:, n % 4].rearrange("p b k -> p (b k)")[:, 0:w], ps[4 + n % 2][:, 0:w], ACT.Copy)\
                .then_inc(p_kept, 1)

        block = stack.enter_context(nc.Block())

        def iterations(eng, body):
            body(0, True)
            with eng.Fori(1, ITERS) as it:
                body(it, False)

        def tiles(eng, body, first=0, last=NG):
            with eng.Fori(first, last) as g:
                for j in range(RING):
                    body(g, j)

        def ahead(g, j, k):
            return g + (j + k) // RING, (j + k) % RING

        def gate_unit(g, j):
            return w_units[:, bass.ds((g * GATE_LANES + j) * GU, GU)]

        def is_first(g):
            return isinstance(g, int) and g == 0

        @block.sync
        def _(sp):
            sp.dma_start(wq_s, wq.rearrange("(c p) e -> p c e", p=P)).then_inc(wqk_in, 16)
            sp.dma_start(wk_s, wk.rearrange("(c p) e -> p c e", p=P)).then_inc(wqk_in, 16)
            sp.dma_start(x_s, x[0].rearrange("(t p) d -> p t d", p=P)).then_inc(x_in, 16)
            sp.dma_start(sm[:, :], small).then_inc(consts_in, 16)
            sp.dma_start(hf[:, :], half).then_inc(consts_in, 16)
            sp.dma_start(winb, win_b).then_inc(winb_in, 16)
            sp.dma_start(pj[:, :], proj_t).then_inc(consts_in, 16)
            sp.dma_start(wv_s, wv.rearrange("(c p) e -> p c e", p=P)).then_inc(wv_in, 16)
            sp.dma_start(wiT, wi_t.rearrange("(c p) e -> p c e", p=P)).then_inc(wi_in, 16)
            for a in range(C):
                sp.dma_start(w_all[:, a, 0:3], wh_u[:, a]).then_inc(wh_in, 16)

            ctx_v = ctx[0].rearrange("(p t) d -> p (t d)", t=NT)

            def load_ctx(g, j):
                sp.dma_start(cx[:, j, :], ctx_v[:, bass.ds((g * RING + j) * D, D)]).then_inc(ctx_in[j], 16)

            for j in range(RING):
                load_ctx(0, j)
            for u in range(QK_UNITS):
                sp.wait_ge(unit_low, u + 1)
                sp.dma_start(wu_dram[u], wr[:, u].rearrange("p a c e -> p (a c e)")).then_inc(unit_stored[u], 16)

            def load_units(it, first, last):
                for u in range(first, last):
                    if is_first(it) and u < WRING:
                        sp.wait_ge(unit_stored[u], 16 if u < QK_UNITS else 16 * GATE_GROUPS)
                    else:
                        sp.wait_ge(unit_used, it * UNITS + (u - WRING + 1))
                    sp.dma_start(wr[:, u % WRING].rearrange("p a c e -> p (a c e)"), wu_dram[u])\
                        .then_inc(unit_in[u % WRING], 16)

            load_units(0, 0, QK_UNITS)

            def store_tile(g, j):
                sp.wait_ge(kept, g * RING + j + 1)
                sp.dma_start(pt_dram[bass.ds(g * RING + j, 1)].rearrange("a p n -> p (a n)"),
                             pt[:, j].rearrange("p a c e -> p (a c e)")).then_inc(stored[j], 16)

            def store_unit(g, j):
                sp.wait_ge(unit_low, g * GATE_LANES + (QK_UNITS + j + 1))
                sp.dma_start(wu_dram[bass.ds(g * GATE_LANES + (QK_UNITS + j), 1)].rearrange("a p n -> p (a n)"),
                             wr[:, QK_UNITS + j].rearrange("p a c e -> p (a c e)")).then_inc(unit_stored[QK_UNITS + j], 16)

            def store_and_load(g, j):
                sp.wait_ge(part_low, g * RING + j + 1)
                load_ctx(g + 1, j)
                store_tile(g, j)

            def store_all(g, j):
                store_and_load(g, j)
                if j < GATE_LANES:
                    store_unit(g - 1, j)

            for j in range(RING):
                store_and_load(0, j)
            tiles(sp, store_all, 1, GATE_GROUPS + 1)
            tiles(sp, store_and_load, GATE_GROUPS + 1, NG - 1)
            for j in range(RING):
                store_tile(NG - 1, j)
            for s in stored:
                sp.wait_ge(s, 16 * (NG))
            for u in range(QK_UNITS, WRING):
                sp.wait_ge(unit_stored[u], 16 * GATE_GROUPS)
            load_units(0, QK_UNITS, UNITS)

            def load_pt(it, g, j):
                sp.wait_ge(scored, it * NT + (g * RING + (j + 1 - RING)))
                sp.dma_start(pt[:, j].rearrange("p a c e -> p (a c e)"),
                             pt_dram[bass.ds(g * RING + j, 1)].rearrange("a p n -> p (a n)")).then_inc(pt_in[j], 16)

            with sp.Fori(1, ITERS) as it:
                load_units(it, 0, QK_UNITS)
                tiles(sp, lambda g, j: load_pt(it, g, j))
                load_units(it, QK_UNITS, UNITS)
            for i in range(TT):
                sp.wait_ge(y_set, i + 1)
                sp.dma_start(out[0, i * P:(i + 1) * P, :], x1[:, i]).then_inc(out_stored, 16)
            sp.wait_ge(out_stored, 16 * TT)


        @block.gpsimd
        def _(pool):
            pool.memset(ones[:, :], 1.0).then_inc(ones_set, 1)
            pool.memset(st[:, 0:1], -0.5).then_inc(ones_set, 1)
            pool.memset(st[:, 1:2], EPS / S_X ** 2).then_inc(ones_set, 1)
            pool.memset(st[:, 2:3], EPS).then_inc(ones_set, 1)
            pool.wait_ge(ones_set, 4)

            def power(src, dst, n, done):
                pool.tensor_tensor(dst, src, st[:, 0:1].to_broadcast([P, n]), ALU.pow).then_inc(done, 1)

            pool.wait_ge(ln_stats, 1)
            power(st[:, 8:12], st[:, 12:16], 4, pool_pow)
            pool.wait_ge(norm_in, 1)
            power(st[:, 16:17], st[:, 18:19], 1, pool_pow)
            pool.wait_ge(norm_in, 2)
            power(st[:, 17:18], st[:, 19:20], 1, pool_pow)

            def iteration(it, first):
                if first:
                    pool.wait_ge(slots_copied, C)
                    pool.wait_ge(wqk_sq, 1)
                else:
                    pool.wait_ge(h_new, C * it)
                pool.tensor_tensor(slot_squares[C - 1], h32[:, C - 1], h32[:, C - 1], ALU.mult).then_inc(slot_sq, 1)
                pool.wait_ge(sum_in, it + 1)
                power(st[:, 32:36], st[:, 36:40], 4, factor)
                pool.memset(acc[:, :], 0.0).then_inc(acc_done, 1)

                def row_scale(g, j):
                    pool.wait_ge(row_sq, g * RING + j + 1)
                    pool.tensor_tensor(st[:, 44 + j:45 + j], st[:, 40 + j:41 + j], st[:, 1:2], ALU.add).then_inc(row_ms, 1)
                    pool.wait_ge(row_ms, g * RING + j + 1)
                    power(st[:, 44 + j:45 + j], st[:, 48 + j:49 + j], 1, row_r)

                def add(g, j):
                    T = it * NT + g * RING + j
                    pool.wait_ge(attn_set, T + 1)
                    pool.wait_ge(acc_done, T + it + 2)
                    pool.tensor_tensor(acc[:, :], acc[:, :], ea[:, 2 + j % 2], ALU.add).then_inc(acc_done, 1)

                def with_scale(g, j):
                    row_scale(*ahead(g, j, LEAD_S))
                    add(g, j)

                if first:
                    for j in range(LEAD_S):
                        row_scale(0, j)
                    tiles(pool, with_scale, 0, NG - 1)
                    for j in range(RING):
                        add(NG - 1, j)
                else:
                    tiles(pool, add)

            pool.sem_inc(acc_done, 1)
            pool.memset(maskb, 0.0).then_inc(mask_set, 1)
            pool.wait_ge(mask_set, 1)
            pool.affine_select(out=maskb, in_=maskb, compare_op=ALU.is_ge, fill=-1e30, base=0,
                               pattern=[[-1, P]], channel_multiplier=1).then_inc(mask_set, 1)
            iterations(pool, iteration)
            pool.wait_ge(updated, ITERS * NT)
            pool.dma_start(x1, x[0].rearrange("(t p) d -> p t d", p=P)).then_inc(x1_in, 16)
            for c in range(C):
                pool.wait_ge(unit_used, (ITERS - 1) * UNITS + QK_UNITS + 4 * c + 2)
                pool.dma_start(wqkv_s[:, c], wqkv_t[c * P:(c + 1) * P, :]).then_inc(wqkv_in, 16)
            pool.wait_ge(unit_used, ITERS * UNITS - 6)
            pool.dma_start(wout_s, wout_t.rearrange("(c p) e -> p c e", p=P)).then_inc(wout_in, 16)
            pool.wait_ge(unit_used, ITERS * UNITS - 3)
            pool.dma_start(w1_s, w1_t.rearrange("(c p) e -> p c e", p=P)).then_inc(w1_in, 16)
            pool.dma_start(w2_s, w2.rearrange("(q p) e -> p q e", p=P)).then_inc(w2_in, 16)
            for n in range(2):
                pool.wait_ge(ln_stats, 2 + n)
                power(st[:, 8:12], st[:, 12:16], 4, pool_pow)
        @block.scalar
        def _(act):
            def split_high(dst, src, scale, done):
                act.activation(dst, src, ACT.Copy, scale=scale).then_inc(done, 1)

            act.wait_ge(consts_in, 48)
            act.wait_ge(wqk_kept, C)
            act.activation(ea[:, :, :], wqk, ACT.Square, accum_out=st[:, 20:21]).then_inc(wqk_sq, 1)
            for c in range(C):
                act.wait_ge(x_turned, c + 1)
                act.activation(h32[:, c], ps[c][:, :], ACT.Copy).then_inc(slots_copied, 1)
                act.wait_ge(slots_copied, c + 1)
                split_high(hs[:, 0, c], h32[:, c], S_X, slots_high)
            for n in range(3 * C):
                c, gt = n // 3, n % 3
                act.wait_ge(g_mm, n + 1)
                act.activation(w_all[:, :, G_PLACE[gt], c, :], ps[4 + n % 4][:, :].rearrange("p (a e) -> p a e", a=C),
                               ACT.Copy, scale=sm[:, WIN + c:WIN + c + 1]).then_inc(g_kept, 1)
                act.wait_ge(g_kept, n + 1)
                if n == 0:
                    act.wait_ge(wqk_sq, 1)
                act.wait_ge(gate_sq, n + min(C, max(0, n - 3)))
                act.activation(ea[:, 0].rearrange("p (a e) -> p a e", a=C), w_all[:, :, G_PLACE[gt], c, :], ACT.Square,
                               accum_out=st[:, 56 + n:57 + n]).then_inc(gate_sq, 1)
                if 3 <= n < 3 + C:
                    a = n - 3
                    act.wait_ge(wh_in, 16 * C)
                    act.wait_ge(gate_sq, n + 1 + a)
                    act.activation(ea[:, 0:3].rearrange("p a k -> p (a k)"),
                                   w_all[:, a, 0:3].rearrange("p g c e -> p (g c e)"), ACT.Square,
                                   accum_out=st[:, 68 + a:69 + a]).then_inc(gate_sq, 1)
                if n == 5:
                    act.wait_ge(scales_set, 1)
                    for u in range(QK_UNITS):
                        split_high(wr[:, u, 0], wqk[:, :, u * P:(u + 1) * P], st[:, 24:25], unit_high)
            def gate_high(g, j):
                if is_first(g):
                    act.wait_ge(scales_set, 2)
                else:
                    act.wait_ge(unit_stored[QK_UNITS + j], 16 * g)
                act.activation(wr[:, QK_UNITS + j, 0].rearrange("p c e -> p (c e)"), gate_unit(g, j), ACT.Copy,
                               scale=st[:, 26:27]).then_inc(unit_high, 1)

            def square_slots(c):
                act.activation(slot_squares[c], h32[:, c], ACT.Square).then_inc(slot_sq, 1)

            def iteration(it, first):
                if first:
                    for c in range(C):
                        act.wait_ge(slots_copied, c + 1)
                        if c < C - 1:
                            square_slots(c)
                for f in range(C):
                    act.wait_ge(q_kept, C * it + f + 1)
                    split_high(qu[:, 0, f], ea[:, f], 1.0, q_high)

                def square(g, j):
                    act.wait_ge(ctx_in[j], 16 * g + 16)
                    act.activation(junk[:, :], cx[:, j, :], ACT.Square, scale=D ** -0.5 / S_X, accum_out=st[:, 40 + j:41 + j]).then_inc(row_sq, 1)

                def keep(g, j):
                    act.wait_ge(turned, g * RING + j + 1)
                    if not is_first(g):
                        act.wait_ge(stored[j], 16 * g)
                    act.activation(pt[:, j].rearrange("p a c e -> p (a c e)"), TP[j % 2][:, :].bitcast(F16), ACT.Copy)\
                        .then_inc(kept, 1)

                def soft(g, j):
                    act.wait_ge(nmaxed, it * NT + g * RING + j + 1)
                    act.activation(ea[:, j % 2], SC[j % 2][:, :], ACT.Exp, bias=st[:, 80 + j % 2:81 + j % 2],
                                   scale=st[:, 25:26], accum_out=st[:, 84 + j % 2:85 + j % 2]).then_inc(exped, 1)

                def high(g, j):
                    act.wait_ge(attn_set, it * NT + g * RING + j + 1)
                    act.activation(ah[:, j % 2, 0], ea[:, 2 + j % 2], ACT.Copy).then_inc(attn_high, 1)

                def plain(g, j):
                    soft(g, j)
                    high(g, j)

                def full(g, j):
                    soft(g, j)
                    square(*ahead(g, j, LEAD_S))
                    high(g, j)
                    keep(*ahead(g, j, 2))

                if first:
                    for j in range(LEAD_S):
                        if j:
                            act.wait_ge(row_sq, j)
                        square(0, j)
                    keep(0, 0)
                    keep(0, 1)
                    def with_gates(g, j):
                        full(g, j)
                        if j < GATE_LANES:
                            gate_high(g, j)

                    for j in range(RING):
                        with_gates(0, j)
                    tiles(act, with_gates, 1, GATE_GROUPS)
                    tiles(act, full, GATE_GROUPS, NG - 1)
                    for j in range(RING):
                        soft(NG - 1, j)
                        high(NG - 1, j)
                        if j + 2 < RING:
                            keep(NG - 1, j + 2)
                else:
                    tiles(act, plain)
                for c in range(C):
                    act.wait_ge(u_kept, C * it + c + 1)
                    split_high(qu[:, 0, c], ea[:, c], 1.0, u_high)
                def high_slots(c):
                    split_high(hs[:, 0, c], h32[:, c], S_X, slots_high)

                for a in range(C):
                    n = C * it + a
                    unit = it * UNITS + QK_UNITS + 6 * a
                    act.wait_ge(unit_used, unit + 4)
                    if a == 0:
                        act.wait_ge(u_low, C * (it + 1))
                    else:
                        act.wait_ge(h_new, n)
                    A = GB(a)
                    act.activation(ea[:, 0], A[0][:, :], ACT.Tanh, bias=gb[:, a:a + 1],
                                   scale=st[:, 27:28]).then_inc(tanh_r, 1)
                    if a == C - 1:
                        high_slots(0)
                        high_slots(1)
                    act.wait_ge(n_in_set, n + 1)
                    act.activation(ea[:, 3], ea[:, 2], ACT.Tanh, bias=sm[:, BI + 8 + a:BI + 9 + a]).then_inc(tanh_n, 1)
                    if a == C - 1:
                        high_slots(2)
                    act.wait_ge(unit_used, unit + 6)
                    act.activation(ea[:, 1], A[1][:, :], ACT.Tanh, bias=gb[:, C + a:C + a + 1],
                                   scale=st[:, 27:28]).then_inc(tanh_z, 1)
                    if a >= 1:
                        square_slots(a - 1)
                act.wait_ge(h_new, C * it + C)
                high_slots(C - 1)

            iterations(act, iteration)

            act.wait_ge(ones_set, 4)
            for i in range(2 * TT):
                act.wait_ge(qk_rot, i + 1)
                act.activation(rope_t[:, 3 + i % 2], rope_t[:, i % 2], ACT.Square).then_inc(rope_sq, 1)
                act.wait_ge(head_sum, i + 1)
                o = (i % 2) * 64
                act.activation(rope_t[:, 5, o + 16:o + 16 + H], rope_t[:, 5, o:o + H], ACT.Sqrt, scale=1 / HD,
                               bias=st[:, 2:3]).then_inc(head_rms, 1)
            for i in range(TT):
                act.wait_ge(qkv_mm, 2 * TT + i + 1)
                act.activation(v_n[:, i], ps[i][:, :], ACT.Copy).then_inc(qkv_kept, 1)
            for n in range(NS):
                _, _, i = steps[n]
                w = (i + 1) * P
                act.wait_ge(s_max, n + 1)
                act.activation(ea[:, n % 4, 0:w], ps[n % 4][:, 0:w], ACT.Exp, bias=st[:, 56 + n % 4:57 + n % 4],
                               accum_out=st[:, 60 + n % 4:61 + n % 4]).then_inc(s_exp, 1)
                if n >= 2:
                    keep_pT(act, n - 2)
            for n in range(NS - 2, NS):
                keep_pT(act, n)
            act.wait_ge(z_mm, 1)
            act.activation(rope_t[:, 0, 0:TT * NE], ps[0][:, 0:TT * NE], ACT.Tanh, scale=1 / QUANT_TEMP).then_inc(z_tanh, 1)
            act.wait_ge(l_sub, 1)
            act.activation(rope_t[:, 2, 128:128 + TT * NE], rope_t[:, 2, 64:64 + TT * NE], ACT.Exp).then_inc(l_exp, 1)
            for q in range(12):
                act.wait_ge(h_mm, q + 1)
                if q >= 2:
                    act.wait_ge(hw_set, q - 1)
                act.activation(ea[:, q % 2], ps[4 + q % 2][:, :], ACT.Gelu_apprx_tanh).then_inc(h_act, 1)

        @block.vector
        def _(dve):
            count = [0]

            def step(ins):
                count[0] += 1
                ins.then_inc(vec, 1)
                dve.wait_ge(vec, count[0])

            def split_low(dst, src, scale, high, done):
                dve.scalar_tensor_tensor(dst, src, scale, high, ALU.mult, ALU.subtract).then_inc(done, 1)

            def post(ins):
                count[0] += 1
                ins.then_inc(vec, 1)

            def layer_norm(src, dst, n, done, make=None):
                for i in range(TT):
                    if make is not None:
                        make(i)
                    post(dve.bn_stats(st[:, 96 + 6 * i:102 + 6 * i], src[:, i]))
                dve.wait_ge(vec, count[0])
                for i in range(TT):
                    post(dve.bn_aggr(st[:, 120 + 2 * i:122 + 2 * i], st[:, 96 + 6 * i:102 + 6 * i]))
                dve.wait_ge(vec, count[0])
                dve.tensor_scalar(st[:, 8:12], st[:, 121:128:2], LN_EPS, None, ALU.add).then_inc(ln_stats, 1)
                dve.wait_ge(pool_pow, n)
                for i in range(TT):
                    dve.tensor_scalar(dst[:, i], src[:, i], st[:, 120 + 2 * i:121 + 2 * i], st[:, 12 + i:13 + i],
                                      ALU.subtract, ALU.mult).then_inc(done, 1)

            dve.wait_ge(x_in, 16)
            layer_norm(x_s, x_s, 1, x_normed)
            dve.wait_ge(consts_in, 48)
            dve.tensor_copy(identb, ident).then_inc(identb_set, 1)
            for c in range(C):
                dve.wait_ge(wqk_mm, c + 1)
                dve.wait_ge(winb_in, 16)
                dve.scalar_tensor_tensor(wqk[:, c], ps[c][:, :], sm[:, WSLOT + c:WSLOT + c + 1], winb,
                                         ALU.mult, ALU.mult).then_inc(wqk_kept, 1)
            step(dve.tensor_tensor(gb[:, 0:8], sm[:, BI:BI + 8], sm[:, BH:BH + 8], ALU.add))
            step(dve.tensor_scalar(gb[:, 0:8], gb[:, 0:8], 0.5, None, ALU.mult))
            step(dve.tensor_scalar(gb[:, 8:12], sm[:, BH + 8:BH + 12], 0.5, None, ALU.mult))
            for c in range(C):
                dve.wait_ge(slots_high, c + 1)
                split_low(hs[:, 1, c], h32[:, c], S_X, hs[:, 0, c], slots_low)
            dve.wait_ge(norm_sum, 1)
            dve.tensor_scalar(st[:, 16:17], ps[0][:, 0:1], S_W ** -2, TINY, ALU.mult, ALU.add).then_inc(norm_in, 1)
            dve.wait_ge(pool_pow, 2)
            step(dve.reciprocal(st[:, 22:23], st[:, 18:19]))
            step(dve.tensor_scalar(st[:, 25:26], st[:, 22:23], SCALE * S_W / S_X ** 2, None, ALU.mult))
            step(dve.tensor_scalar(st[:, 28:29], st[:, 25:26], -1.0, None, ALU.mult))
            dve.tensor_copy(st[:, 24:25], st[:, 18:19]).then_inc(scales_set, 1)
            for u in range(QK_UNITS):
                dve.wait_ge(unit_high, u + 1)
                split_low(wr[:, u, 1], wqk[:, :, u * P:(u + 1) * P], st[:, 24:25], wr[:, u, 0], unit_low)
            dve.wait_ge(gate_sq, 4 * C)
            dve.reduce_sum(st[:, 21:22], st[:, 56:56 + 4 * C], AX.X).then_inc(gate_sq_sum, 1)
            dve.wait_ge(norm_sum, 2)
            dve.tensor_scalar(st[:, 17:18], ps[0][:, 8:9], S_W ** -2, TINY, ALU.mult, ALU.add).then_inc(norm_in, 1)
            dve.wait_ge(pool_pow, 3)
            step(dve.reciprocal(st[:, 23:24], st[:, 19:20]))
            step(dve.tensor_scalar(st[:, 29:30], st[:, 23:24], 1 / S_X, None, ALU.mult))
            step(dve.tensor_scalar(st[:, 27:28], st[:, 23:24], 0.5 / S_X, None, ALU.mult))
            dve.tensor_copy(st[:, 26:27], st[:, 19:20]).then_inc(scales_set, 1)

            def gate_low(g, j):
                dve.wait_ge(unit_high, g * GATE_LANES + (QK_UNITS + j + 1))
                split_low(wr[:, QK_UNITS + j, 1].rearrange("p c e -> p (c e)"), gate_unit(g, j), st[:, 26:27],
                          wr[:, QK_UNITS + j, 0].rearrange("p c e -> p (c e)"), unit_low)

            def iteration(it, first):
                def spread(n):
                    for i in range(TT):
                        dve.tensor_scalar(diag[:, i], ident, st[:, 36 + i:37 + i], None, ALU.mult).then_inc(diag_set, 1)
                    dve.wait_ge(bc_mm, 2 * it + n + 1)
                    dve.tensor_copy(rb[:, :], BC[:, :]).then_inc(bc_kept, 1)
                    dve.wait_ge(bc_kept, 2 * it + n + 1)

                dve.wait_ge(sum_mm, 2 * it + 1)
                dve.tensor_scalar(st[:, 32:36], RED[:, 0:TT], 1 / D, EPS, ALU.mult, ALU.add).then_inc(sum_in, 1)
                dve.wait_ge(factor, it + 1)
                spread(0)
                def query_low(f):
                    dve.wait_ge(q_high, C * it + f + 1)
                    dve.tensor_tensor(qu[:, 1, f], ea[:, f], qu[:, 0, f], ALU.subtract).then_inc(q_low, 1)

                for f in range(C):
                    dve.wait_ge(unit_used, it * UNITS + f + 1)
                    dve.scalar_tensor_tensor(ea[:, f], QB[f][:, :], 1 / S_W, rb[:, :], ALU.mult, ALU.mult).then_inc(q_kept, 1)
                    if f >= 1:
                        query_low(f - 1)
                query_low(C - 1)

                def prepare(g, j):
                    t = g * RING + j
                    dve.wait_ge(row_r, t + 1)
                    dve.tensor_scalar(pn_tile(t, 0), cx[:, j], st[:, 48 + j:49 + j], None, ALU.mult).then_inc(part_high, 1)
                    dve.wait_ge(part_high, t + 1)
                    split_low(pn_tile(t, 1), cx[:, j], st[:, 48 + j:49 + j], pn_tile(t, 0), part_low)

                def maximum(g, j):
                    T, b = it * NT + g * RING + j, j % 2
                    dve.wait_ge(scored, T + 1)
                    dve.reduce_max(st[:, 88 + b:89 + b], SC[b][:, :], AX.X).then_inc(maxed, 1)
                    dve.wait_ge(maxed, T + 1)
                    dve.tensor_scalar(st[:, 80 + b:81 + b], st[:, 88 + b:89 + b], st[:, 28:29], None, ALU.mult)\
                        .then_inc(nmaxed, 1)

                def weights(g, j):
                    T, b = it * NT + g * RING + j, j % 2
                    dve.wait_ge(exped, T + 1)
                    dve.reciprocal(st[:, 90 + b:91 + b], st[:, 84 + b:85 + b]).then_inc(recip, 1)
                    dve.wait_ge(recip, T + 1)
                    dve.wait_ge(acc_done, T + it + 1)
                    dve.tensor_scalar(ea[:, 2 + b], ea[:, b], st[:, 90 + b:91 + b], S_A, ALU.mult, ALU.mult)\
                        .then_inc(attn_set, 1)
                    dve.wait_ge(attn_high, T + 1)
                    dve.tensor_tensor(ah[:, b, 1], ea[:, 2 + b], ah[:, b, 0], ALU.subtract).then_inc(attn_low, 1)

                def plain(g, j):
                    maximum(g, j)
                    weights(g, j)

                def full(g, j):
                    maximum(g, j)
                    prepare(*ahead(g, j, LEAD_T))
                    weights(g, j)

                if first:
                    for j in range(LEAD_T):
                        prepare(0, j)

                    def with_gates(g, j):
                        maximum(g, j)
                        prepare(*ahead(g, j, LEAD_T))
                        if 0 < j <= GATE_LANES:
                            gate_low(g, j - 1)
                        weights(g, j)

                    tiles(dve, with_gates, 0, GATE_GROUPS)
                    tiles(dve, full, GATE_GROUPS, NG - 1)
                    for j in range(RING):
                        maximum(NG - 1, j)
                        if j + LEAD_T < RING:
                            prepare(NG - 1, j + LEAD_T)
                        weights(NG - 1, j)
                else:
                    tiles(dve, plain)
                dve.wait_ge(sum_mm, 2 * it + 2)
                dve.tensor_scalar(st[:, 32:36], RED[:, 0:TT], EPS * S_A, None, ALU.add).then_inc(gru_step, 1)
                dve.wait_ge(gru_step, 2 * it + 1)
                dve.reciprocal(st[:, 36:40], st[:, 32:36]).then_inc(gru_step, 1)
                dve.wait_ge(gru_step, 2 * it + 2)
                spread(1)
                def update_low(c):
                    dve.wait_ge(u_high, C * it + c + 1)
                    dve.tensor_tensor(qu[:, 1, c], ea[:, c], qu[:, 0, c], ALU.subtract).then_inc(u_low, 1)

                for c in range(C):
                    dve.tensor_tensor(ea[:, c], U[c][:, :], rb[:, :], ALU.mult).then_inc(u_kept, 1)
                    if c >= 1:
                        update_low(c - 1)
                update_low(C - 1)
                def low_slots(c):
                    dve.wait_ge(slots_high, C * (it + 1) + c + 1)
                    split_low(hs[:, 1, c], h32[:, c], S_X, hs[:, 0, c], slots_low)

                for a in range(C):
                    n = C * it + a
                    A = GB(a)
                    unit = it * UNITS + QK_UNITS + 6 * a
                    dve.wait_ge(unit_used, unit + 3)
                    dve.wait_ge(tanh_r, n + 1)
                    dve.tensor_scalar(ea[:, 2], A[2][:, :], st[:, 27:28], gb[:, 8 + a:9 + a], ALU.mult, ALU.add).then_inc(hid_set, 1)
                    dve.wait_ge(hid_set, 2 * n + 1)
                    dve.scalar_tensor_tensor(ea[:, 2], ea[:, 0], 1.0, ea[:, 2], ALU.add, ALU.mult).then_inc(hid_set, 1)
                    dve.wait_ge(hid_set, 2 * n + 2)
                    if a == C - 1:
                        low_slots(0)
                        low_slots(1)
                    dve.wait_ge(unit_used, unit + 5)
                    dve.scalar_tensor_tensor(ea[:, 2], A[3][:, :], st[:, 29:30], ea[:, 2], ALU.mult, ALU.add).then_inc(n_in_set, 1)
                    if a == C - 1:
                        low_slots(2)
                    dve.wait_ge(tanh_n, n + 1)
                    dve.tensor_tensor(ea[:, 2], h32[:, a], ea[:, 3], ALU.subtract).then_inc(z_step, 1)
                    dve.wait_ge(z_step, 2 * n + 1)
                    dve.wait_ge(tanh_z, n + 1)
                    dve.scalar_tensor_tensor(ea[:, 2], ea[:, 1], 1.0, ea[:, 2], ALU.add, ALU.mult).then_inc(z_step, 1)
                    dve.wait_ge(z_step, 2 * n + 2)
                    dve.scalar_tensor_tensor(h32[:, a], ea[:, 2], 0.5, ea[:, 3], ALU.mult, ALU.add).then_inc(h_new, 1)
                low_slots(C - 1)

            iterations(dve, iteration)

            dve.wait_ge(x1_in, 16)
            def add_slots(i):
                dve.wait_ge(back_turned, i + 1)
                dve.tensor_tensor(x1[:, i], x1[:, i], ps[4 + i][:, :], ALU.add).then_inc(x1_set, 1)
                dve.wait_ge(x1_set, i + 1)

            layer_norm(x1, xn, 4, xn_set, add_slots)
            for c in range(C):
                dve.wait_ge(xn_turned, c + 1)
                dve.tensor_copy(xnT[:, c], ps[c][:, :]).then_inc(xnT_set, 1)
            def rotate(n):
                i, w = n // 2, n % 2
                src = ps[n][:, :]
                cos = sm[:, COS + i * HD:COS + (i + 1) * HD].unsqueeze(1).to_broadcast([P, H, HD])
                sn = sm[:, SIN + i * HD:SIN + (i + 1) * HD].rearrange("p (s d) -> p s d", s=2)
                sh = src.rearrange("p (h s d) -> p h s d", h=H, s=2)
                sw = rope_t[:, 2].rearrange("p (h s d) -> p h s d", h=H, s=2)
                rot = rope_t[:, n % 2]
                dve.wait_ge(qkv_mm, n + 1)
                if n >= 2:
                    dve.wait_ge(qk_set, n - 1)
                dve.tensor_tensor(rot.rearrange("p (h d) -> p h d", h=H), src.rearrange("p (h d) -> p h d", h=H),
                                  cos, ALU.mult).then_inc(rope_step, 1)
                if n >= 1:
                    dve.wait_ge(qk_rot, n)
                for s in range(2):
                    dve.tensor_tensor(sw[:, :, s], sh[:, :, 1 - s], sn[:, s].unsqueeze(1).to_broadcast([P, H, HD // 2]),
                                      ALU.mult).then_inc(rope_step, 1)
                dve.wait_ge(rope_step, 3 * n + 3)
                dve.tensor_tensor(rot, rot, rope_t[:, 2], ALU.add).then_inc(qk_rot, 1)

            def head_norm(n):
                dve.wait_ge(rope_sq, n + 1)
                dve.reduce_sum(rope_t[:, 5, (n % 2) * 64:(n % 2) * 64 + H],
                               rope_t[:, 3 + n % 2].rearrange("p (h d) -> p h d", h=H), AX.X).then_inc(head_sum, 1)

            def head_scale(n):
                dst, o = (q_n, k_n)[n % 2][:, n // 2], (n % 2) * 64
                rms, r = rope_t[:, 5, o + 16:o + 16 + H], rope_t[:, 5, o + 32:o + 32 + H]
                dve.wait_ge(head_rms, n + 1)
                step(dve.reciprocal(r, rms))
                dve.tensor_tensor(dst.rearrange("p (h d) -> p h d", h=H), rope_t[:, n % 2].rearrange("p (h d) -> p h d", h=H),
                                  r.unsqueeze(2).to_broadcast([P, H, HD]), ALU.mult).then_inc(qk_set, 1)

            for n in range(2 * TT + 1):
                if n < 2 * TT:
                    if n >= 2:
                        head_scale(n - 2)
                    rotate(n)
                if n >= 1:
                    head_norm(n - 1)
            head_scale(2 * TT - 2)
            head_scale(2 * TT - 1)
            step(dve.tensor_scalar(st[:, 52:53], sm[:, QW:QW + 1], sm[:, KW:KW + 1], ATT_SCALE, ALU.mult, ALU.mult))
            for n in range(2 * HG):
                dve.wait_ge(qk_turned, n + 1)
                if n < HG:
                    dve.tensor_scalar(qT[:, n], ps[n][:, :], st[:, 52:53], None, ALU.mult).then_inc(qk_kept, 1)
                else:
                    dve.tensor_copy(kT[:, n - HG], ps[n][:, :]).then_inc(qk_kept, 1)

            def s_maximum(n):
                w = (steps[n][2] + 1) * P
                dve.wait_ge(s_mm, n + 1)
                dve.tensor_reduce(st[:, 56 + n % 4:57 + n % 4], ps[n % 4][:, 0:w], AX.X, ALU.max, negate=True).then_inc(s_max, 1)

            def s_normal(n):
                w = (steps[n][2] + 1) * P
                dve.wait_ge(s_exp, n + 1)
                step(dve.reciprocal(st[:, 72 + n % 2:73 + n % 2], st[:, 60 + n % 4:61 + n % 4]))
                dve.tensor_scalar(ea[:, n % 4, 0:w], ea[:, n % 4, 0:w], st[:, 72 + n % 2:73 + n % 2], None, ALU.mult)\
                    .then_inc(p_set, 1)

            def keep_att(hg):
                dve.wait_ge(pv_mm, 16 * hg + 16)
                dve.tensor_copy(attT[:, hg], ps[6 + hg % 2][:, :]).then_inc(att_kept, 1)

            for n in range(NS + 1):
                if n < NS:
                    s_maximum(n)
                if n >= 1:
                    s_normal(n - 1)
                if n >= 24 and (n - 24) % 16 == 0:
                    keep_att((n - 24) // 16)
            keep_att(HG - 1)
            def add_attention(i):
                dve.wait_ge(o_mm, i + 1)
                dve.tensor_tensor(x1[:, i], x1[:, i], ps[4 + i][:, :], ALU.add).then_inc(x1_set, 1)
                dve.wait_ge(x1_set, TT + i + 1)

            layer_norm(x1, xn, 5, xn_set, add_attention)
            for c in range(C):
                dve.wait_ge(xn_turned, C + c + 1)
                dve.tensor_copy(xnT[:, c], ps[c][:, :]).then_inc(xnT_set, 1)
            dve.tensor_copy(pick, ident[0:NE, 0:NE].unsqueeze(2).to_broadcast([NE, NE, P])).then_inc(pick_set, 1)
            q_r = rope_t[:, 0, 0:TT * NE].rearrange("p (t d) -> p t d", t=TT)
            prod = rope_t[:, 1, 0:TT * NE * NE].rearrange("p (t e d) -> p t e d", t=TT, e=NE)
            logit = rope_t[:, 2, 0:TT * NE]
            lg = logit.rearrange("p (t e) -> p t e", t=TT)
            top = rope_t[:, 2, 192:192 + TT]
            gt_, eq_ = (rope_t[:, 3, o:o + TT * NE * NE].rearrange("p (t e d) -> p t e d", t=TT, e=NE) for o in (0, 160))
            rank = rope_t[:, 3, 320:320 + TT * NE]
            shifted = rope_t[:, 2, 64:64 + TT * NE]
            ex = rope_t[:, 2, 128:128 + TT * NE]
            step(dve.tensor_scalar(st[:, 53:54], sm[:, TEMP:TEMP + 1], 0.1, None, ALU.max))
            step(dve.reciprocal(st[:, 54:55], st[:, 53:54]))
            step(dve.tensor_scalar(st[:, 54:55], st[:, 54:55], 0.5, None, ALU.mult))
            anch = sm[:, ANCH:ANCH + NE * NE].rearrange("p (e d) -> p e d", e=NE)
            lower = sm[:, LOWER:LOWER + NE * NE].rearrange("p (e d) -> p e d", e=NE)
            full4 = [P, TT, NE, NE]
            dve.wait_ge(z_tanh, 1)
            step(dve.tensor_tensor(prod, q_r.unsqueeze(2).to_broadcast(full4), anch.unsqueeze(1).to_broadcast(full4), ALU.mult))
            step(dve.reduce_sum(logit, prod.rearrange("p t e d -> p (t e) d"), AX.X))
            step(dve.tensor_scalar(logit, logit, -6.0, st[:, 54:55], ALU.add, ALU.mult))
            l_e, l_j = lg.unsqueeze(3).to_broadcast(full4), lg.unsqueeze(2).to_broadcast(full4)
            step(dve.tensor_tensor(gt_, l_j, l_e, ALU.is_gt))
            step(dve.tensor_tensor(eq_, l_j, l_e, ALU.is_equal))
            step(dve.tensor_tensor(eq_, eq_, lower.unsqueeze(1).to_broadcast(full4), ALU.mult))
            step(dve.tensor_tensor(gt_, gt_, eq_, ALU.add))
            step(dve.reduce_sum(rank, gt_.rearrange("p t e d -> p (t e) d"), AX.X))
            step(dve.tensor_scalar(rank, rank, float(TOPK), None, ALU.is_lt))
            step(dve.reduce_max(top, lg, AX.X))
            dve.tensor_tensor(shifted.rearrange("p (t e) -> p t e", t=TT), lg, top.unsqueeze(2).to_broadcast([P, TT, NE]),
                              ALU.subtract).then_inc(l_sub, 1)
            dve.wait_ge(l_exp, 1)
            step(dve.tensor_tensor(ex, ex, rank, ALU.mult))
            step(dve.reduce_sum(top, ex.rearrange("p (t e) -> p t e", t=TT), AX.X))
            step(dve.reciprocal(top, top))
            dve.tensor_tensor(shifted.rearrange("p (t e) -> p t e", t=TT), ex.rearrange("p (t e) -> p t e", t=TT),
                              top.unsqueeze(2).to_broadcast([P, TT, NE]), ALU.mult).then_inc(w_set, 1)
            dve.wait_ge(w_turned, 1)
            dve.tensor_copy(rb[0:NE, :], ps[6][0:NE, :]).then_inc(wT_kept, 1)
            for q in range(12):
                dve.wait_ge(h_act, q + 1)
                dve.wait_ge(wb_mm, q // 2 + 1)
                dve.tensor_tensor(hw_s[:, q], ea[:, q % 2], ps[6 + (q // 2) % 2][:, :], ALU.mult).then_inc(hw_set, 1)
            for i in range(TT):
                dve.wait_ge(y_mm, i + 1)
                dve.tensor_tensor(x1[:, i], x1[:, i], ps[i][:, :], ALU.add).then_inc(y_set, 1)

        @block.tensor
        def _(pe):
            def mm(o, w, r, start=True, stop=True, **kw):
                return pe.matmul(o, w, r, start=start, stop=stop, **kw)

            def turn(o, i):
                return pe.transpose(o, i, ident)

            pe.wait_ge(wqk_in, 32)
            for c in range(C):
                for k in range(C):
                    ins = mm(ps[c][:, :], wq_s[:, k, c * P:(c + 1) * P], wk_s[:, k, :], k == 0, k == C - 1)
                ins.then_inc(wqk_mm, 1)

            def gate_product(n):
                c, gt = n // 3, n % 3
                if n >= 4:
                    pe.wait_ge(g_kept, n - 3)
                for k in range(C):
                    ins = mm(ps[4 + n % 4][:, :], wv_s[:, k, c * P:(c + 1) * P], wiT[:, k, gt * D:(gt + 1) * D], k == 0, k == C - 1)
                ins.then_inc(g_mm, 1)

            pe.wait_ge(wv_in, 16)
            pe.wait_ge(wi_in, 16)
            for n in range(3):
                gate_product(n)
            pe.wait_ge(x_normed, TT)
            pe.wait_ge(consts_in, 48)
            for c in range(C):
                pe.wait_ge(wqk_kept, c + 1)
                for i in range(TT):
                    ins = turn(ps[c][:, i * P:(i + 1) * P], x_s[:, i, c * P:(c + 1) * P])
                ins.then_inc(x_turned, 1)
            for n in range(3, 6):
                gate_product(n)
            pe.wait_ge(ones_set, 1)
            pe.wait_ge(wqk_sq, 1)
            pe.wait_ge(slots_copied, 1)
            mm(ps[0][:, 0:1], ones[:, :], st[:, 20:21]).then_inc(norm_sum, 1)
            for n in range(6, 12):
                gate_product(n)
            pe.wait_ge(gate_sq_sum, 1)
            pe.wait_ge(norm_in, 1)
            mm(ps[0][:, 8:9], ones[:, :], st[:, 21:22]).then_inc(norm_sum, 1)

            def iteration(it, first):
                def unit_part(u, bank, move, starts, stops, chunks=range(C), ready=None):
                    if 0 in chunks:
                        pe.wait_ge(unit_in[u % WRING], it * (16 * (UNITS // WRING)) + 16 * (u // WRING + 1))
                    for c in chunks:
                        if ready is not None:
                            ready(c)
                        for pi, (a, b) in enumerate(PARTS3):
                            ins = mm(bank[:, :], wr[:, u % WRING, a, c, :], move[:, b, c, :],
                                     starts and c == 0 and pi == 0, stops and c == C - 1 and pi == 2)
                    if C - 1 in chunks:
                        ins.then_inc(unit_used, 1)

                def slot_sums(col):
                    for i in range(TT):
                        cs = col(i)
                        for m, src in enumerate(cs):
                            ins = mm(RED[:, i:i + 1], src, ones[:, 0:1], m == 0, m == len(cs) - 1)
                    ins.then_inc(sum_mm, 1)

                def broadcast(n):
                    pe.wait_ge(diag_set, TT * (2 * it + n + 1))
                    mm(BC[:, :], ones[:, :], diag[:, :, :].rearrange("p a b -> p (a b)")).then_inc(bc_mm, 1)

                def slots_ready(c):
                    pe.wait_ge(slots_high, C * it + c + 1)
                    pe.wait_ge(slots_low, C * it + c + 1)

                if first:
                    pe.wait_ge(norm_in, 2)
                else:
                    pe.wait_ge(h_new, C * it - 1)
                for f in range(C):
                    if f == C - 1 and not first:
                        pe.wait_ge(tanh_r, C * it)
                    unit_part(f, QB[f], hs, True, False, range(C - 1), slots_ready if f == 0 else None)
                pe.wait_ge(slot_sq, C * (it + 1))
                slot_sums(lambda i: [sq[:, i * P:(i + 1) * P] for sq in slot_squares])
                slots_ready(C - 1)
                for f in range(C):
                    unit_part(f, QB[f], hs, False, True, range(C - 1, C))
                broadcast(0)

                def queries_ready(c):
                    pe.wait_ge(q_high, C * it + c + 1)
                    pe.wait_ge(q_low, C * it + c + 1)

                def turn_tile(g, j):
                    t = g * RING + j
                    pe.wait_ge(part_low, t + 1)
                    for a in range(2):
                        for c in range(C):
                            ins = pe.transpose(TP[j % 2][:, :].bitcast(F16)[:, (a * C + c) * P:(a * C + c + 1) * P],
                                               pn_w(t, a, c), ident16)
                    ins.then_inc(turned, 1)

                def scores(g, j, ready=None):
                    if first:
                        pe.wait_ge(kept, g * RING + j + 1)
                    else:
                        pe.wait_ge(pt_in[j], (it - 1) * (16 * NG) + (16 * g + 16))
                    for c in range(C):
                        if ready is not None:
                            ready(c)
                        for pi, (a, b) in enumerate(PARTS3):
                            ins = mm(SC[j % 2][:, :], pt[:, j, a, c, :], qu[:, b, c, :], c == 0 and pi == 0, c == C - 1 and pi == 2)
                    ins.then_inc(scored, 1)

                def update(g, j, last=False):
                    t = g * RING + j
                    pe.wait_ge(attn_high, it * NT + t + 1)
                    pe.wait_ge(attn_low, it * NT + t + 1)
                    for c in range(C):
                        for pi, (a, b) in enumerate(PARTS3):
                            ins = mm(U[c][:, :], pn_w(t, a, c), ah[:, j % 2, b], False, last and pi == 2, skip_group_check=True)
                    ins.then_inc(updated, 1)

                if first:
                    pe.wait_ge(q_kept, C * (it + 1))
                    pe.wait_ge(bc_kept, 2 * it + 1)
                    turn_tile(0, 0)
                    turn_tile(0, 1)
                    pe.wait_ge(kept, 1)
                    turn_tile(0, 2)
                pe.wait_ge(q_kept, C * it + 2)
                scores(0, 0, queries_ready)
                scores(0, 1)
                for c in range(C):
                    mm(U[c][:, :], zeros16, qu[:, 0, 0, :], True, False, skip_group_check=True)

                def turn_ahead(g, j):
                    pe.wait_ge(kept, g * RING + j + LEAD_T - 1)
                    turn_tile(*ahead(g, j, LEAD_T))

                def scores_ahead(g, j):
                    pe.wait_ge(exped, it * NT + g * RING + j + 1)
                    scores(*ahead(g, j, 2))

                def full(g, j):
                    update(g, j)
                    if first:
                        turn_ahead(g, j)
                    scores_ahead(g, j)

                tiles(pe, full, 0, NG - 1)
                for j in range(RING):
                    if j == RING - 1:
                        unit_part(QK_UNITS, GB(0)[0], hs, True, False)
                    update(NG - 1, j, j == RING - 1)
                    if first and j + LEAD_T < RING:
                        turn_ahead(NG - 1, j)
                    if j + 2 < RING:
                        scores_ahead(NG - 1, j)

                pe.wait_ge(acc_done, it * NT + NT + it + 2)
                slot_sums(lambda i: [acc[:, i * P:(i + 1) * P]])

                def updates_ready(c):
                    pe.wait_ge(u_high, C * it + c + 1)
                    pe.wait_ge(u_low, C * it + c + 1)

                for a in range(C):
                    B = GB(a)
                    u0 = QK_UNITS + 6 * a
                    n = C * it + a
                    if a >= 2:
                        pe.wait_ge(h_new, n - 1)
                    if a > 0:
                        unit_part(u0, B[0], hs, True, False)
                    else:
                        pe.wait_ge(exped, (it + 1) * NT)
                    unit_part(u0 + 1, B[1], hs, True, False)
                    if a == 0:
                        broadcast(1)
                    unit_part(u0 + 2, B[2], hs, True, True)
                    unit_part(u0 + 3, B[0], qu, False, True, ready=updates_ready if a == 0 else None)
                    if a == 0:
                        pe.wait_ge(bc_kept, 2 * it + 2)
                    unit_part(u0 + 4, B[3], qu, True, True)
                    unit_part(u0 + 5, B[1], qu, False, True)

            iterations(pe, iteration)

            pe.wait_ge(h_new, C * ITERS - 1)
            for c in range(C):
                if c == C - 1:
                    pe.wait_ge(h_new, C * ITERS)
                for i in range(TT):
                    ins = turn(ps[4 + i][:, c * P:(c + 1) * P], h32[:, c, i * P:(i + 1) * P])
                    if c == C - 1:
                        ins.then_inc(back_turned, 1)

            def turn_xn(n):
                pe.wait_ge(xn_set, TT * (n + 1))
                for c in range(C):
                    for i in range(TT):
                        ins = turn(ps[c][:, i * P:(i + 1) * P], xn[:, i, c * P:(c + 1) * P])
                    ins.then_inc(xn_turned, 1)
                pe.wait_ge(xnT_set, C * (n + 1))

            turn_xn(0)
            pe.wait_ge(wqkv_in, 16 * C)
            for n, (i, w) in enumerate([(i, w) for i in range(TT) for w in range(2)] + [(i, 2) for i in range(TT)]):
                if n >= 2 * TT:
                    pe.wait_ge(qk_rot, n - 2 * TT + 1)
                elif n < C:
                    pe.wait_ge(xnT_set, C)
                for c in range(C):
                    ins = mm(ps[n % 8][:, :], xnT[:, c, i * P:(i + 1) * P], wqkv_s[:, c, w * D:(w + 1) * D], c == 0, c == C - 1)
                ins.then_inc(qkv_mm, 1)
            pe.wait_ge(qk_set, 2 * TT)
            pe.wait_ge(qkv_kept, TT)
            for n in range(2 * HG):
                src = q_n if n < HG else k_n
                for i in range(TT):
                    ins = turn(ps[n][:, i * P:(i + 1) * P], src[:, i, (n % HG) * P:(n % HG + 1) * P])
                ins.then_inc(qk_turned, 1)
            pe.wait_ge(qk_kept, 2 * HG)
            pe.wait_ge(mask_set, 2)
            pe.wait_ge(identb_set, 1)

            def s_product(n):
                hg, hh, i = steps[n]
                w = (i + 1) * P
                r = slice(HD * hh, HD * hh + HD)
                if n >= 4:
                    pe.wait_ge(s_exp, n - 3)
                mm(ps[n % 4][:, 0:w], qT[r, hg, i * P:(i + 1) * P], kT[r, hg, 0:w], True, False,
                   tile_position=(HD * hh, 0), skip_group_check=True)
                mm(ps[n % 4][:, i * P:w], identb, maskb, False, True, skip_group_check=True).then_inc(s_mm, 1)

            def turn_p(n):
                i = steps[n][2]
                pe.wait_ge(p_set, n + 1)
                if n >= 2:
                    pe.wait_ge(p_kept, n - 1)
                for b in range(i + 1):
                    ins = turn(ps[4 + n % 2][:, b * P:(b + 1) * P], ea[:, n % 4, b * P:(b + 1) * P])
                ins.then_inc(p_turned, 1)

            def pv(n):
                hg, hh, i = steps[n]
                pe.wait_ge(p_kept, n + 1)
                if hg >= 2 and hh == 0 and i == 0:
                    pe.wait_ge(att_kept, hg - 1)
                for b in range(i + 1):
                    ins = mm(ps[6 + hg % 2][HD * hh:HD * hh + HD, i * P:(i + 1) * P],
                             v_n[:, b, (4 * hg + hh) * HD:(4 * hg + hh + 1) * HD], pT[:, n % 4, b], b == 0, b == i,
                             tile_position=(0, HD * hh), skip_group_check=True)
                ins.then_inc(pv_mm, 1)

            for n in range(LEAD):
                s_product(n)
            for n in range(NS + 2):
                if n + LEAD < NS:
                    s_product(n + LEAD)
                if n < NS:
                    turn_p(n)
                if n >= 2:
                    pv(n - 2)
            pe.wait_ge(att_kept, HG)
            pe.wait_ge(wout_in, 16)
            for i in range(TT):
                for g in range(HG):
                    ins = mm(ps[4 + i][:, :], attT[:, g, i * P:(i + 1) * P], wout_s[:, g, :], g == 0, g == HG - 1)
                ins.then_inc(o_mm, 1)
            turn_xn(1)
            for i in range(TT):
                for c in range(C):
                    ins = mm(ps[0][:, i * NE:(i + 1) * NE], xnT[:, c, i * P:(i + 1) * P], pj[:, c * NE:(c + 1) * NE], c == 0, c == C - 1)
            ins.then_inc(z_mm, 1)
            pe.wait_ge(w1_in, 16)
            pe.wait_ge(w2_in, 16)

            def hidden(q):
                if q >= 2:
                    pe.wait_ge(h_act, q - 1)
                for c in range(C):
                    ins = mm(ps[4 + q % 2][:, :], w1_s[:, c, q * P:(q + 1) * P], xnT[:, c, :], c == 0, c == C - 1)
                ins.then_inc(h_mm, 1)

            def weight_rows(e):
                if e >= 2:
                    pe.wait_ge(hw_set, 2 * (e - 1))
                mm(ps[6 + e % 2][:, :], pick[:, e], rb[0:NE, :]).then_inc(wb_mm, 1)

            def expert_out(q):
                pe.wait_ge(hw_set, q + 1)
                for i in range(TT):
                    ins = mm(ps[i][:, :], hw_s[:, q, i * P:(i + 1) * P], w2_s[:, q, :], q == 0, q == 11)
                    if q == 11:
                        ins.then_inc(y_mm, 1)

            hidden(0)
            hidden(1)
            pe.wait_ge(w_set, 1)
            for i in range(TT):
                ins = pe.transpose(ps[6][0:NE, i * P:(i + 1) * P], rope_t[:, 2, 64 + i * NE:64 + (i + 1) * NE], ident)
            ins.then_inc(w_turned, 1)
            pe.wait_ge(wT_kept, 1)
            pe.wait_ge(pick_set, 1)
            weight_rows(0)
            weight_rows(1)
            for q in range(12):
                if q + 2 < 12:
                    hidden(q + 2)
                if q % 2 == 1 and q // 2 + 2 < NE:
                    weight_rows(q // 2 + 2)
                expert_out(q)


_INS = ['x', 'ctx', 'wq', 'wk', 'wv', 'wi_t', 'wh_u', 'win_b', 'small', 'half', 'wqkv_t', 'wout_t', 'w1_t', 'w2', 'proj_t']


def layouts(x, ctx_1024, L0_xattn_Wq, L0_xattn_Wk, L0_xattn_Wv, L0_xattn_gru_wi, L0_xattn_gru_wh,
            L0_xattn_gru_bi, L0_xattn_gru_bh, L0_xattn_slot_norm_w, L0_xattn_input_norm_w, L0_attn_w_qkv,
            L0_attn_w_out, L0_attn_q_norm_w, L0_attn_k_norm_w, L0_ffn_proj_w, L0_ffn_anchors,
            L0_ffn_routing_temp, L0_ffn_w1, L0_ffn_w2):
    f = lambda a: np.asarray(a)
    cols = lambda a, n: f(a).reshape(n, P).T
    rows = lambda a: np.broadcast_to(f(a).reshape(1, -1), (P, f(a).size))
    half = HD // 2
    inv = (1.0 / np.float32(10000.0) ** (np.arange(half, dtype=np.float32) * np.float32(2.0) / np.float32(HD))).astype(np.float32)
    ang = np.arange(K, dtype=np.float32)[:, None] * inv[None, :]
    cos, sin = np.cos(ang), np.sin(ang)
    by_tile = lambda a: a.reshape(TT, P, HD).transpose(1, 0, 2).reshape(P, TT * HD)
    cos = by_tile(np.concatenate([cos, cos], axis=1).astype(np.float32))
    sin = by_tile(np.concatenate([-sin, sin], axis=1).astype(np.float32))
    lower = rows(np.tril(np.ones((NE, NE), np.float32), -1))
    small = np.concatenate([
        cols(L0_xattn_gru_bi, 12), cols(L0_xattn_gru_bh, 12), cols(L0_xattn_slot_norm_w, C), cols(L0_xattn_input_norm_w, C),
        np.tile(f(L0_attn_q_norm_w), 4)[:, None], np.tile(f(L0_attn_k_norm_w), 4)[:, None], rows(L0_ffn_routing_temp),
        rows(L0_ffn_anchors), lower, cos, sin, np.eye(P, dtype=np.float32)], axis=1)
    wh_u = f(L0_xattn_gru_wh).reshape(3, C, P, C, P).transpose(4, 1, 0, 3, 2)
    return {
        "x": f(x), "ctx": f(ctx_1024), "wq": f(L0_xattn_Wq), "wk": f(L0_xattn_Wk), "wv": f(L0_xattn_Wv),
        "wi_t": f(L0_xattn_gru_wi).T, "wh_u": wh_u, "win_b": rows(L0_xattn_input_norm_w), "small": small,
        "half": np.concatenate([np.eye(P), np.zeros((P, P))], axis=1).astype(np.float16),
        "wqkv_t": f(L0_attn_w_qkv).T, "wout_t": f(L0_attn_w_out).T,
        "w1_t": f(L0_ffn_w1).transpose(1, 0, 2).reshape(D, NE * DE), "w2": f(L0_ffn_w2).reshape(NE * DE, D),
        "proj_t": f(L0_ffn_proj_w).reshape(NE, C, P).transpose(2, 1, 0).reshape(P, C * NE),
    }


def kernel(**inputs):
    import concourse.bacc as _bacc
    from concourse.bass_utils import run_bass_kernel_spmd as _run

    nc = _bacc.Bacc("TRN2", target_bir_lowering=False, num_devices=1)
    arrays, args = {}, []
    laid = layouts(**inputs)
    for name in _INS:
        a = np.ascontiguousarray(laid[name])
        arrays[f"in_{name}"] = a
        args.append(nc.dram_tensor(f"in_{name}", a.shape, mybir.dt.from_np(a.dtype), kind="ExternalInput").ap())
    args.append(nc.dram_tensor("out_0", (1, K, D), F32, kind="ExternalOutput").ap())
    slot_kernel(nc, *args)
    r = _run(nc, [arrays], core_ids=[0])
    return r.results[0]["out_0"]
```

```python
from contextlib import ExitStack

import numpy as np

import concourse.bass as bass
from concourse import mybir

F32 = mybir.dt.float32
F16 = mybir.dt.float16
BF16 = mybir.dt.bfloat16
ALU = mybir.AluOpType
ACT = mybir.ActivationFunctionType
AX = mybir.AxisListType

P = 128
D = 512
C = D // P
K = 512
TT = K // P
M = 8192
NT = M // P
NG = 16
RING = NT // NG
ITERS = 3
H = 16
HD = D // H
HG = H // 4
NE = 6
DE = 256
TOPK = 2
EPS = 1e-6
LN_EPS = 1e-5
QUANT_TEMP = 0.3
SCALE = float(D) ** -0.5
ATT_SCALE = float(HD) ** -0.5

S_X = 2.0 ** 10
S_A = 2.0 ** 15
S_W = 2.0 ** 15
TINY = 1e-30

G_PLACE = (3, 5, 4)
QK_UNITS = C
GATE_UNITS = 6 * C
UNITS = QK_UNITS + GATE_UNITS
WRING = 7
GATE_LANES = WRING - QK_UNITS
GATE_GROUPS = GATE_UNITS // GATE_LANES
assert GATE_UNITS % GATE_LANES == 0 and GATE_LANES < RING and GATE_GROUPS < NG - 1
assert UNITS % WRING == 0 and NT % RING == 0 and NG >= 3

BI, BH, WSLOT, WIN = 0, 12, 24, 28
QW, KW, TEMP, ANCH = 32, 33, 34, 35
LOWER = ANCH + 36
COS = LOWER + 36
SIN = COS + TT * HD
IDENT = SIN + TT * HD
SMALL = IDENT + P

PARTS3 = ((0, 0), (0, 1), (1, 0))


def slot_kernel(nc, x, ctx, wq, wk, wv, wi_t, wh_u, win_b, small, half, wqkv_t, wout_t, w1_t, w2,
                proj_t, out):
    stack = ExitStack()
    with stack:
        def sb(name, shape, dt=F32):
            return stack.enter_context(nc.sbuf_tensor(name, shape, dt))

        def sem(name):
            return stack.enter_context(nc.semaphore(name))

        pt_dram = nc.dram_tensor("pt_scratch", (NT, P, 2 * C * P), F16, kind="Internal").ap()
        wu_dram = nc.dram_tensor("weight_units", (UNITS, P, 2 * C * P), F16, kind="Internal").ap()

        pn = sb("pn", [P, NT * 2 * D], F16)
        pt = sb("pt", [P, RING, 2, C, P], F16)
        cx = sb("cx", [P, RING, D])
        wr = sb("wr", [P, WRING, 2, C, P], F16)
        h32 = sb("h32", [P, C, K])
        hs = sb("hs", [P, 2, C, K], F16)
        qu = sb("qu", [P, 2, C, K], F16)
        ea = sb("ea", [P, 4, K])
        ah = sb("ah", [P, 2, 2, K], F16)
        acc = sb("acc", [P, K])
        diag = sb("diag", [P, TT, P])
        rb = sb("rb", [P, K])
        sm = sb("sm", [P, SMALL])
        hf = sb("hf", [P, 2 * P], F16)
        bm = sb("bm", [P, 2 * P], BF16)
        ones = sb("ones", [P, P])
        st = sb("st", [P, 128])
        pj = sb("pj", [P, C * NE])
        ident = sm[:, IDENT:IDENT + P]
        ident16, zeros16 = hf[:, 0:P], hf[:, P:2 * P]
        identb, maskb = bm[:, 0:P], bm[:, P:2 * P]

        def pn_tile(t, part):
            return pn[:, bass.ds(t * (2 * D) + part * D, D)]

        def pn_w(t, part, c):
            return pn[:, bass.ds(t * (2 * D) + part * D + c * P, P)]

        pn32 = pn[:, :].bitcast(F32)

        def region(at, n):
            return pn32[:, at:at + n]

        base = NT * D
        GU = C * P
        pick = ea[:, 2:4].rearrange("p a k -> p (a k)")[0:NE, 0:NE * P].rearrange("p (e k) -> p e k", e=NE)
        def take(n):
            nonlocal base
            base -= n
            return region(base, n)
        w_all = take(GATE_UNITS * GU).rearrange("p (a g c e) -> p a g c e", a=C, g=6, c=C)
        w_units = w_all.rearrange("p a g c e -> p (a g c e)")
        wiT = take(C * 3 * D).rearrange("p (c e) -> p c e", c=C)
        wv_s = take(C * D).rearrange("p (c e) -> p c e", c=C)
        wq_s = take(C * D).rearrange("p (c e) -> p c e", c=C)
        wk_s = take(C * D).rearrange("p (c e) -> p c e", c=C)
        wqk = take(C * D).rearrange("p (c e) -> p c e", c=C)
        winb = take(D)
        x_s = take(TT * D).rearrange("p (t d) -> p t d", t=TT)
        assert base >= 4 * D
        wqkv_s = region(0, C * 3 * D).rearrange("p (c e) -> p c e", c=C)
        wout_s = region(C * 3 * D, C * D).rearrange("p (c e) -> p c e", c=C)
        w1_s = region(C * 4 * D, 12 * GU).rearrange("p (c e) -> p c e", c=C)
        w2_s = region(C * 4 * D + 12 * GU, 12 * D).rearrange("p (q e) -> p q e", q=12)
        w_ffn = region(C * 4 * D, 12 * GU + 12 * D)
        w1h = region(0, 12 * GU).bitcast(F16).rearrange("p (a c e) -> p a c e", a=2, c=C)
        w2h = region(C * 4 * D, 12 * GU).bitcast(F16).rearrange("p (a q e) -> p a q e", a=2, q=12)
        hwh = region(C * 4 * D + 12 * GU, 12 * K).bitcast(F16).rearrange("p (a q t) -> p a q t", a=2, q=12)
        TAIL_W = C * 4 * D + 12 * GU + 12 * D
        vals = [region(TAIL_W + i * TT * D, TT * D).rearrange("p (t d) -> p t d", t=TT) for i in range(6)]
        x1, xn, xnT, q_n, k_n, v_n = vals
        assert TAIL_W + 6 * TT * D <= NT * D
        xh = [b.rearrange("p t d -> p (t d)").bitcast(F16).rearrange("p (a c t) -> p a c t", a=2, c=C) for b in (xnT, q_n)]
        qT = cx[:, :, :]
        qkvh = (hs[:, :, :, :], qu[:, :, :, :],
                h32[:, :, :].rearrange("p c k -> p (c k)").bitcast(F16).rearrange("p (a c e) -> p a c e", a=2, c=C))
        kT = pt[:, :, :, :, :].bitcast(F32).rearrange("p a b c d -> p a (b c d)")
        attT = hs[:, :, :, :].bitcast(F32).rearrange("p a c k -> p (a c k)").rearrange("p (h t) -> p h t", h=HG)
        pT = qu[:, :, :, :].bitcast(F32).rearrange("p a c k -> p (a c k)").rearrange("p (s b k) -> p s b k", s=4, b=TT)
        rope_t = wr[:, :, :, :, :].bitcast(F32).rearrange("p s a c k -> p (s a c k)")[:, 0:6 * D].rearrange("p (s d) -> p s d", s=6)

        ps = [stack.enter_context(nc.psum_tensor(f"bank{i}", [P, 512], F32)) for i in range(8)]
        U = ps[0:4]
        SC = ps[4:6]
        TP = ps[6:8]
        RED, BC = ps[7], ps[7]
        QB = (ps[4], ps[5], ps[6], ps[0])
        slot_squares = (acc[:, :], rb[:, :], diag[:, :, :].rearrange("p a b -> p (a b)"), ea[:, 3])

        consts_in = sem("consts_in")
        x_in, wqk_in, wqk_rest_in, wh_in = (sem(n) for n in ("x_in", "wqk_in", "wqk_rest_in", "wh_in"))
        wi_in = [sem(f"wi_in{i}") for i in range(3)]
        ones_set = sem("ones_set")
        vec = sem("vec_step")
        pool_pow = sem("pool_pow")
        ln_stats = sem("ln_stats")
        x_normed = sem("x_normed")
        x_turned = sem("x_turned")
        slots_copied = sem("slots_copied")
        slots_high, slots_low = sem("slots_high"), sem("slots_low")
        wqk_mm, wqk_kept, wqk_sq = sem("wqk_mm"), sem("wqk_kept"), sem("wqk_sq")
        g_mm, g_kept = sem("g_mm"), sem("g_kept")
        gate_sq = sem("gate_sq")
        norm_sum = sem("norm_sum")
        norm_in = sem("norm_in")
        sq_summed = sem("sq_summed")
        scales_set = sem("scales_set")
        unit_high, unit_low = sem("unit_high"), sem("unit_low")
        unit_stored = [sem(f"unit_stored{i}") for i in range(WRING)]
        unit_in = [sem(f"unit_in{i}") for i in range(WRING)]
        unit_used = sem("unit_used")
        ctx_in = [sem(f"ctx_in{i}") for i in range(RING)]
        row_sq, row_ms, row_r = sem("row_sq"), sem("row_ms"), sem("row_r")
        part_high, part_low = sem("part_high"), sem("part_low")
        turned, kept = sem("tile_turned"), sem("tile_kept")
        stored = [sem(f"tile_stored{i}") for i in range(RING)]
        pt_in = [sem(f"pt_in{i}") for i in range(RING)]
        slot_sq = sem("slot_sq")
        slot_sq_sum = sem("slot_sq_sum")
        sum_mm = sem("sum_mm")
        sum_in = sem("sum_in")
        factor = sem("factor")
        diag_set = sem("diag_set")
        bc_mm = sem("bc_mm")
        bc_kept = sem("bc_kept")
        q_kept, q_high, q_low = sem("q_kept"), sem("q_high"), sem("q_low")
        scored, maxed, nmaxed, exped = sem("scored"), sem("maxed"), sem("nmaxed"), sem("exped")
        recip = sem("recip")
        attn_set, attn_high, attn_low = sem("attn_set"), sem("attn_high"), sem("attn_low")
        updated = sem("updated")
        acc_done = sem("acc_done")
        u_kept, u_high, u_low = sem("u_kept"), sem("u_high"), sem("u_low")
        tanh_r, tanh_z, tanh_n = sem("tanh_r"), sem("tanh_z"), sem("tanh_n")
        hid_set, n_in_set, h_new = sem("hid_set"), sem("n_in_set"), sem("h_new")
        gru_step = sem("gru_step")

        wqkv_in, x1_in, wout_in, w1_in, w2_in = (sem(n) for n in ("wqkv_in", "x1_in", "wout_in", "w1_in", "w2_in"))
        y_set, out_stored = sem("y_set"), sem("out_stored")
        back_turned, x1_set, xn_set, xn_turned = (sem(n) for n in ("back_turned", "x1_set", "xn_set", "xn_turned"))
        OTHER_UNITS = [8, 9, 10, 11, 20, 21, 22, 23]
        POOL_UNITS = [u for u in range(24) if u not in OTHER_UNITS]
        OTHER_AT = {8: 8, 14: 9, 20: 10, 26: 11, 40: 20, 46: 21, 52: 22, 58: 23}
        ffn_high_pool, ffn_low_pool = sem("ffn_high_pool"), sem("ffn_low_pool")

        def ffn_unit(u):
            if u < 12:
                e = slice((u // C) * D, (u // C) * D + D)
                return w1_s[:, u % C, e], w1h[:, 0, u % C, e], w1h[:, 1, u % C, e]
            return w2_s[:, u - 12], w2h[:, 0, u - 12], w2h[:, 1, u - 12]

        HW32 = (rope_t[:, 4], rope_t[:, 5])
        qkv_mm, qkv_kept = sem("qkv_mm"), sem("qkv_kept")
        rope_sq, head_rms, qk_set = sem("rope_sq"), sem("head_rms"), sem("qk_set")
        qT_turned, qT_kept, kT_turned, kT_kept = (sem(n) for n in ("qT_turned", "qT_kept", "kT_turned", "kT_kept"))
        head_r = sem("head_r")
        s_mm, s_max, s_exp, p_set, p_turned, p_kept, pv_mm, att_kept = (
            sem(n) for n in ("s_mm", "s_max", "s_exp", "p_set", "p_turned", "p_kept", "pv_mm", "att_kept"))
        o_mm = sem("o_mm")
        z_mm, router_exps, l_sub, w_set, w_turned, wT_kept = (
            sem(n) for n in ("z_mm", "router_exps", "l_sub", "w_set", "w_turned", "wT_kept"))
        h_mm, h_act, wb_mm, hw_set, y_mm = (sem(n) for n in ("h_mm", "h_act", "wb_mm", "hw_set", "y_mm"))
        steps = [(hg, hh, i) for hg in range(HG) for hh in range(4) for i in range(TT)]
        NS = len(steps)
        LEAD = 3
        LEAD_T = 3
        LEAD_S = RING
        pickers_set = sem("pickers_set")
        qkv_sq, qkv_scales = sem("qkv_sq"), sem("qkv_scales")
        qkvh_high, qkvh_low = sem("qkvh_high"), sem("qkvh_low")
        v_low, w_scaled = sem("v_low"), sem("w_scaled")
        xh_high, xh_low = sem("xh_high"), sem("xh_low")
        ffn_sq, ffn_high, ffn_low = sem("ffn_sq"), sem("ffn_high"), sem("ffn_low")
        x32_set, hw_high, hw_low = sem("x32_set"), sem("hw_high"), sem("hw_low")
        head_sum = sem("head_sum")
        mask_set = sem("mask_set")
        z_step, rope_step = sem("z_step"), sem("rope_step")
        junk = sb("junk", [P, D], F16)
        gb = sb("gb", [P, 3 * C])
        qk_rot = sem("qk_rot")

        def GB(a):
            return (ps[6], ps[4], ps[5], ps[7]) if a % 2 == 0 else ps[0:4]

        def keep_pT(act, n):
            w = (steps[n][2] + 1) * P
            act.wait_ge(p_turned, n + 1)
            if n >= 4:
                act.wait_ge(pv_mm, n - 3)
            act.activation(pT[:, n % 4].rearrange("p b k -> p (b k)")[:, 0:w], ps[4 + n % 2][:, 0:w], ACT.Copy)\
                .then_inc(p_kept, 1)

        block = stack.enter_context(nc.Block())

        def iterations(eng, body):
            body(0, True)
            with eng.Fori(1, ITERS) as it:
                body(it, False)

        def tiles(eng, body, first=0, last=NG):
            with eng.Fori(first, last) as g:
                for j in range(RING):
                    body(g, j)

        def ahead(g, j, k):
            return g + (j + k) // RING, (j + k) % RING

        def gate_unit(g, j):
            return w_units[:, bass.ds((g * GATE_LANES + j) * GU, GU)]

        def is_first(g):
            return isinstance(g, int) and g == 0

        @block.sync
        def _(sp):
            for half_in, h in ((wqk_in, slice(0, C // 2)), (wqk_rest_in, slice(C // 2, C))):
                for dst, src in ((wq_s, wq), (wk_s, wk)):
                    sp.dma_start(dst[:, h], src.rearrange("(c p) e -> p c e", p=P)[:, h]).then_inc(half_in, 16)
            sp.dma_start(sm[:, :], small).then_inc(consts_in, 16)
            sp.dma_start(hf[:, :], half).then_inc(consts_in, 16)
            sp.dma_start(winb, win_b).then_inc(consts_in, 16)
            sp.dma_start(pj[:, :], proj_t).then_inc(consts_in, 16)
            sp.dma_start(wv_s, wv.rearrange("(c p) e -> p c e", p=P)).then_inc(wi_in[0], 16)
            for gt in range(3):
                if gt == 2:
                    sp.dma_start(x_s, x[0].rearrange("(t p) d -> p t d", p=P)).then_inc(x_in, 16)
                e = slice(gt * D, (gt + 1) * D)
                sp.dma_start(wiT[:, :, e], wi_t.rearrange("(c p) e -> p c e", p=P)[:, :, e]).then_inc(wi_in[gt], 16)
            for a in range(C):
                sp.dma_start(w_all[:, a, 0:3], wh_u[:, a]).then_inc(wh_in, 16)

            ctx_v = ctx[0].rearrange("(p t) d -> p (t d)", t=NT)

            def load_ctx(g, j):
                sp.dma_start(cx[:, j, :], ctx_v[:, bass.ds((g * RING + j) * D, D)]).then_inc(ctx_in[j], 16)

            for j in range(RING):
                load_ctx(0, j)
            for u in range(QK_UNITS):
                sp.wait_ge(unit_low, u + 1)
                sp.dma_start(wu_dram[u], wr[:, u].rearrange("p a c e -> p (a c e)")).then_inc(unit_stored[u], 16)

            def load_units(it, first, last):
                for u in range(first, last):
                    if is_first(it) and u < WRING:
                        sp.wait_ge(unit_stored[u], 16 if u < QK_UNITS else 16 * GATE_GROUPS)
                    else:
                        sp.wait_ge(unit_used, it * UNITS + (u - WRING + 1))
                    sp.dma_start(wr[:, u % WRING].rearrange("p a c e -> p (a c e)"), wu_dram[u])\
                        .then_inc(unit_in[u % WRING], 16)

            load_units(0, 0, QK_UNITS)

            def store_tile(g, j):
                sp.wait_ge(kept, g * RING + j + 1)
                sp.dma_start(pt_dram[bass.ds(g * RING + j, 1)].rearrange("a p n -> p (a n)"),
                             pt[:, j].rearrange("p a c e -> p (a c e)")).then_inc(stored[j], 16)

            def store_unit(g, j):
                sp.wait_ge(unit_low, g * GATE_LANES + (QK_UNITS + j + 1))
                sp.dma_start(wu_dram[bass.ds(g * GATE_LANES + (QK_UNITS + j), 1)].rearrange("a p n -> p (a n)"),
                             wr[:, QK_UNITS + j].rearrange("p a c e -> p (a c e)")).then_inc(unit_stored[QK_UNITS + j], 16)

            def store_and_load(g, j):
                sp.wait_ge(part_low, g * RING + j + 1)
                load_ctx(g + 1, j)
                store_tile(g, j)

            def store_all(g, j):
                store_and_load(g, j)
                if j < GATE_LANES:
                    store_unit(g - 1, j)

            for j in range(RING):
                store_and_load(0, j)
            tiles(sp, store_all, 1, GATE_GROUPS + 1)
            tiles(sp, store_and_load, GATE_GROUPS + 1, NG - 1)
            for j in range(RING):
                store_tile(NG - 1, j)
            for s in stored:
                sp.wait_ge(s, 16 * (NG))
            for u in range(QK_UNITS, WRING):
                sp.wait_ge(unit_stored[u], 16 * GATE_GROUPS)
            load_units(0, QK_UNITS, UNITS)

            def load_pt(it, g, j):
                sp.wait_ge(scored, it * NT + (g * RING + (j + 1 - RING)))
                sp.dma_start(pt[:, j].rearrange("p a c e -> p (a c e)"),
                             pt_dram[bass.ds(g * RING + j, 1)].rearrange("a p n -> p (a n)")).then_inc(pt_in[j], 16)

            with sp.Fori(1, ITERS) as it:
                load_units(it, 0, QK_UNITS)
                tiles(sp, lambda g, j: load_pt(it, g, j))
                load_units(it, QK_UNITS, UNITS)
            for i in range(TT):
                sp.wait_ge(y_set, i + 1)
                sp.dma_start(out[0, i * P:(i + 1) * P, :], x1[:, i]).then_inc(out_stored, 16)
            sp.wait_ge(out_stored, 16 * TT)


        @block.gpsimd
        def _(pool):
            pool.memset(ones[:, :], 1.0).then_inc(ones_set, 1)
            pool.memset(st[:, 0:1], -0.5).then_inc(ones_set, 1)
            pool.memset(st[:, 1:2], EPS / S_X ** 2).then_inc(ones_set, 1)
            pool.memset(st[:, 2:3], EPS).then_inc(ones_set, 1)
            pool.wait_ge(ones_set, 4)

            def power(src, dst, n, done):
                pool.tensor_tensor(dst, src, st[:, 0:1].to_broadcast([P, n]), ALU.pow).then_inc(done, 1)

            pool.wait_ge(ln_stats, 1)
            power(st[:, 8:12], st[:, 12:16], 4, pool_pow)
            pool.wait_ge(norm_in, 1)
            power(st[:, 16:17], st[:, 18:19], 1, pool_pow)

            def iteration(it, first):
                if not first:
                    pool.wait_ge(sum_in, it + 1)
                    power(st[:, 32:36], st[:, 36:40], 4, factor)
                    pool.memset(acc[:, :], 0.0).then_inc(acc_done, 1)

                def row_scale(g, j):
                    pool.wait_ge(row_sq, g * RING + j + 1)
                    pool.tensor_tensor(st[:, 44 + j:45 + j], st[:, 40 + j:41 + j], st[:, 1:2], ALU.add).then_inc(row_ms, 1)
                    pool.wait_ge(row_ms, g * RING + j + 1)
                    power(st[:, 44 + j:45 + j], st[:, 48 + j:49 + j], 1, row_r)

                def add(g, j):
                    T = it * NT + g * RING + j
                    pool.wait_ge(attn_set, T + 1)
                    pool.wait_ge(acc_done, T + it + 2)
                    pool.tensor_tensor(acc[:, :], acc[:, :], ea[:, 2 + j % 2], ALU.add).then_inc(acc_done, 1)

                def with_scale(g, j):
                    row_scale(*ahead(g, j, LEAD_S))
                    add(g, j)

                if first:
                    row_scale(0, 0)
                    pool.wait_ge(sum_in, 1)
                    power(st[:, 32:36], st[:, 36:40], 4, factor)
                    pool.memset(acc[:, :], 0.0).then_inc(acc_done, 1)
                    for j in range(1, LEAD_S):
                        row_scale(0, j)
                    pool.wait_ge(norm_in, 2)
                    power(st[:, 17:18], st[:, 19:20], 1, pool_pow)
                    tiles(pool, with_scale, 0, NG - 1)
                    for j in range(RING):
                        add(NG - 1, j)
                else:
                    tiles(pool, add)

            pool.sem_inc(acc_done, 1)
            pool.memset(maskb, 0.0).then_inc(mask_set, 1)
            pool.wait_ge(mask_set, 1)
            pool.affine_select(out=maskb, in_=maskb, compare_op=ALU.is_ge, fill=-1e30, base=0,
                               pattern=[[-1, P]], channel_multiplier=1).then_inc(mask_set, 1)
            iterations(pool, iteration)
            pool.wait_ge(updated, ITERS * NT)
            pool.dma_start(x1, x[0].rearrange("(t p) d -> p t d", p=P)).then_inc(x1_in, 16)
            for c in range(C):
                pool.wait_ge(unit_used, (ITERS - 1) * UNITS + QK_UNITS + 4 * c + 2)
                pool.dma_start(wqkv_s[:, c], wqkv_t[c * P:(c + 1) * P, :]).then_inc(wqkv_in, 16)
            pool.wait_ge(unit_used, ITERS * UNITS - 6)
            pool.dma_start(wout_s, wout_t.rearrange("(c p) e -> p c e", p=P)).then_inc(wout_in, 16)
            pool.wait_ge(unit_used, ITERS * UNITS - 3)
            pool.dma_start(w1_s, w1_t.rearrange("(c p) e -> p c e", p=P)).then_inc(w1_in, 16)
            pool.dma_start(w2_s, w2.rearrange("(q p) e -> p q e", p=P)).then_inc(w2_in, 16)
            def row_powers(n):
                for i in range(TT):
                    pool.wait_ge(ln_stats, n + i + 1)
                    power(st[:, 8 + i:9 + i], st[:, 12 + i:13 + i], 1, pool_pow)

            row_powers(1)
            pool.wait_ge(norm_in, 3)
            power(st[:, 74:75], st[:, 75:76], 1, pool_pow)
            pool.wait_ge(pool_pow, 8)
            pool.wait_ge(slot_sq_sum, 4 * (ITERS + 1))
            scaled = (acc[:, :], diag[:, :, :].rearrange("p a b -> p (a b)"))
            for c in range(C):
                if c >= 2:
                    pool.wait_ge(v_low, c - 1)
                pool.tensor_scalar(scaled[c % 2], wqkv_s[:, c, 2 * D:3 * D], st[:, 75:76], None, ALU.mult).then_inc(w_scaled, 1)
                pool.wait_ge(w_scaled, c + 1)
                pool.wait_ge(qkvh_high, 2 * C + c + 1)
                pool.tensor_tensor(qkvh[2][:, 1, c], scaled[c % 2], qkvh[2][:, 0, c], ALU.subtract).then_inc(v_low, 1)
            for n in range(2 * TT):
                o = (n % 2) * 64
                pool.wait_ge(qk_rot, n + 1)
                pool.wait_ge(head_r, n + 1)
                pool.tensor_tensor((q_n, k_n)[n // TT][:, n % TT].rearrange("p (h d) -> p h d", h=H),
                                   rope_t[:, n % 2].rearrange("p (h d) -> p h d", h=H),
                                   rope_t[:, 5, o + 32:o + 32 + H].unsqueeze(2).to_broadcast([P, H, HD]), ALU.mult)\
                    .then_inc(qk_set, 1)
            pool.wait_ge(norm_in, 4)
            power(st[:, 90:92], st[:, 92:94], 2, pool_pow)
            pool.wait_ge(pool_pow, 9)
            pool.wait_ge(qkv_mm, 3 * TT)
            for m, u in enumerate(POOL_UNITS):
                src, hi, lo = ffn_unit(u)
                s_w = st[:, 92 + u // 12:93 + u // 12]
                if m >= 2:
                    pool.wait_ge(ffn_low_pool, m - 1)
                else:
                    pool.wait_ge(v_low, C)
                if u >= 12:
                    pool.wait_ge(ffn_low, sum(v < 12 for v in OTHER_UNITS))
                    pool.wait_ge(ffn_low_pool, sum(v < 12 for v in POOL_UNITS))
                pool.tensor_scalar(hi, src, s_w, None, ALU.mult).then_inc(ffn_high_pool, 1)
                pool.tensor_scalar(scaled[m % 2], src, s_w, None, ALU.mult).then_inc(w_scaled, 1)
                pool.wait_ge(ffn_high_pool, m + 1)
                pool.wait_ge(w_scaled, C + m + 1)
                pool.tensor_tensor(lo, scaled[m % 2], hi, ALU.subtract).then_inc(ffn_low_pool, 1)
            row_powers(1 + TT)
        @block.scalar
        def _(act):
            def split_high(dst, src, scale, done):
                act.activation(dst, src, ACT.Copy, scale=scale).then_inc(done, 1)

            def square_slots(c):
                act.activation(slot_squares[c], h32[:, c], ACT.Square).then_inc(slot_sq, 1)

            act.wait_ge(consts_in, 64)
            act.wait_ge(wqk_kept, C)
            act.activation(ea[:, :, :], wqk, ACT.Square, accum_out=st[:, 20:21]).then_inc(wqk_sq, 1)
            def put_slots():
                for c in range(C):
                    act.wait_ge(x_turned, c + 1)
                    act.activation(h32[:, c], ps[c][:, :], ACT.Copy).then_inc(slots_copied, 1)
                    act.wait_ge(slots_copied, c + 1)
                    split_high(hs[:, 0, c], h32[:, c], S_X, slots_high)
                    if c < C - 1:
                        square_slots(c)

            for n in range(3 * C):
                if n == 3:
                    put_slots()
                c, gt = n // 3, n % 3
                act.wait_ge(g_mm, n + 1)
                act.activation(w_all[:, :, G_PLACE[gt], c, :], ps[4 + n % 4][:, :].rearrange("p (a e) -> p a e", a=C),
                               ACT.Copy, scale=sm[:, WIN + c:WIN + c + 1]).then_inc(g_kept, 1)
                act.wait_ge(g_kept, n + 1)
                if n == 0:
                    act.wait_ge(wqk_sq, 1)
                act.wait_ge(gate_sq, n + min(C, max(0, n - 3)))
                act.activation(ea[:, 0].rearrange("p (a e) -> p a e", a=C), w_all[:, :, G_PLACE[gt], c, :], ACT.Square,
                               accum_out=st[:, 56 + n:57 + n]).then_inc(gate_sq, 1)
                if 3 <= n < 3 + C:
                    a = n - 3
                    act.wait_ge(wh_in, 16 * C)
                    act.wait_ge(gate_sq, n + 1 + a)
                    act.activation(ea[:, 0:3].rearrange("p a k -> p (a k)"),
                                   w_all[:, a, 0:3].rearrange("p g c e -> p (g c e)"), ACT.Square,
                                   accum_out=st[:, 68 + a:69 + a]).then_inc(gate_sq, 1)
                if n == 5:
                    act.wait_ge(scales_set, 1)
                    for u in range(QK_UNITS):
                        split_high(wr[:, u, 0], wqk[:, :, u * P:(u + 1) * P], st[:, 24:25], unit_high)
            def gate_high(g, j):
                if is_first(g):
                    act.wait_ge(scales_set, 2)
                else:
                    act.wait_ge(unit_stored[QK_UNITS + j], 16 * g)
                act.activation(wr[:, QK_UNITS + j, 0].rearrange("p c e -> p (c e)"), gate_unit(g, j), ACT.Copy,
                               scale=st[:, 26:27]).then_inc(unit_high, 1)

            def iteration(it, first):
                def query_high():
                    for f in range(C):
                        act.wait_ge(q_kept, C * it + f + 1)
                        split_high(qu[:, 0, f], ea[:, f], 1.0, q_high)

                if not first:
                    query_high()

                def square(g, j):
                    act.wait_ge(ctx_in[j], 16 * g + 16)
                    act.activation(junk[:, :], cx[:, j, :], ACT.Square, scale=D ** -0.5 / S_X, accum_out=st[:, 40 + j:41 + j]).then_inc(row_sq, 1)

                def keep(g, j):
                    act.wait_ge(turned, g * RING + j + 1)
                    if not is_first(g):
                        act.wait_ge(stored[j], 16 * g)
                    act.activation(pt[:, j].rearrange("p a c e -> p (a c e)"), TP[j % 2][:, :].bitcast(F16), ACT.Copy)\
                        .then_inc(kept, 1)

                def soft(g, j):
                    act.wait_ge(nmaxed, it * NT + g * RING + j + 1)
                    act.activation(ea[:, j % 2], SC[j % 2][:, :], ACT.Exp, bias=st[:, 80 + j % 2:81 + j % 2],
                                   scale=st[:, 25:26], accum_out=st[:, 84 + j % 2:85 + j % 2]).then_inc(exped, 1)

                def high(g, j):
                    act.wait_ge(attn_set, it * NT + g * RING + j + 1)
                    act.activation(ah[:, j % 2, 0], ea[:, 2 + j % 2], ACT.Copy).then_inc(attn_high, 1)

                def plain(g, j):
                    soft(g, j)
                    high(g, j)

                def full(g, j):
                    soft(g, j)
                    square(*ahead(g, j, LEAD_S))
                    high(g, j)
                    keep(*ahead(g, j, 2))

                if first:
                    for j in range(LEAD_S):
                        if j:
                            act.wait_ge(row_sq, j)
                        square(0, j)
                    query_high()
                    keep(0, 0)
                    keep(0, 1)
                    def with_gates(g, j):
                        full(g, j)
                        if j < GATE_LANES:
                            gate_high(g, j)

                    for j in range(RING):
                        with_gates(0, j)
                    tiles(act, with_gates, 1, GATE_GROUPS)
                    tiles(act, full, GATE_GROUPS, NG - 1)
                    for j in range(RING):
                        soft(NG - 1, j)
                        high(NG - 1, j)
                        if j + 2 < RING:
                            keep(NG - 1, j + 2)
                else:
                    tiles(act, plain)
                for c in range(C):
                    act.wait_ge(u_kept, C * it + c + 1)
                    split_high(qu[:, 0, c], ea[:, c], 1.0, u_high)
                def high_slots(c):
                    split_high(hs[:, 0, c], h32[:, c], S_X, slots_high)

                for a in range(C):
                    n = C * it + a
                    unit = it * UNITS + QK_UNITS + 6 * a
                    act.wait_ge(unit_used, unit + 4)
                    if a == 0:
                        act.wait_ge(u_low, C * (it + 1))
                    else:
                        act.wait_ge(h_new, n)
                    A = GB(a)
                    act.activation(ea[:, 0], A[0][:, :], ACT.Tanh, bias=gb[:, a:a + 1],
                                   scale=st[:, 27:28]).then_inc(tanh_r, 1)
                    if a >= 1:
                        square_slots(a - 1)
                    if a == C - 1:
                        high_slots(0)
                        high_slots(1)
                    act.wait_ge(n_in_set, n + 1)
                    act.activation(ea[:, 3], ea[:, 2], ACT.Tanh, bias=sm[:, BI + 8 + a:BI + 9 + a]).then_inc(tanh_n, 1)
                    if a == C - 1:
                        high_slots(2)
                    act.wait_ge(unit_used, unit + 6)
                    act.activation(ea[:, 1], A[1][:, :], ACT.Tanh, bias=gb[:, C + a:C + a + 1],
                                   scale=st[:, 27:28]).then_inc(tanh_z, 1)
                act.wait_ge(h_new, C * it + C)
                high_slots(C - 1)

            iterations(act, iteration)

            act.wait_ge(wqkv_in, 16 * C)
            w_flat = wqkv_s.rearrange("p c e -> p (c e)")
            for m in range(3):
                if m >= 1:
                    act.wait_ge(qkv_sq, m)
                act.activation(v_n.rearrange("p t d -> p (t d)"), w_flat[:, m * C * D:(m + 1) * C * D], ACT.Square,
                               accum_out=st[:, 64 + m:65 + m]).then_inc(qkv_sq, 1)

            def high_w(w, c):
                split_high(qkvh[w][:, 0, c], wqkv_s[:, c, w * D:(w + 1) * D], st[:, 75:76], qkvh_high)

            def high_x(n, c):
                act.wait_ge(xn_turned, C * n + c + 1)
                split_high(xh[n][:, 0, c], ps[c][:, :], S_X, xh_high)

            act.wait_ge(slots_high, C * (ITERS + 1))
            act.wait_ge(slots_low, C * (ITERS + 1))
            act.wait_ge(unit_used, ITERS * UNITS)
            act.wait_ge(pool_pow, 8)
            for c in range(C):
                high_w(0, c)
                high_x(0, c)
            for c in range(C):
                high_w(1, c)
            act.wait_ge(back_turned, TT)
            for c in range(C):
                high_w(2, c)
            act.wait_ge(qkv_scales, 1)

            def head_squares(n):
                act.wait_ge(qkv_mm, n + 1)
                act.activation(rope_t[:, 3 + n % 2], ps[n][:, :], ACT.Square).then_inc(rope_sq, 1)

            head_squares(0)
            for n in range(2 * TT):
                act.wait_ge(head_sum, n + 1)
                if n >= 2:
                    act.wait_ge(head_r, n - 1)
                o = (n % 2) * 64
                act.activation(rope_t[:, 5, o + 16:o + 16 + H], rope_t[:, 5, o:o + H], ACT.Sqrt, scale=1 / HD,
                               bias=st[:, 78:79]).then_inc(head_rms, 1)
                if n + 1 < 2 * TT:
                    head_squares(n + 1)
                if n == 0:
                    act.wait_ge(slot_sq_sum, 4 * (ITERS + 1))
                act.wait_ge((w1_in, w2_in)[n // 4], 16)
                act.wait_ge(ffn_sq, n)
                act.activation(ea[:, 0:3].rearrange("p a k -> p (a k)"), w_ffn[:, n * 3 * D:(n + 1) * 3 * D], ACT.Square,
                               accum_out=st[:, 80 + n:81 + n]).then_inc(ffn_sq, 1)
                if n in (6, 7):
                    for i in (2 * (n - 6), 2 * (n - 6) + 1):
                        act.wait_ge(qkv_mm, 2 * TT + i + 1)
                        act.activation(v_n[:, i], ps[i][:, :], ACT.Copy, scale=st[:, 77:78]).then_inc(qkv_kept, 1)
            for g in range(HG):
                act.wait_ge(qT_turned, g + 1)
                act.activation(qT[:, g], ps[g][:, :], ACT.Copy, scale=st[:, 52:53]).then_inc(qT_kept, 1)
            for n in range(NS):
                _, _, i = steps[n]
                w = (i + 1) * P
                act.wait_ge(s_max, n + 1)
                act.activation(ea[:, n % 4, 0:w], ps[n % 4][:, 0:w], ACT.Exp, bias=st[:, 56 + n % 4:57 + n % 4],
                               accum_out=st[:, 60 + n % 4:61 + n % 4]).then_inc(s_exp, 1)
                if n >= 2:
                    keep_pT(act, n - 2)
                if n in OTHER_AT:
                    u = OTHER_AT[n]
                    src, hi, _ = ffn_unit(u)
                    act.wait_ge(pool_pow, 9)
                    act.wait_ge(qkv_mm, 3 * TT)
                    if u >= 12:
                        act.wait_ge(ffn_low_pool, sum(v < 12 for v in POOL_UNITS))
                        act.wait_ge(ffn_low, sum(v < 12 for v in OTHER_UNITS))
                    split_high(hi, src, st[:, 92 + u // 12:93 + u // 12], ffn_high)
            for n in range(NS - 2, NS):
                keep_pT(act, n)
            for c in range(C):
                high_x(1, c)
            for c in range(C):
                act.wait_ge(xh_low, C + c + 1)
                act.activation(xnT[:, c], ps[c][:, :], ACT.Copy).then_inc(x32_set, 1)
            act.wait_ge(z_mm, 1)
            act.activation(rope_t[:, 0, 0:TT * NE], ps[0][:, 0:TT * NE], ACT.Tanh, scale=1 / QUANT_TEMP).then_inc(router_exps, 1)
            act.wait_ge(l_sub, 1)
            act.activation(rope_t[:, 2, 128:128 + TT * NE], rope_t[:, 2, 64:64 + TT * NE], ACT.Exp).then_inc(router_exps, 1)
            for q in range(13):
                if q < 12:
                    act.wait_ge(h_mm, q + 1)
                    if q >= 2:
                        act.wait_ge(hw_set, q - 1)
                    act.activation(ea[:, q % 2], ps[4 + q % 2][:, :], ACT.Gelu_apprx_tanh, scale=st[:, 4:5]).then_inc(h_act, 1)
                if q >= 1:
                    act.wait_ge(hw_set, q)
                    act.activation(hwh[:, 0, q - 1], HW32[q % 2], ACT.Copy).then_inc(hw_high, 1)

        @block.vector
        def _(dve):
            count = [0]

            def step(ins):
                count[0] += 1
                ins.then_inc(vec, 1)
                dve.wait_ge(vec, count[0])

            def split_low(dst, src, scale, high, done):
                dve.scalar_tensor_tensor(dst, src, scale, high, ALU.mult, ALU.subtract).then_inc(done, 1)

            def post(ins):
                count[0] += 1
                ins.then_inc(vec, 1)

            def layer_norm(src, dst, done):
                for i in range(TT):
                    post(dve.bn_stats(st[:, 96 + 6 * i:102 + 6 * i], src[:, i]))
                dve.wait_ge(vec, count[0])
                for i in range(TT):
                    post(dve.bn_aggr(st[:, 120 + 2 * i:122 + 2 * i], st[:, 96 + 6 * i:102 + 6 * i]))
                dve.wait_ge(vec, count[0])
                dve.tensor_scalar(st[:, 8:12], st[:, 121:128:2], LN_EPS, None, ALU.add).then_inc(ln_stats, 1)
                dve.wait_ge(pool_pow, 1)
                for i in range(TT):
                    dve.tensor_scalar(dst[:, i], src[:, i], st[:, 120 + 2 * i:121 + 2 * i], st[:, 12 + i:13 + i],
                                      ALU.subtract, ALU.mult).then_inc(done, 1)

            def layer_norm_by_tile(src, dst, powers, done, make, besides=()):
                def norm(i):
                    dve.wait_ge(pool_pow, powers + i + 1)
                    dve.tensor_scalar(dst[:, i], src[:, i], st[:, 120 + 2 * i:121 + 2 * i], st[:, 12 + i:13 + i],
                                      ALU.subtract, ALU.mult).then_inc(done, 1)

                for i in range(TT):
                    make(i)
                    step(dve.bn_stats(st[:, 96 + 6 * i:102 + 6 * i], src[:, i]))
                    step(dve.bn_aggr(st[:, 120 + 2 * i:122 + 2 * i], st[:, 96 + 6 * i:102 + 6 * i]))
                    dve.tensor_scalar(st[:, 8 + i:9 + i], st[:, 121 + 2 * i:122 + 2 * i], LN_EPS, None, ALU.add)\
                        .then_inc(ln_stats, 1)
                    if i >= TT - len(besides):
                        besides[i - TT + len(besides)]()
                    if i >= 1:
                        norm(i - 1)
                norm(TT - 1)

            dve.wait_ge(x_in, 16)
            layer_norm(x_s, x_s, x_normed)
            dve.wait_ge(consts_in, 64)
            dve.tensor_copy(identb, ident).then_inc(pickers_set, 1)
            for c in range(C):
                dve.wait_ge(wqk_mm, c + 1)
                dve.scalar_tensor_tensor(wqk[:, c], ps[c][:, :], sm[:, WSLOT + c:WSLOT + c + 1], winb,
                                         ALU.mult, ALU.mult).then_inc(wqk_kept, 1)
            step(dve.tensor_tensor(gb[:, 0:8], sm[:, BI:BI + 8], sm[:, BH:BH + 8], ALU.add))
            step(dve.tensor_scalar(gb[:, 0:8], gb[:, 0:8], 0.5, None, ALU.mult))
            step(dve.tensor_scalar(gb[:, 8:12], sm[:, BH + 8:BH + 12], 0.5, None, ALU.mult))
            for c in range(C):
                dve.wait_ge(slots_high, c + 1)
                split_low(hs[:, 1, c], h32[:, c], S_X, hs[:, 0, c], slots_low)
            dve.wait_ge(norm_sum, 1)
            dve.tensor_scalar(st[:, 16:17], ps[0][:, 0:1], S_W ** -2, TINY, ALU.mult, ALU.add).then_inc(norm_in, 1)
            dve.wait_ge(pool_pow, 2)
            step(dve.reciprocal(st[:, 22:23], st[:, 18:19]))
            step(dve.tensor_scalar(st[:, 25:26], st[:, 22:23], SCALE * S_W / S_X ** 2, None, ALU.mult))
            step(dve.tensor_scalar(st[:, 28:29], st[:, 25:26], -1.0, None, ALU.mult))
            dve.tensor_copy(st[:, 24:25], st[:, 18:19]).then_inc(scales_set, 1)
            for u in range(QK_UNITS):
                dve.wait_ge(unit_high, u + 1)
                split_low(wr[:, u, 1], wqk[:, :, u * P:(u + 1) * P], st[:, 24:25], wr[:, u, 0], unit_low)
            def add_squares(b):
                sq = slot_squares
                dve.wait_ge(slot_sq, (C - 1) * (b + 1))
                dve.tensor_tensor(sq[0], sq[0], sq[1], ALU.add).then_inc(slot_sq_sum, 1)
                dve.wait_ge(slot_sq_sum, 4 * b + 1)
                dve.tensor_tensor(sq[0], sq[0], sq[2], ALU.add).then_inc(slot_sq_sum, 1)

            def add_last_square(b):
                sq = slot_squares
                dve.tensor_tensor(sq[C - 1], h32[:, C - 1], h32[:, C - 1], ALU.mult).then_inc(slot_sq_sum, 1)
                dve.wait_ge(slot_sq_sum, 4 * b + 3)
                dve.tensor_tensor(sq[0], sq[0], sq[C - 1], ALU.add).then_inc(slot_sq_sum, 1)

            add_squares(0)
            dve.wait_ge(slots_copied, C)
            dve.wait_ge(wqk_sq, 1)
            add_last_square(0)
            dve.wait_ge(gate_sq, 4 * C)
            dve.reduce_sum(st[:, 21:22], st[:, 56:56 + 4 * C], AX.X).then_inc(sq_summed, 1)

            def gate_scales():
                dve.wait_ge(pool_pow, 3)
                step(dve.reciprocal(st[:, 23:24], st[:, 19:20]))
                step(dve.tensor_scalar(st[:, 29:30], st[:, 23:24], 1 / S_X, None, ALU.mult))
                step(dve.tensor_scalar(st[:, 27:28], st[:, 23:24], 0.5 / S_X, None, ALU.mult))
                dve.tensor_copy(st[:, 26:27], st[:, 19:20]).then_inc(scales_set, 1)

            def gate_low(g, j):
                dve.wait_ge(unit_high, g * GATE_LANES + (QK_UNITS + j + 1))
                split_low(wr[:, QK_UNITS + j, 1].rearrange("p c e -> p (c e)"), gate_unit(g, j), st[:, 26:27],
                          wr[:, QK_UNITS + j, 0].rearrange("p c e -> p (c e)"), unit_low)

            def iteration(it, first):
                def spread(n):
                    for i in range(TT):
                        dve.tensor_scalar(diag[:, i], ident, st[:, 36 + i:37 + i], None, ALU.mult).then_inc(diag_set, 1)
                    dve.wait_ge(bc_mm, 2 * it + n + 1)
                    dve.tensor_copy(rb[:, :], BC[:, :]).then_inc(bc_kept, 1)
                    dve.wait_ge(bc_kept, 2 * it + n + 1)

                def prepare(g, j):
                    t = g * RING + j
                    dve.wait_ge(row_r, t + 1)
                    dve.tensor_scalar(pn_tile(t, 0), cx[:, j], st[:, 48 + j:49 + j], None, ALU.mult).then_inc(part_high, 1)
                    dve.wait_ge(part_high, t + 1)
                    split_low(pn_tile(t, 1), cx[:, j], st[:, 48 + j:49 + j], pn_tile(t, 0), part_low)

                dve.wait_ge(sum_mm, 2 * it + 1)
                dve.tensor_scalar(st[:, 32:36], RED[:, 0:TT], 1 / D, EPS, ALU.mult, ALU.add).then_inc(sum_in, 1)
                if first:
                    prepare(0, 0)
                dve.wait_ge(factor, it + 1)
                spread(0)
                def query_low(f):
                    dve.wait_ge(q_high, C * it + f + 1)
                    dve.tensor_tensor(qu[:, 1, f], ea[:, f], qu[:, 0, f], ALU.subtract).then_inc(q_low, 1)

                if first:
                    dve.wait_ge(norm_sum, 2)
                    dve.tensor_scalar(st[:, 17:18], ps[3][:, 0:1], S_W ** -2, TINY, ALU.mult, ALU.add).then_inc(norm_in, 1)
                for f in range(C):
                    if first and 1 <= f < LEAD_T:
                        prepare(0, f)
                    dve.wait_ge(unit_used, it * UNITS + f + 1)
                    dve.scalar_tensor_tensor(ea[:, f], QB[f][:, :], 1 / S_W, rb[:, :], ALU.mult, ALU.mult).then_inc(q_kept, 1)
                    if f >= 1:
                        query_low(f - 1)
                query_low(C - 1)

                def maximum(g, j):
                    T, b = it * NT + g * RING + j, j % 2
                    dve.wait_ge(scored, T + 1)
                    dve.reduce_max(st[:, 88 + b:89 + b], SC[b][:, :], AX.X).then_inc(maxed, 1)
                    dve.wait_ge(maxed, T + 1)
                    dve.tensor_scalar(st[:, 80 + b:81 + b], st[:, 88 + b:89 + b], st[:, 28:29], None, ALU.mult)\
                        .then_inc(nmaxed, 1)

                def weights(g, j):
                    T, b = it * NT + g * RING + j, j % 2
                    dve.wait_ge(exped, T + 1)
                    dve.reciprocal(st[:, 90 + b:91 + b], st[:, 84 + b:85 + b]).then_inc(recip, 1)
                    dve.wait_ge(recip, T + 1)
                    dve.wait_ge(acc_done, T + it + 1)
                    dve.tensor_scalar(ea[:, 2 + b], ea[:, b], st[:, 90 + b:91 + b], S_A, ALU.mult, ALU.mult)\
                        .then_inc(attn_set, 1)
                    dve.wait_ge(attn_high, T + 1)
                    dve.tensor_tensor(ah[:, b, 1], ea[:, 2 + b], ah[:, b, 0], ALU.subtract).then_inc(attn_low, 1)

                def plain(g, j):
                    maximum(g, j)
                    weights(g, j)

                def full(g, j):
                    maximum(g, j)
                    prepare(*ahead(g, j, LEAD_T))
                    weights(g, j)

                if first:
                    gate_scales()

                    def with_gates(g, j):
                        maximum(g, j)
                        prepare(*ahead(g, j, LEAD_T))
                        if 0 < j <= GATE_LANES:
                            gate_low(g, j - 1)
                        weights(g, j)

                    tiles(dve, with_gates, 0, GATE_GROUPS)
                    tiles(dve, full, GATE_GROUPS, NG - 1)
                    for j in range(RING):
                        maximum(NG - 1, j)
                        if j + LEAD_T < RING:
                            prepare(NG - 1, j + LEAD_T)
                        weights(NG - 1, j)
                else:
                    tiles(dve, plain)
                dve.wait_ge(sum_mm, 2 * it + 2)
                dve.tensor_scalar(st[:, 32:36], RED[:, 0:TT], EPS * S_A, None, ALU.add).then_inc(gru_step, 1)
                dve.wait_ge(gru_step, 2 * it + 1)
                dve.reciprocal(st[:, 36:40], st[:, 32:36]).then_inc(gru_step, 1)
                dve.wait_ge(gru_step, 2 * it + 2)
                spread(1)
                def update_low(c):
                    dve.wait_ge(u_high, C * it + c + 1)
                    dve.tensor_tensor(qu[:, 1, c], ea[:, c], qu[:, 0, c], ALU.subtract).then_inc(u_low, 1)

                for c in range(C):
                    dve.tensor_tensor(ea[:, c], U[c][:, :], rb[:, :], ALU.mult).then_inc(u_kept, 1)
                    if c >= 1:
                        update_low(c - 1)
                update_low(C - 1)
                def low_slots(c):
                    dve.wait_ge(slots_high, C * (it + 1) + c + 1)
                    split_low(hs[:, 1, c], h32[:, c], S_X, hs[:, 0, c], slots_low)

                for a in range(C):
                    n = C * it + a
                    A = GB(a)
                    unit = it * UNITS + QK_UNITS + 6 * a
                    dve.wait_ge(unit_used, unit + 3)
                    dve.wait_ge(tanh_r, n + 1)
                    dve.tensor_scalar(ea[:, 2], A[2][:, :], st[:, 27:28], gb[:, 8 + a:9 + a], ALU.mult, ALU.add).then_inc(hid_set, 1)
                    dve.wait_ge(hid_set, 2 * n + 1)
                    dve.scalar_tensor_tensor(ea[:, 2], ea[:, 0], 1.0, ea[:, 2], ALU.add, ALU.mult).then_inc(hid_set, 1)
                    dve.wait_ge(hid_set, 2 * n + 2)
                    if a == C - 1:
                        low_slots(0)
                        low_slots(1)
                    dve.wait_ge(unit_used, unit + 5)
                    dve.scalar_tensor_tensor(ea[:, 2], A[3][:, :], st[:, 29:30], ea[:, 2], ALU.mult, ALU.add).then_inc(n_in_set, 1)
                    if a == C - 1:
                        low_slots(2)
                        add_squares(it + 1)
                    dve.wait_ge(tanh_n, n + 1)
                    dve.tensor_tensor(ea[:, 2], h32[:, a], ea[:, 3], ALU.subtract).then_inc(z_step, 1)
                    dve.wait_ge(z_step, 2 * n + 1)
                    dve.wait_ge(tanh_z, n + 1)
                    dve.scalar_tensor_tensor(ea[:, 2], ea[:, 1], 1.0, ea[:, 2], ALU.add, ALU.mult).then_inc(z_step, 1)
                    dve.wait_ge(z_step, 2 * n + 2)
                    dve.scalar_tensor_tensor(h32[:, a], ea[:, 2], 0.5, ea[:, 3], ALU.mult, ALU.add).then_inc(h_new, 1)
                dve.wait_ge(h_new, C * (it + 1))
                add_last_square(it + 1)
                low_slots(C - 1)

            iterations(dve, iteration)

            dve.wait_ge(x1_in, 16)
            def add_slots(i):
                dve.wait_ge(back_turned, i + 1)
                dve.tensor_tensor(x1[:, i], x1[:, i], ps[4 + i][:, :], ALU.add).then_inc(x1_set, 1)
                dve.wait_ge(x1_set, i + 1)

            def wqkv_sum():
                dve.wait_ge(qkv_sq, 3)
                dve.reduce_sum(st[:, 67:68], st[:, 64:67], AX.X).then_inc(sq_summed, 1)

            def wqkv_norm():
                dve.wait_ge(norm_sum, 3)
                dve.tensor_scalar(st[:, 74:75], ps[0][:, 0:1], S_W ** -2, TINY, ALU.mult, ALU.add).then_inc(norm_in, 1)

            layer_norm_by_tile(x1, xn, 3, xn_set, add_slots, (wqkv_sum, wqkv_norm))
            dve.wait_ge(pool_pow, 8)
            step(dve.tensor_scalar(st[:, 76:77], st[:, 75:76], S_X, None, ALU.mult))
            step(dve.reciprocal(st[:, 77:78], st[:, 76:77]))
            step(dve.tensor_scalar(st[:, 52:53], sm[:, QW:QW + 1], sm[:, KW:KW + 1], ATT_SCALE, ALU.mult, ALU.mult))
            dve.tensor_scalar(st[:, 78:79], st[:, 76:77], st[:, 76:77], EPS, ALU.mult, ALU.mult).then_inc(qkv_scales, 1)

            def low_x(n, c):
                dve.wait_ge(xh_high, C * n + c + 1)
                split_low(xh[n][:, 1, c], ps[c][:, :], S_X, xh[n][:, 0, c], xh_low)

            def low_w(w, c):
                dve.wait_ge(qkvh_high, w * C + c + 1)
                split_low(qkvh[w][:, 1, c], wqkv_s[:, c, w * D:(w + 1) * D], st[:, 75:76], qkvh[w][:, 0, c], qkvh_low)

            for c in range(C):
                low_w(0, c)
                low_x(0, c)
            for c in range(C):
                low_w(1, c)
            def rotate(n):
                i, w = n % TT, n // TT
                src = ps[n][:, :]
                cos = sm[:, COS + i * HD:COS + (i + 1) * HD].unsqueeze(1).to_broadcast([P, H, HD])
                sn = sm[:, SIN + i * HD:SIN + (i + 1) * HD].rearrange("p (s d) -> p s d", s=2)
                sh = src.rearrange("p (h s d) -> p h s d", h=H, s=2)
                sw = rope_t[:, 2].rearrange("p (h s d) -> p h s d", h=H, s=2)
                rot = rope_t[:, n % 2]
                if n >= 2:
                    dve.wait_ge(qk_set, n - 1)
                dve.tensor_tensor(rot.rearrange("p (h d) -> p h d", h=H), src.rearrange("p (h d) -> p h d", h=H),
                                  cos, ALU.mult).then_inc(rope_step, 1)
                if n >= 1:
                    dve.wait_ge(qk_rot, n)
                for s in range(2):
                    dve.tensor_tensor(sw[:, :, s], sh[:, :, 1 - s], sn[:, s].unsqueeze(1).to_broadcast([P, H, HD // 2]),
                                      ALU.mult).then_inc(rope_step, 1)
                dve.wait_ge(rope_step, 3 * n + 3)
                dve.tensor_tensor(rot, rot, rope_t[:, 2], ALU.add).then_inc(qk_rot, 1)

            def head_norm(n):
                dve.wait_ge(rope_sq, n + 1)
                dve.reduce_sum(rope_t[:, 5, (n % 2) * 64:(n % 2) * 64 + H],
                               rope_t[:, 3 + n % 2].rearrange("p (h d) -> p h d", h=H), AX.X).then_inc(head_sum, 1)

            for n in range(2 * TT):
                head_norm(n)
                rotate(n)
                o = (n % 2) * 64
                dve.wait_ge(head_rms, n + 1)
                dve.reciprocal(rope_t[:, 5, o + 32:o + 32 + H], rope_t[:, 5, o + 16:o + 16 + H]).then_inc(head_r, 1)
            dve.wait_ge(ffn_sq, 8)
            dve.reduce_sum(st[:, 88:90], st[:, 80:88].rearrange("p (m k) -> p m k", m=2), AX.X).then_inc(sq_summed, 1)
            for g in range(HG):
                dve.wait_ge(kT_turned, g + 1)
                if g == 1:
                    dve.wait_ge(norm_sum, 4)
                    dve.tensor_scalar(st[:, 90:92], ps[7][:, 0:2], S_W ** -2, TINY, ALU.mult, ALU.add).then_inc(norm_in, 1)
                dve.tensor_copy(kT[:, g], ps[4 + g][:, :]).then_inc(kT_kept, 1)

            def s_maximum(n):
                w = (steps[n][2] + 1) * P
                dve.wait_ge(s_mm, n + 1)
                dve.tensor_reduce(st[:, 56 + n % 4:57 + n % 4], ps[n % 4][:, 0:w], AX.X, ALU.max, negate=True).then_inc(s_max, 1)

            def s_normal(n):
                w = (steps[n][2] + 1) * P
                dve.wait_ge(s_exp, n + 1)
                step(dve.reciprocal(st[:, 72 + n % 2:73 + n % 2], st[:, 60 + n % 4:61 + n % 4]))
                dve.tensor_scalar(ea[:, n % 4, 0:w], ea[:, n % 4, 0:w], st[:, 72 + n % 2:73 + n % 2], None, ALU.mult)\
                    .then_inc(p_set, 1)

            def keep_att(hg):
                dve.wait_ge(pv_mm, 16 * hg + 16)
                dve.tensor_copy(attT[:, hg], ps[6 + hg % 2][:, :]).then_inc(att_kept, 1)

            for n in range(NS + 1):
                if n - 2 in OTHER_AT:
                    u = OTHER_AT[n - 2]
                    src, hi, lo = ffn_unit(u)
                    dve.wait_ge(ffn_high, OTHER_UNITS.index(u) + 1)
                    split_low(lo, src, st[:, 92 + u // 12:93 + u // 12], hi, ffn_low)
                if n < NS:
                    s_maximum(n)
                if n >= 1:
                    s_normal(n - 1)
                if n >= 24 and (n - 24) % 16 == 0:
                    keep_att((n - 24) // 16)
            keep_att(HG - 1)
            def add_attention(i):
                dve.wait_ge(o_mm, i + 1)
                dve.tensor_tensor(x1[:, i], x1[:, i], ps[4 + i][:, :], ALU.add).then_inc(x1_set, 1)
                dve.wait_ge(x1_set, TT + i + 1)

            dve.wait_ge(pool_pow, 9)
            step(dve.reciprocal(st[:, 94:96], st[:, 92:94]))
            step(dve.tensor_scalar(st[:, 4:5], st[:, 94:95], 1 / S_X, None, ALU.mult))
            step(dve.tensor_scalar(st[:, 5:6], st[:, 92:93], 1 / 32, None, ALU.mult))
            step(dve.tensor_scalar(st[:, 6:7], st[:, 94:95], st[:, 95:96], 32.0, ALU.mult, ALU.mult))
            layer_norm_by_tile(x1, xn, 9, xn_set, add_attention)
            for c in range(C):
                low_x(1, c)
            dve.tensor_copy(pick, ident[0:NE, 0:NE].unsqueeze(2).to_broadcast([NE, NE, P])).then_inc(pickers_set, 1)
            q_r = rope_t[:, 0, 0:TT * NE].rearrange("p (t d) -> p t d", t=TT)
            prod = rope_t[:, 1, 0:TT * NE * NE].rearrange("p (t e d) -> p t e d", t=TT, e=NE)
            logit = rope_t[:, 2, 0:TT * NE]
            lg = logit.rearrange("p (t e) -> p t e", t=TT)
            top = rope_t[:, 2, 192:192 + TT]
            gt_, eq_ = (rope_t[:, 3, o:o + TT * NE * NE].rearrange("p (t e d) -> p t e d", t=TT, e=NE) for o in (0, 160))
            rank = rope_t[:, 3, 320:320 + TT * NE]
            shifted = rope_t[:, 2, 64:64 + TT * NE]
            ex = rope_t[:, 2, 128:128 + TT * NE]
            step(dve.tensor_scalar(st[:, 53:54], sm[:, TEMP:TEMP + 1], 0.1, None, ALU.max))
            step(dve.reciprocal(st[:, 54:55], st[:, 53:54]))
            step(dve.tensor_scalar(st[:, 54:55], st[:, 54:55], 0.5, None, ALU.mult))
            anch = sm[:, ANCH:ANCH + NE * NE].rearrange("p (e d) -> p e d", e=NE)
            lower = sm[:, LOWER:LOWER + NE * NE].rearrange("p (e d) -> p e d", e=NE)
            full4 = [P, TT, NE, NE]
            dve.wait_ge(router_exps, 1)
            step(dve.tensor_tensor(prod, q_r.unsqueeze(2).to_broadcast(full4), anch.unsqueeze(1).to_broadcast(full4), ALU.mult))
            step(dve.reduce_sum(logit, prod.rearrange("p t e d -> p (t e) d"), AX.X))
            step(dve.tensor_scalar(logit, logit, -6.0, st[:, 54:55], ALU.add, ALU.mult))
            l_e, l_j = lg.unsqueeze(3).to_broadcast(full4), lg.unsqueeze(2).to_broadcast(full4)
            step(dve.tensor_tensor(gt_, l_j, l_e, ALU.is_gt))
            step(dve.tensor_tensor(eq_, l_j, l_e, ALU.is_equal))
            step(dve.tensor_tensor(eq_, eq_, lower.unsqueeze(1).to_broadcast(full4), ALU.mult))
            step(dve.tensor_tensor(gt_, gt_, eq_, ALU.add))
            step(dve.reduce_sum(rank, gt_.rearrange("p t e d -> p (t e) d"), AX.X))
            step(dve.tensor_scalar(rank, rank, float(TOPK), None, ALU.is_lt))
            step(dve.reduce_max(top, lg, AX.X))
            dve.tensor_tensor(shifted.rearrange("p (t e) -> p t e", t=TT), lg, top.unsqueeze(2).to_broadcast([P, TT, NE]),
                              ALU.subtract).then_inc(l_sub, 1)
            dve.wait_ge(router_exps, 2)
            step(dve.tensor_tensor(ex, ex, rank, ALU.mult))
            step(dve.reduce_sum(top, ex.rearrange("p (t e) -> p t e", t=TT), AX.X))
            step(dve.reciprocal(top, top))
            dve.tensor_tensor(shifted.rearrange("p (t e) -> p t e", t=TT), ex.rearrange("p (t e) -> p t e", t=TT),
                              top.unsqueeze(2).to_broadcast([P, TT, NE]), ALU.mult).then_inc(w_set, 1)
            dve.wait_ge(w_turned, 1)
            dve.tensor_scalar(rb[0:NE, :], ps[6][0:NE, :], st[0:NE, 5:6], None, ALU.mult).then_inc(wT_kept, 1)
            dve.wait_ge(ffn_low_pool, len(POOL_UNITS))
            for q in range(13):
                if q < 12:
                    dve.wait_ge(h_act, q + 1)
                    dve.wait_ge(wb_mm, q // 2 + 1)
                    if q >= 2:
                        dve.wait_ge(hw_low, q - 1)
                    dve.tensor_tensor(HW32[(q + 1) % 2], ea[:, q % 2], ps[6 + (q // 2) % 2][:, :], ALU.mult).then_inc(hw_set, 1)
                if q >= 1:
                    dve.wait_ge(hw_high, q)
                    dve.tensor_tensor(hwh[:, 1, q - 1], HW32[q % 2], hwh[:, 0, q - 1], ALU.subtract).then_inc(hw_low, 1)
            for i in range(TT):
                dve.wait_ge(y_mm, i + 1)
                dve.scalar_tensor_tensor(x1[:, i], ps[i][:, :], st[:, 6:7], x1[:, i], ALU.mult, ALU.add).then_inc(y_set, 1)

        @block.tensor
        def _(pe):
            def mm(o, w, r, start=True, stop=True, **kw):
                return pe.matmul(o, w, r, start=start, stop=stop, **kw)

            def turn(o, i):
                return pe.transpose(o, i, ident)

            for first_k, half_in in ((0, wqk_in), (C // 2, wqk_rest_in)):
                pe.wait_ge(half_in, 32)
                for c in range(C):
                    for k in range(first_k, first_k + C // 2):
                        ins = mm(ps[c][:, :], wq_s[:, k, c * P:(c + 1) * P], wk_s[:, k, :], k == 0, k == C - 1)
                    if first_k:
                        ins.then_inc(wqk_mm, 1)

            def gate_product(n):
                c, gt = n // 3, n % 3
                if n >= 4:
                    pe.wait_ge(g_kept, n - 3)
                for k in range(C):
                    ins = mm(ps[4 + n % 4][:, :], wv_s[:, k, c * P:(c + 1) * P], wiT[:, k, gt * D:(gt + 1) * D], k == 0, k == C - 1)
                ins.then_inc(g_mm, 1)

            for n in range(3):
                pe.wait_ge(wi_in[n], 32 if n == 0 else 16)
                gate_product(n)
            pe.wait_ge(x_normed, TT)
            pe.wait_ge(consts_in, 64)
            for c in range(C):
                pe.wait_ge(wqk_kept, c + 1)
                for i in range(TT):
                    ins = turn(ps[c][:, i * P:(i + 1) * P], x_s[:, i, c * P:(c + 1) * P])
                ins.then_inc(x_turned, 1)
            for n in range(3, 6):
                gate_product(n)
            pe.wait_ge(ones_set, 1)
            pe.wait_ge(wqk_sq, 1)
            pe.wait_ge(slots_copied, 1)
            mm(ps[0][:, 0:1], ones[:, :], st[:, 20:21]).then_inc(norm_sum, 1)
            for n in range(6, 12):
                gate_product(n)

            def iteration(it, first):
                def unit_part(u, bank, move, starts, stops, chunks=range(C), ready=None):
                    if 0 in chunks:
                        pe.wait_ge(unit_in[u % WRING], it * (16 * (UNITS // WRING)) + 16 * (u // WRING + 1))
                    for c in chunks:
                        if ready is not None:
                            ready(c)
                        for pi, (a, b) in enumerate(PARTS3):
                            ins = mm(bank[:, :], wr[:, u % WRING, a, c, :], move[:, b, c, :],
                                     starts and c == 0 and pi == 0, stops and c == C - 1 and pi == 2)
                    if C - 1 in chunks:
                        ins.then_inc(unit_used, 1)

                def slot_sums():
                    for i in range(TT):
                        ins = mm(RED[:, i:i + 1], acc[:, i * P:(i + 1) * P], ones[:, 0:1])
                    ins.then_inc(sum_mm, 1)

                def broadcast(n):
                    pe.wait_ge(diag_set, TT * (2 * it + n + 1))
                    mm(BC[:, :], ones[:, :], diag[:, :, :].rearrange("p a b -> p (a b)")).then_inc(bc_mm, 1)

                def slots_ready(c):
                    pe.wait_ge(slots_high, C * it + c + 1)
                    pe.wait_ge(slots_low, C * it + c + 1)

                if first:
                    for f in range(C):
                        if f < C - 1:
                            pe.wait_ge(g_kept, 2 * C + 1 + f)
                        else:
                            pe.wait_ge(norm_in, 1)
                        unit_part(f, QB[f], hs, True, True, range(C), slots_ready if f == 0 else None)
                        if f == 0:
                            pe.wait_ge(slot_sq_sum, 4)
                            pe.wait_ge(g_kept, 3 * C)
                            slot_sums()
                            pe.wait_ge(sq_summed, 1)
                            mm(ps[3][:, 0:1], ones[:, :], st[:, 21:22]).then_inc(norm_sum, 1)
                        elif f == 1:
                            broadcast(0)
                else:
                    pe.wait_ge(h_new, C * it - 1)
                    for f in range(C):
                        if f == C - 1:
                            pe.wait_ge(slot_sq_sum, 4 * (it + 1))
                            slot_sums()
                            pe.wait_ge(tanh_r, C * it)
                        unit_part(f, QB[f], hs, True, False, range(C - 1), slots_ready if f == 0 else None)
                    slots_ready(C - 1)
                    for f in range(C):
                        if f == 2:
                            broadcast(0)
                        unit_part(f, QB[f], hs, False, True, range(C - 1, C))

                def queries_ready(c):
                    pe.wait_ge(q_high, C * it + c + 1)
                    pe.wait_ge(q_low, C * it + c + 1)

                def turn_tile(g, j):
                    t = g * RING + j
                    pe.wait_ge(part_low, t + 1)
                    for a in range(2):
                        for c in range(C):
                            ins = pe.transpose(TP[j % 2][:, :].bitcast(F16)[:, (a * C + c) * P:(a * C + c + 1) * P],
                                               pn_w(t, a, c), ident16)
                    ins.then_inc(turned, 1)

                def scores(g, j, ready=None):
                    if first:
                        pe.wait_ge(kept, g * RING + j + 1)
                    else:
                        pe.wait_ge(pt_in[j], (it - 1) * (16 * NG) + (16 * g + 16))
                    for c in range(C):
                        if ready is not None:
                            ready(c)
                        for pi, (a, b) in enumerate(PARTS3):
                            ins = mm(SC[j % 2][:, :], pt[:, j, a, c, :], qu[:, b, c, :], c == 0 and pi == 0, c == C - 1 and pi == 2)
                    ins.then_inc(scored, 1)

                def update(g, j, last=False):
                    t = g * RING + j
                    pe.wait_ge(attn_high, it * NT + t + 1)
                    pe.wait_ge(attn_low, it * NT + t + 1)
                    for c in range(C):
                        for pi, (a, b) in enumerate(PARTS3):
                            ins = mm(U[c][:, :], pn_w(t, a, c), ah[:, j % 2, b], False, last and pi == 2, skip_group_check=True)
                    ins.then_inc(updated, 1)

                if first:
                    pe.wait_ge(q_kept, C - 1)
                    pe.wait_ge(bc_kept, 2 * it + 1)
                    turn_tile(0, 0)
                    turn_tile(0, 1)
                    pe.wait_ge(kept, 1)
                    turn_tile(0, 2)
                pe.wait_ge(q_kept, C * it + 2)
                scores(0, 0, queries_ready)
                scores(0, 1)
                if first:
                    pe.wait_ge(q_kept, C)
                    pe.wait_ge(norm_in, 2)
                for c in range(C):
                    mm(U[c][:, :], zeros16, qu[:, 0, 0, :], True, False, skip_group_check=True)

                def turn_ahead(g, j):
                    pe.wait_ge(kept, g * RING + j + LEAD_T - 1)
                    turn_tile(*ahead(g, j, LEAD_T))

                def scores_ahead(g, j):
                    pe.wait_ge(exped, it * NT + g * RING + j + 1)
                    scores(*ahead(g, j, 2))

                def full(g, j):
                    update(g, j)
                    if first:
                        turn_ahead(g, j)
                    scores_ahead(g, j)

                tiles(pe, full, 0, NG - 1)
                for j in range(RING):
                    if j == RING - 1:
                        unit_part(QK_UNITS, GB(0)[0], hs, True, False)
                    update(NG - 1, j, j == RING - 1)
                    if first and j + LEAD_T < RING:
                        turn_ahead(NG - 1, j)
                    if j + 2 < RING:
                        scores_ahead(NG - 1, j)

                pe.wait_ge(acc_done, it * NT + NT + it + 2)
                slot_sums()

                def updates_ready(c):
                    pe.wait_ge(u_high, C * it + c + 1)
                    pe.wait_ge(u_low, C * it + c + 1)

                for a in range(C):
                    B = GB(a)
                    u0 = QK_UNITS + 6 * a
                    n = C * it + a
                    if a >= 2:
                        pe.wait_ge(h_new, n - 1)
                    if a > 0:
                        unit_part(u0, B[0], hs, True, False)
                    else:
                        pe.wait_ge(exped, (it + 1) * NT)
                    unit_part(u0 + 1, B[1], hs, True, False, range(C // 2))
                    if a == 0:
                        broadcast(1)
                    unit_part(u0 + 1, B[1], hs, True, False, range(C // 2, C))
                    unit_part(u0 + 2, B[2], hs, True, True)
                    unit_part(u0 + 3, B[0], qu, False, True, ready=updates_ready if a == 0 else None)
                    if a == 0:
                        pe.wait_ge(bc_kept, 2 * it + 2)
                    unit_part(u0 + 4, B[3], qu, True, True)
                    unit_part(u0 + 5, B[1], qu, False, True)

            iterations(pe, iteration)

            pe.wait_ge(h_new, C * ITERS - 1)
            for c in range(C):
                if c == C - 1:
                    pe.wait_ge(h_new, C * ITERS)
                for i in range(TT):
                    ins = turn(ps[4 + i][:, c * P:(c + 1) * P], h32[:, c, i * P:(i + 1) * P])
                    if c == C - 1:
                        ins.then_inc(back_turned, 1)

            def turn_xn(n, before=None):
                if before is not None:
                    before()
                for i in range(TT):
                    pe.wait_ge(xn_set, TT * n + i + 1)
                    for c in range(C):
                        ins = turn(ps[c][:, i * P:(i + 1) * P], xn[:, i, c * P:(c + 1) * P])
                        if i == TT - 1:
                            ins.then_inc(xn_turned, 1)

            def wqkv_norm():
                pe.wait_ge(sq_summed, 2)
                mm(ps[0][:, 0:1], ones[:, :], st[:, 67:68]).then_inc(norm_sum, 1)
                pe.wait_ge(norm_in, 3)

            turn_xn(0, wqkv_norm)
            for n, (w, i) in enumerate([(w, i) for w in range(3) for i in range(TT)]):
                if w == 2:
                    pe.wait_ge(qk_rot, i + 1)
                if i == 0 and w >= 1:
                    pe.wait_ge(xh_low, C)
                for c in range(C):
                    if n == 0:
                        pe.wait_ge(xh_low, c + 1)
                    if i == 0:
                        pe.wait_ge(qkvh_high, w * C + c + 1)
                        pe.wait_ge(*((qkvh_low, w * C + c + 1) if w < 2 else (v_low, c + 1)))
                    for pi, (a, b) in enumerate(PARTS3):
                        ins = mm(ps[n % 8][:, :], xh[0][:, b, c, i * P:(i + 1) * P], qkvh[w][:, a, c, :],
                                 c == 0 and pi == 0, c == C - 1 and pi == 2)
                ins.then_inc(qkv_mm, 1)
            pe.wait_ge(qk_set, TT)
            for g in range(HG):
                pe.wait_ge(qkv_kept, g + 1)
                for t in range(TT):
                    ins = turn(ps[g][:, t * P:(t + 1) * P], q_n[:, t, g * P:(g + 1) * P])
                ins.then_inc(qT_turned, 1)
            pe.wait_ge(qk_set, 2 * TT)
            for g in range(HG):
                if g == 1:
                    pe.wait_ge(sq_summed, 3)
                    mm(ps[7][:, 0:2], ones[:, :], st[:, 88:90]).then_inc(norm_sum, 1)
                if g == HG - 1:
                    pe.wait_ge(norm_in, 4)
                for t in range(TT):
                    ins = turn(ps[4 + g][:, t * P:(t + 1) * P], k_n[:, t, g * P:(g + 1) * P])
                ins.then_inc(kT_turned, 1)
            pe.wait_ge(kT_kept, HG)
            pe.wait_ge(qT_kept, HG)
            pe.wait_ge(mask_set, 2)
            pe.wait_ge(pickers_set, 1)

            def s_product(n):
                hg, hh, i = steps[n]
                w = (i + 1) * P
                r = slice(HD * hh, HD * hh + HD)
                if n >= 4:
                    pe.wait_ge(s_exp, n - 3)
                mm(ps[n % 4][:, 0:w], qT[r, hg, i * P:(i + 1) * P], kT[r, hg, 0:w], True, False,
                   tile_position=(HD * hh, 0), skip_group_check=True)
                mm(ps[n % 4][:, i * P:w], identb, maskb, False, True, skip_group_check=True).then_inc(s_mm, 1)

            def turn_p(n):
                i = steps[n][2]
                pe.wait_ge(p_set, n + 1)
                if n >= 2:
                    pe.wait_ge(p_kept, n - 1)
                for b in range(i + 1):
                    ins = turn(ps[4 + n % 2][:, b * P:(b + 1) * P], ea[:, n % 4, b * P:(b + 1) * P])
                ins.then_inc(p_turned, 1)

            def pv(n):
                hg, hh, i = steps[n]
                pe.wait_ge(p_kept, n + 1)
                if hg >= 2 and hh == 0 and i == 0:
                    pe.wait_ge(att_kept, hg - 1)
                for b in range(i + 1):
                    ins = mm(ps[6 + hg % 2][HD * hh:HD * hh + HD, i * P:(i + 1) * P],
                             v_n[:, b, (4 * hg + hh) * HD:(4 * hg + hh + 1) * HD], pT[:, n % 4, b], b == 0, b == i,
                             tile_position=(0, HD * hh), skip_group_check=True)
                ins.then_inc(pv_mm, 1)

            for n in range(LEAD):
                s_product(n)
            for n in range(NS + 2):
                if n + LEAD < NS:
                    s_product(n + LEAD)
                if n < NS:
                    turn_p(n)
                if n >= 2:
                    pv(n - 2)
            pe.wait_ge(att_kept, HG)
            pe.wait_ge(wout_in, 16)
            for i in range(TT):
                for g in range(HG):
                    ins = mm(ps[4 + i][:, :], attT[:, g, i * P:(i + 1) * P], wout_s[:, g, :], g == 0, g == HG - 1)
                ins.then_inc(o_mm, 1)
            turn_xn(1)
            pe.wait_ge(ffn_low, len(OTHER_UNITS))
            pe.wait_ge(ffn_low_pool, len(POOL_UNITS))

            def hidden(q):
                if q >= 2:
                    pe.wait_ge(h_act, q - 1)
                for c in range(C):
                    for pi, (a, b) in enumerate(PARTS3):
                        ins = mm(ps[4 + q % 2][:, :], w1h[:, a, c, q * P:(q + 1) * P], xh[1][:, b, c, :],
                                 c == 0 and pi == 0, c == C - 1 and pi == 2)
                ins.then_inc(h_mm, 1)

            def weight_rows(e):
                if e >= 2:
                    pe.wait_ge(hw_set, 2 * (e - 1))
                mm(ps[6 + e % 2][:, :], pick[:, e], rb[0:NE, :]).then_inc(wb_mm, 1)

            def expert_out(q):
                pe.wait_ge(hw_low, q + 1)
                for i in range(TT):
                    for pi, (a, b) in enumerate(PARTS3):
                        ins = mm(ps[i][:, :], hwh[:, b, q, i * P:(i + 1) * P], w2h[:, a, q, :], q == 0 and pi == 0,
                                 q == 11 and pi == 2)
                    if q == 11:
                        ins.then_inc(y_mm, 1)

            pe.wait_ge(xh_low, 2 * C)
            hidden(0)
            pe.wait_ge(x32_set, C)
            for i in range(TT):
                for c in range(C):
                    ins = mm(ps[0][:, i * NE:(i + 1) * NE], xnT[:, c, i * P:(i + 1) * P], pj[:, c * NE:(c + 1) * NE], c == 0, c == C - 1)
            ins.then_inc(z_mm, 1)
            hidden(1)
            pe.wait_ge(w_set, 1)
            for i in range(TT):
                ins = pe.transpose(ps[6][0:NE, i * P:(i + 1) * P], rope_t[:, 2, 64 + i * NE:64 + (i + 1) * NE], ident)
            ins.then_inc(w_turned, 1)
            pe.wait_ge(wT_kept, 1)
            pe.wait_ge(pickers_set, 2)
            weight_rows(0)
            weight_rows(1)
            for q in range(12):
                if q + 2 < 12:
                    hidden(q + 2)
                if q % 2 == 1 and q // 2 + 2 < NE:
                    weight_rows(q // 2 + 2)
                expert_out(q)


_INS = ['x', 'ctx', 'wq', 'wk', 'wv', 'wi_t', 'wh_u', 'win_b', 'small', 'half', 'wqkv_t', 'wout_t', 'w1_t', 'w2', 'proj_t']


def layouts(x, ctx_1024, L0_xattn_Wq, L0_xattn_Wk, L0_xattn_Wv, L0_xattn_gru_wi, L0_xattn_gru_wh,
            L0_xattn_gru_bi, L0_xattn_gru_bh, L0_xattn_slot_norm_w, L0_xattn_input_norm_w, L0_attn_w_qkv,
            L0_attn_w_out, L0_attn_q_norm_w, L0_attn_k_norm_w, L0_ffn_proj_w, L0_ffn_anchors,
            L0_ffn_routing_temp, L0_ffn_w1, L0_ffn_w2):
    f = lambda a: np.asarray(a)
    cols = lambda a, n: f(a).reshape(n, P).T
    rows = lambda a: np.broadcast_to(f(a).reshape(1, -1), (P, f(a).size))
    half = HD // 2
    inv = (1.0 / np.float32(10000.0) ** (np.arange(half, dtype=np.float32) * np.float32(2.0) / np.float32(HD))).astype(np.float32)
    ang = np.arange(K, dtype=np.float32)[:, None] * inv[None, :]
    cos, sin = np.cos(ang), np.sin(ang)
    by_tile = lambda a: a.reshape(TT, P, HD).transpose(1, 0, 2).reshape(P, TT * HD)
    cos = by_tile(np.concatenate([cos, cos], axis=1).astype(np.float32))
    sin = by_tile(np.concatenate([-sin, sin], axis=1).astype(np.float32))
    lower = rows(np.tril(np.ones((NE, NE), np.float32), -1))
    small = np.concatenate([
        cols(L0_xattn_gru_bi, 12), cols(L0_xattn_gru_bh, 12), cols(L0_xattn_slot_norm_w, C), cols(L0_xattn_input_norm_w, C),
        np.tile(f(L0_attn_q_norm_w), 4)[:, None], np.tile(f(L0_attn_k_norm_w), 4)[:, None], rows(L0_ffn_routing_temp),
        rows(L0_ffn_anchors), lower, cos, sin, np.eye(P, dtype=np.float32)], axis=1)
    wh_u = f(L0_xattn_gru_wh).reshape(3, C, P, C, P).transpose(4, 1, 0, 3, 2)
    return {
        "x": f(x), "ctx": f(ctx_1024), "wq": f(L0_xattn_Wq), "wk": f(L0_xattn_Wk), "wv": f(L0_xattn_Wv),
        "wi_t": f(L0_xattn_gru_wi).T, "wh_u": wh_u, "win_b": rows(L0_xattn_input_norm_w), "small": small,
        "half": np.concatenate([np.eye(P), np.zeros((P, P))], axis=1).astype(np.float16),
        "wqkv_t": f(L0_attn_w_qkv).T, "wout_t": f(L0_attn_w_out).T,
        "w1_t": f(L0_ffn_w1).transpose(1, 0, 2).reshape(D, NE * DE), "w2": f(L0_ffn_w2).reshape(NE * DE, D),
        "proj_t": f(L0_ffn_proj_w).reshape(NE, C, P).transpose(2, 1, 0).reshape(P, C * NE),
    }


def kernel(**inputs):
    import concourse.bacc as _bacc
    from concourse.bass_utils import run_bass_kernel_spmd as _run

    nc = _bacc.Bacc("TRN2", target_bir_lowering=False, num_devices=1)
    arrays, args = {}, []
    laid = layouts(**inputs)
    for name in _INS:
        a = np.ascontiguousarray(laid[name])
        arrays[f"in_{name}"] = a
        args.append(nc.dram_tensor(f"in_{name}", a.shape, mybir.dt.from_np(a.dtype), kind="ExternalInput").ap())
    args.append(nc.dram_tensor("out_0", (1, K, D), F32, kind="ExternalOutput").ap())
    slot_kernel(nc, *args)
    r = _run(nc, [arrays], core_ids=[0])
    return r.results[0]["out_0"]
```
